# Optimizing a Trainium2 kernel written in Bass

```python
import numpy as np
import jax
import jax.numpy as jnp

def _softmax(x, axis=-1):
    return jax.nn.softmax(x, axis=axis)

def _gelu(x):
    return jax.nn.gelu(x, approximate=True)

def _silu(x):
    return jax.nn.silu(x)

def _sigmoid(x):
    return jax.nn.sigmoid(x)

def _layernorm(x, axis=-1, eps=1e-05):
    m = jnp.mean(x, axis=axis, keepdims=True)
    v = jnp.var(x, axis=axis, keepdims=True)
    return (x - m) / jnp.sqrt(v + eps)

def _scatter_add(tgt, idx, src, axis=0):
    return tgt.at[idx].add(src)

def _segment_sum(src, seg, n):
    return jax.ops.segment_sum(src, seg, n)
kernel_name = 'mk_xattn_ffn_d2_seqx_r8_f46558'

def setup_inputs(seed: int=0):
    np.random.seed(seed)
    _w = jnp.asarray

    def _rec_inputs():
        import jax
        import jax.numpy as jnp
        _rk = jax.random.key(seed)
        x = -0.0002928 + 1 * jax.random.normal(jax.random.fold_in(_rk, 1), (4, 512, 128), jnp.float32)
        _lenS = 512 - jax.random.randint(jax.random.fold_in(_rk, 7), (4,), 0, max(1, 512 // 4) + 1, jnp.int32)
        _lenS2 = 77 - jax.random.randint(jax.random.fold_in(_rk, 8), (4,), 0, max(1, 77 // 4) + 1, jnp.int32)
        _ctx_1024P = jax.random.normal(jax.random.fold_in(_rk, 11), (4, 16, 128), jnp.float32)
        _ctx_1024c = jax.random.dirichlet(jax.random.fold_in(_rk, 511), 0.3 * jnp.ones((16,), jnp.float32), (4, 77))
        _ctx_1024t = jnp.einsum('bsk,bkd->bsd', _ctx_1024c, _ctx_1024P)
        _ctx_1024t = _ctx_1024t * jax.lax.rsqrt(jnp.mean(jnp.square(_ctx_1024t)) + 1e-12) * 0.953939
        ctx_1024 = -1.39393e-06 + 0.999914 * (_ctx_1024t + 0.3 * jax.random.normal(jax.random.fold_in(_rk, 611), (4, 77, 128), jnp.float32))
        _validS = jnp.arange(512)[None, :] < _lenS[:, None]
        _validS2 = jnp.arange(77)[None, :] < _lenS2[:, None]
        _causal = jnp.tril(jnp.ones((512, 512), dtype=bool))
        mask_BxS2_bf1 = jnp.ones((4, 77), dtype=bool)
        return (x, ctx_1024, mask_BxS2_bf1)
    x, ctx_1024, mask_BxS2_bf1 = _rec_inputs()

    def _L0_xattn_setup():
        import jax, jax.numpy as jnp
        import numpy as np
        N_HEADS = 16
        D_MODEL = 128
        HEAD_DIM = D_MODEL // N_HEADS
        MASK_FILL = -100000000.0

        def _split_heads(x):
            B, S, _ = x.shape
            return x.reshape(B, S, N_HEADS, HEAD_DIM).transpose(0, 2, 1, 3)
        key = jax.random.key(seed)
        ks = jax.random.split(key, 12)
        B, L, P = (2, 256, 256)
        s = 1.0 / np.sqrt(D_MODEL).astype(np.float32)
        inp = {'q': jax.random.normal(ks[0], (B, L, D_MODEL), dtype=jnp.float32), 'k': jax.random.normal(ks[1], (B, P, D_MODEL), dtype=jnp.float32), 'v': jax.random.normal(ks[2], (B, P, D_MODEL), dtype=jnp.float32), 'attention_mask': jnp.ones((B, P), dtype=bool), 'Wq': jax.random.normal(ks[3], (D_MODEL, D_MODEL), dtype=jnp.float32) * s, 'bq': jnp.zeros((D_MODEL,), dtype=jnp.float32), 'Wk': jax.random.normal(ks[4], (D_MODEL, D_MODEL), dtype=jnp.float32) * s, 'bk': jnp.zeros((D_MODEL,), dtype=jnp.float32), 'Wv': jax.random.normal(ks[5], (D_MODEL, D_MODEL), dtype=jnp.float32) * s, 'bv': jnp.zeros((D_MODEL,), dtype=jnp.float32), 'Wo': jax.random.normal(ks[6], (D_MODEL, D_MODEL), dtype=jnp.float32) * s, 'bo': jnp.zeros((D_MODEL,), dtype=jnp.float32)}
        return inp
    _L0_xattn_all = _L0_xattn_setup()
    _L0_xattn_in = {k: v for k, v in _L0_xattn_all.items() if k in ('Wq', 'bq', 'Wk', 'bk', 'Wv', 'bv', 'Wo', 'bo')}
    del _L0_xattn_all

    def _L0_ffn_setup():
        import jax, jax.numpy as jnp
        import numpy as np
        D = 128
        H = 4
        HD = D // H
        E = 8
        FF = 512
        CAP_FACTOR = 1.0

        def _ln(x, g, b, eps=1e-05):
            mu = jnp.mean(x, -1, keepdims=True)
            v = jnp.mean((x - mu) ** 2, -1, keepdims=True)
            return (x - mu) * jax.lax.rsqrt(v + eps) * g + b

        def _mha(x, w, b, ow, ob):
            L, N, _ = x.shape
            qkv = x @ w.T + b
            q, k, v = jnp.split(qkv, 3, axis=-1)
            rh = lambda t: t.reshape(L, N, H, HD).transpose(1, 2, 0, 3)
            q, k, v = (rh(q), rh(k), rh(v))
            scores = jnp.einsum('nhld,nhmd->nhlm', q, k) / np.float32(np.sqrt(HD))
            attn = jax.nn.softmax(scores, axis=-1)
            o = jnp.einsum('nhlm,nhmd->nhld', attn, v).transpose(2, 0, 1, 3).reshape(L, N, D)
            return o @ ow.T + ob

        def _moe(x, wg, w1, b1, w2, b2):
            L, N, _ = x.shape
            S = L * N
            cap = int(CAP_FACTOR * S) // E
            xf = x.reshape(S, D)
            gates = jax.nn.softmax(xf @ wg, axis=-1)
            idx = jnp.argmax(gates, axis=-1)
            mask1 = jax.nn.one_hot(idx, E, dtype=x.dtype)
            loc = jnp.sum((jnp.cumsum(mask1, 0) - 1.0) * mask1, -1).astype(jnp.int32)
            keep = loc < cap
            gate_val = jnp.take_along_axis(gates, idx[:, None], -1)[:, 0]
            slot = jnp.where(keep, idx.astype(jnp.int32) * cap + loc, E * cap)
            disp = jnp.zeros((E * cap, D), x.dtype).at[slot].set(xf, mode='drop')
            disp = disp.reshape(E, cap, D)
            h = jnp.einsum('ecd,edf->ecf', disp, w1) + b1[:, None, :]
            y = (jnp.einsum('ecf,efd->ecd', h, w2) + b2[:, None, :]).reshape(E * cap, D)
            out = jnp.where(keep[:, None], gate_val[:, None] * y[jnp.minimum(slot, E * cap - 1)], 0.0)
            return out.reshape(L, N, D)
        key = jax.random.key(seed)
        ks = jax.random.split(key, 8)
        L, N = (128, 16)
        s = 0.02
        return {'x': jax.random.normal(ks[0], (L, N, D), jnp.float32), 'in_proj_w': jax.random.normal(ks[1], (3 * D, D), jnp.float32) * s, 'in_proj_b': jnp.zeros((3 * D,), jnp.float32), 'out_proj_w': jax.random.normal(ks[2], (D, D), jnp.float32) * s, 'out_proj_b': jnp.zeros((D,), jnp.float32), 'ln1_g': jnp.ones((D,), jnp.float32), 'ln1_b': jnp.zeros((D,), jnp.float32), 'ln2_g': jnp.ones((D,), jnp.float32), 'ln2_b': jnp.zeros((D,), jnp.float32), 'wg': jax.random.normal(ks[3], (D, E), jnp.float32) * s, 'w1': jax.random.normal(ks[4], (E, D, FF), jnp.float32) * s, 'b1': jnp.zeros((E, FF), jnp.float32), 'w2': jax.random.normal(ks[5], (E, FF, D), jnp.float32) * s, 'b2': jnp.zeros((E, D), jnp.float32)}
    _L0_ffn_all = _L0_ffn_setup()
    _L0_ffn_in = {k: v for k, v in _L0_ffn_all.items() if k in ('in_proj_w', 'in_proj_b', 'out_proj_w', 'out_proj_b', 'ln1_g', 'ln1_b', 'ln2_g', 'ln2_b', 'wg', 'w1', 'b1', 'w2', 'b2')}
    del _L0_ffn_all

    def _L1_xattn_setup():
        import jax, jax.numpy as jnp
        import numpy as np
        NUM_HEADS = 16
        DIM_HIDDEN = 128
        DIM_ATTN = DIM_HIDDEN // NUM_HEADS
        SCALE = DIM_ATTN ** (-0.5)
        TOP_K = 32

        def _split_heads(x, b, s):
            return x.reshape(b, s, NUM_HEADS, DIM_ATTN).transpose(0, 2, 1, 3)
        rng = jax.random.key(seed)
        k1, k2, k3, k4, k5 = jax.random.split(rng, 5)
        b, sq, sk, d = (2, 256, 256, DIM_HIDDEN)
        lim = 1.0 / np.sqrt(d)
        return {'query': jax.random.normal(k1, (b, sq, d), jnp.float32), 'key': jax.random.normal(k2, (b, sk, d), jnp.float32), 'value': jax.random.normal(k3, (b, sk, d), jnp.float32), 'Wq': jax.random.uniform(k4, (d, d), jnp.float32, -lim, lim), 'Wk': jax.random.uniform(k5, (d, d), jnp.float32, -lim, lim)}
    _L1_xattn_all = _L1_xattn_setup()
    _L1_xattn_in = {k: v for k, v in _L1_xattn_all.items() if k in ('Wq', 'Wk')}
    del _L1_xattn_all

    def _L1_ffn_setup():
        import jax, jax.numpy as jnp
        import numpy as np
        DIM = 128

        def _reference_tuple_inner(x, W_r, W_k, W_v, mu_r, mu_k):
            B, T, C = x.shape
            x_prev = jnp.concatenate([jnp.zeros((B, 1, C), x.dtype), x[:, :-1, :]], axis=1)
            xr = mu_r * x + (1.0 - mu_r) * x_prev
            xk = mu_k * x + (1.0 - mu_k) * x_prev
            r = jax.nn.sigmoid(jnp.einsum('btc,dc->btd', xr, W_r))
            k = jnp.einsum('btc,dc->btd', xk, W_k)
            k_act = jnp.square(jax.nn.relu(k))
            out = r * jnp.einsum('btc,dc->btd', k_act, W_v)
            new_state = x[:, -1, :]
            return (out, new_state)
        key = jax.random.key(seed)
        ks = jax.random.split(key, 6)
        B, T, C = (8, 256, DIM)
        x = jax.random.normal(ks[0], (B, T, C), dtype=jnp.float32)
        s = 1.0 / np.sqrt(C)
        W_r = jax.random.uniform(ks[1], (C, C), jnp.float32, -s, s)
        W_k = jax.random.uniform(ks[2], (C, C), jnp.float32, -s, s)
        W_v = jax.random.uniform(ks[3], (C, C), jnp.float32, -s, s)
        mu_r = jax.random.uniform(ks[4], (C,), jnp.float32)
        mu_k = jax.random.uniform(ks[5], (C,), jnp.float32)
        return {'x': x, 'W_r': W_r, 'W_k': W_k, 'W_v': W_v, 'mu_r': mu_r, 'mu_k': mu_k}
    _L1_ffn_all = _L1_ffn_setup()
    _L1_ffn_in = {k: v for k, v in _L1_ffn_all.items() if k in ('W_r', 'W_k', 'W_v', 'mu_r', 'mu_k')}
    del _L1_ffn_all
    return {'x': x, 'ctx_1024': ctx_1024, 'mask_BxS2_bf1': mask_BxS2_bf1, 'L0_xattn_Wq': _L0_xattn_in['Wq'], 'L0_xattn_bq': _L0_xattn_in['bq'], 'L0_xattn_Wk': _L0_xattn_in['Wk'], 'L0_xattn_bk': _L0_xattn_in['bk'], 'L0_xattn_Wv': _L0_xattn_in['Wv'], 'L0_xattn_bv': _L0_xattn_in['bv'], 'L0_xattn_Wo': _L0_xattn_in['Wo'], 'L0_xattn_bo': _L0_xattn_in['bo'], 'L0_ffn_in_proj_w': _L0_ffn_in['in_proj_w'], 'L0_ffn_in_proj_b': _L0_ffn_in['in_proj_b'], 'L0_ffn_out_proj_w': _L0_ffn_in['out_proj_w'], 'L0_ffn_out_proj_b': _L0_ffn_in['out_proj_b'], 'L0_ffn_ln1_g': _L0_ffn_in['ln1_g'], 'L0_ffn_ln1_b': _L0_ffn_in['ln1_b'], 'L0_ffn_ln2_g': _L0_ffn_in['ln2_g'], 'L0_ffn_ln2_b': _L0_ffn_in['ln2_b'], 'L0_ffn_wg': _L0_ffn_in['wg'], 'L0_ffn_w1': _L0_ffn_in['w1'], 'L0_ffn_b1': _L0_ffn_in['b1'], 'L0_ffn_w2': _L0_ffn_in['w2'], 'L0_ffn_b2': _L0_ffn_in['b2'], 'L1_xattn_Wq': _L1_xattn_in['Wq'], 'L1_xattn_Wk': _L1_xattn_in['Wk'], 'L1_ffn_W_r': _L1_ffn_in['W_r'], 'L1_ffn_W_k': _L1_ffn_in['W_k'], 'L1_ffn_W_v': _L1_ffn_in['W_v'], 'L1_ffn_mu_r': _L1_ffn_in['mu_r'], 'L1_ffn_mu_k': _L1_ffn_in['mu_k']}

def reference(x, ctx_1024, mask_BxS2_bf1, L0_xattn_Wq, L0_xattn_bq, L0_xattn_Wk, L0_xattn_bk, L0_xattn_Wv, L0_xattn_bv, L0_xattn_Wo, L0_xattn_bo, L0_ffn_in_proj_w, L0_ffn_in_proj_b, L0_ffn_out_proj_w, L0_ffn_out_proj_b, L0_ffn_ln1_g, L0_ffn_ln1_b, L0_ffn_ln2_g, L0_ffn_ln2_b, L0_ffn_wg, L0_ffn_w1, L0_ffn_b1, L0_ffn_w2, L0_ffn_b2, L1_xattn_Wq, L1_xattn_Wk, L1_ffn_W_r, L1_ffn_W_k, L1_ffn_W_v, L1_ffn_mu_r, L1_ffn_mu_k):
    import jax
    import jax.numpy as jnp

    def _L0_xattn_ref(q, k, v, attention_mask, Wq, bq, Wk, bk, Wv, bv, Wo, bo):
        import jax, jax.numpy as jnp
        import numpy as np
        N_HEADS = 16
        D_MODEL = 128
        HEAD_DIM = D_MODEL // N_HEADS
        MASK_FILL = -100000000.0

        def _split_heads(x):
            B, S, _ = x.shape
            return x.reshape(B, S, N_HEADS, HEAD_DIM).transpose(0, 2, 1, 3)
        qm = _split_heads(q @ Wq.T + bq)
        km = _split_heads(k @ Wk.T + bk)
        vm = _split_heads(v @ Wv.T + bv)
        scores = jnp.einsum('bnlh,bnph->bnlp', qm, km) / np.sqrt(HEAD_DIM).astype(np.float32)
        mask = attention_mask[:, None, None, :]
        scores = jnp.where(mask, scores, MASK_FILL)
        attn = jax.nn.softmax(scores, axis=-1)
        out = jnp.einsum('bnlp,bnph->bnlh', attn, vm)
        B, _, L, _ = out.shape
        out = out.transpose(0, 2, 1, 3).reshape(B, L, D_MODEL)
        return out @ Wo.T + bo

    def _L0_ffn_ref(x, in_proj_w, in_proj_b, out_proj_w, out_proj_b, ln1_g, ln1_b, ln2_g, ln2_b, wg, w1, b1, w2, b2):
        import jax, jax.numpy as jnp
        import numpy as np
        D = 128
        H = 4
        HD = D // H
        E = 8
        FF = 512
        CAP_FACTOR = 1.0

        def _ln(x, g, b, eps=1e-05):
            mu = jnp.mean(x, -1, keepdims=True)
            v = jnp.mean((x - mu) ** 2, -1, keepdims=True)
            return (x - mu) * jax.lax.rsqrt(v + eps) * g + b

        def _mha(x, w, b, ow, ob):
            L, N, _ = x.shape
            qkv = x @ w.T + b
            q, k, v = jnp.split(qkv, 3, axis=-1)
            rh = lambda t: t.reshape(L, N, H, HD).transpose(1, 2, 0, 3)
            q, k, v = (rh(q), rh(k), rh(v))
            scores = jnp.einsum('nhld,nhmd->nhlm', q, k) / np.float32(np.sqrt(HD))
            attn = jax.nn.softmax(scores, axis=-1)
            o = jnp.einsum('nhlm,nhmd->nhld', attn, v).transpose(2, 0, 1, 3).reshape(L, N, D)
            return o @ ow.T + ob

        def _moe(x, wg, w1, b1, w2, b2):
            L, N, _ = x.shape
            S = L * N
            cap = int(CAP_FACTOR * S) // E
            xf = x.reshape(S, D)
            gates = jax.nn.softmax(xf @ wg, axis=-1)
            idx = jnp.argmax(gates, axis=-1)
            mask1 = jax.nn.one_hot(idx, E, dtype=x.dtype)
            loc = jnp.sum((jnp.cumsum(mask1, 0) - 1.0) * mask1, -1).astype(jnp.int32)
            keep = loc < cap
            gate_val = jnp.take_along_axis(gates, idx[:, None], -1)[:, 0]
            slot = jnp.where(keep, idx.astype(jnp.int32) * cap + loc, E * cap)
            disp = jnp.zeros((E * cap, D), x.dtype).at[slot].set(xf, mode='drop')
            disp = disp.reshape(E, cap, D)
            h = jnp.einsum('ecd,edf->ecf', disp, w1) + b1[:, None, :]
            y = (jnp.einsum('ecf,efd->ecd', h, w2) + b2[:, None, :]).reshape(E * cap, D)
            out = jnp.where(keep[:, None], gate_val[:, None] * y[jnp.minimum(slot, E * cap - 1)], 0.0)
            return out.reshape(L, N, D)
        y1 = _ln(x + _mha(x, in_proj_w, in_proj_b, out_proj_w, out_proj_b), ln1_g, ln1_b)
        y2 = _ln(y1 + _moe(y1, wg, w1, b1, w2, b2), ln2_g, ln2_b)
        return y2

    def _L1_xattn_ref(query, key, value, Wq, Wk):
        import jax, jax.numpy as jnp
        import numpy as np
        NUM_HEADS = 16
        DIM_HIDDEN = 128
        DIM_ATTN = DIM_HIDDEN // NUM_HEADS
        SCALE = DIM_ATTN ** (-0.5)
        TOP_K = 32

        def _split_heads(x, b, s):
            return x.reshape(b, s, NUM_HEADS, DIM_ATTN).transpose(0, 2, 1, 3)
        b, sq, d = query.shape
        sk = key.shape[1]
        q = _split_heads(query @ Wq.T, b, sq)
        k = _split_heads(key @ Wk.T, b, sk)
        v = _split_heads(value, b, sk)
        scores = jnp.einsum('bhqa,bhka->bhqk', q, k) * SCALE
        top_vals = jax.lax.top_k(scores, TOP_K)[0]
        cutoff = top_vals[..., -1:]
        masked = jnp.where(scores >= cutoff, scores, -jnp.inf)
        w = jax.nn.softmax(masked, axis=-1)
        e = jnp.einsum('bhqk,bhka->bhqa', w, v)
        return e.transpose(0, 2, 1, 3).reshape(b, sq, d)

    def _L1_ffn_ref(x, W_r, W_k, W_v, mu_r, mu_k):
        import jax, jax.numpy as jnp
        import numpy as np
        DIM = 128

        def _reference_tuple_inner(x, W_r, W_k, W_v, mu_r, mu_k):
            B, T, C = x.shape
            x_prev = jnp.concatenate([jnp.zeros((B, 1, C), x.dtype), x[:, :-1, :]], axis=1)
            xr = mu_r * x + (1.0 - mu_r) * x_prev
            xk = mu_k * x + (1.0 - mu_k) * x_prev
            r = jax.nn.sigmoid(jnp.einsum('btc,dc->btd', xr, W_r))
            k = jnp.einsum('btc,dc->btd', xk, W_k)
            k_act = jnp.square(jax.nn.relu(k))
            out = r * jnp.einsum('btc,dc->btd', k_act, W_v)
            new_state = x[:, -1, :]
            return (out, new_state)
        return _reference_tuple_inner(x, W_r, W_k, W_v, mu_r, mu_k)[0]
    x = x + _L0_xattn_ref(_layernorm(x, axis=-1), ctx_1024, ctx_1024, mask_BxS2_bf1, L0_xattn_Wq, L0_xattn_bq, L0_xattn_Wk, L0_xattn_bk, L0_xattn_Wv, L0_xattn_bv, L0_xattn_Wo, L0_xattn_bo)
    x = x + _L0_ffn_ref(_layernorm(x, axis=-1), L0_ffn_in_proj_w, L0_ffn_in_proj_b, L0_ffn_out_proj_w, L0_ffn_out_proj_b, L0_ffn_ln1_g, L0_ffn_ln1_b, L0_ffn_ln2_g, L0_ffn_ln2_b, L0_ffn_wg, L0_ffn_w1, L0_ffn_b1, L0_ffn_w2, L0_ffn_b2)
    x = x + _L1_xattn_ref(_layernorm(x, axis=-1), ctx_1024, ctx_1024, L1_xattn_Wq, L1_xattn_Wk)
    x = x + _L1_ffn_ref(_layernorm(x, axis=-1), L1_ffn_W_r, L1_ffn_W_k, L1_ffn_W_v, L1_ffn_mu_r, L1_ffn_mu_k)
    return x

_drawn_inputs = setup_inputs


def setup_inputs(seed=0):
    import zlib

    import numpy as np

    out = dict(_drawn_inputs(seed))
    spreads = {'L0_xattn_bq': (0.0, 0.33),
     'L0_xattn_bk': (0.0, 0.8),
     'L0_xattn_bv': (0.0, 0.1),
     'L0_xattn_bo': (0.0, 0.1),
     'L0_ffn_in_proj_b': (0.0, 0.588),
     'L0_ffn_out_proj_b': (0.0, 0.1),
     'L0_ffn_ln1_g': (1.0, 0.2),
     'L0_ffn_ln1_b': (0.0, 0.1),
     'L0_ffn_ln2_g': (1.0, 0.2),
     'L0_ffn_ln2_b': (0.0, 0.1),
     'L0_ffn_b1': (0.0, 0.8),
     'L0_ffn_b2': (0.0, 0.8)}
    factors = {'L0_ffn_in_proj_w': 4.202,
     'L0_ffn_out_proj_w': 3.263,
     'L0_ffn_wg': 5.225,
     'L0_ffn_w1': 6.59,
     'L0_ffn_w2': 6.139,
     'L1_ffn_W_r': 6.093,
     'L1_ffn_mu_r': 8.0,
     'L1_ffn_mu_k': 2.782}
    for name, (base, spread) in spreads.items():
        noise = np.random.default_rng([zlib.crc32(name.encode()), seed]).standard_normal(out[name].shape)
        drawn = base * np.exp(spread * noise) if base else spread * noise
        out[name] = jnp.asarray(drawn.astype(out[name].dtype))
    for name, factor in factors.items():
        out[name] = (out[name] * factor).astype(out[name].dtype)
    return out
```

```python
from contextlib import ExitStack

import concourse.bass as bass
from concourse import mybir

P = 128
B, SEQ, D = 4, 512, 128
NJ = SEQ // P
NT = B * NJ
KEYS = 77
H, HD = 16, 8
G = 4
HG = H // G
GW = HG * KEYS
SW = H * KEYS
NCH = -(-SW // P)
LAST = SW - (NCH - 1) * P
VW = D + H
TOPK = 32
MH, MHD = 4, 32
E, FF = 8, 512
FC = FF // P
CAP = B * SEQ // E
EPS = 1e-5
MASK_FILL = -1e8
SCALE = float(HD) ** -0.5
MSCALE = float(MHD) ** -0.5
GONE = -3.0e38
TINY = 1e-30

F32 = mybir.dt.float32
BF16 = mybir.dt.bfloat16
U8 = mybir.dt.uint8
ALU = mybir.AluOpType
ACT = mybir.ActivationFunctionType
AX = mybir.AxisListType.X

CONSTS = dict(ident=P, tri=P, blk=HG, prio=E, notfirst=NT, headmask=NCH * VW)
WEIGHTS = dict(wk0=D, wv0=D, wq0=D, wo0=D, inw=3 * D, outw=D, wq1=D, wk1=D, wr=D, wk=D, wv=D, wg=E)
COLS = dict(bq=1, bk=1, bv=1, mur=1, muk=1)
ROWS = dict(bo=D, inb=3 * D, ob=D, g1=D, b1=D, g2=D, b2=D)


def parts(ap, widths):
    at, out = 0, {}
    for name, width in widths.items():
        out[name] = ap[:, at:at + width]
        at += width
    return out


def fill_parts():
    import numpy as np
    rest = np.float32(MASK_FILL / SCALE)
    out = []
    for _ in range(3):
        top = (rest.view(np.uint32) & np.uint32(0xFFFF0000)).view(np.float32)
        out.append(float(top))
        rest = np.float32(rest - top)
    return out


def build(nc, x, ctxT, mask, consts_d, weights_d, cols_d, rows_d, b1T_d, b2_d, w1T_d, w2_d, out):
    with ExitStack() as stack:
        def sb(name, shape, dt=F32):
            return stack.enter_context(nc.sbuf_tensor(name, shape, dt))

        def pb(name, shape, dt=F32):
            return stack.enter_context(nc.psum_tensor(name, shape, dt))

        def sem(name):
            return stack.enter_context(nc.semaphore(name))

        consts = sb("consts", [P, sum(CONSTS.values())])
        C = parts(consts, CONSTS)
        weights = sb("weights", [P, sum(WEIGHTS.values())])
        Wt = parts(weights, WEIGHTS)
        cols = sb("cols", [P, len(COLS)])
        Cl = parts(cols, COLS)
        rows = sb("rows", [P, sum(ROWS.values())])
        Rw = parts(rows, ROWS)
        ident, tri, blk = C["ident"], C["tri"], C["blk"]
        headmask = C["headmask"].rearrange("p (c n) -> p c n", n=VW)
        ones = sb("ones", [P, P])
        expo = sb("expo", [P, HG])
        tiny = sb("tiny", [P, 1])

        xs = sb("xs", [P, NT, D])
        x1 = sb("x1", [P, NT, D])
        yg = sb("yg", [P, NT, D + E])
        x2 = sb("x2", [P, 4, D])

        ctx_sb = sb("ctx_sb", [P, B, KEYS])
        area_a = sb("area_a", [P, 4 * SW])
        area_b = sb("area_b", [P, B * NCH * P])
        ctxrep = area_b.rearrange("p (b n) -> p b n", b=B)
        mask_u8 = sb("mask_u8", [P, B, KEYS], U8)
        mask_f = sb("mask_f", [P, B, KEYS])
        mrow = sb("mrow", [65, B, HG, KEYS], BF16)
        mones = sb("mones", [65, P], BF16)
        k0 = sb("k0", [P, B, KEYS])
        k1 = sb("k1", [P, B, KEYS])
        kblk0 = sb("kblk0", [P, B, HG, KEYS])
        kblk1 = sb("kblk1", [P, B, HG, KEYS])
        vblk0 = sb("vblk0", [P, B, NCH, VW])
        vblk1 = sb("vblk1", [P, B, NCH, VW])

        stats = sb("stats", [P, NJ, 6])
        mv = sb("mv", [P, NJ, 2])
        veps = sb("veps", [P, NJ])
        rstd = sb("rstd", [P, NJ])
        xn = sb("xn", [P, B, D])
        xnT = sb("xnT", [P, B, P])
        q0T = sb("q0T", [P, B, P])
        mx0 = sb("mx0", [P, H])
        d0 = sb("d0", [P, H, KEYS])
        e0 = sb("e0", [P, SW])
        pT = sb("pT", [P, NCH, P])
        rden = sb("rden", [P, H])
        at0 = sb("at0", [P, D])
        at0T = sb("at0T", [P, P])
        zt = sb("zt", [P, B, D])
        zob = sb("zob", [P, B, D])
        qkv = sb("qkv", [P, B, 3 * D])
        prod = sb("prod", [P, B, 4 * D])
        sc = sb("sc", [P, B, B, MH])
        scx = sb("scx", [P, B, MH])
        sce = sb("sce", [P, B, B, MH])
        scs = sb("scs", [P, B, MH])
        scr = sb("scr", [P, B, MH])
        oo = sb("oo", [P, B, D])
        y1s = sb("y1s", [P, B, D])
        gmx = sb("gmx", [P, B])
        gd = sb("gd", [P, B, E])
        geq = sb("geq", [P, B, E])
        ge = sb("ge", [P, B, E])
        gsum = sb("gsum", [P, B])
        gval = sb("gval", [P, B])
        gp = sb("gp", [P, B, E])
        gpm = sb("gpm", [P, B])
        oh = sb("oh", [P, NT, E])
        ohg = sb("ohg", [P, NT, E])
        before = sb("before", [P, NT, E])

        w1T = area_a[:, 0:FC * E * D].rearrange("p (c e n) -> p c e n", c=FC, e=E)
        w2 = area_b[:, 0:FC * E * D].rearrange("p (c e n) -> p c e n", c=FC, e=E)
        b1T = sb("b1T", [P, FC, E])
        b1z = sb("b1z", [P, FC, E * E])
        b2 = sb("b2", [E, D])
        w12 = qkv.rearrange("p b n -> p (b n)")[:, 0:E * D].rearrange("p (e n) -> p e n", e=E)
        b12 = sb("b12", [E, D])
        omu = sb("omu", [P, 2])
        wr_now = sb("wr_now", [P, D])
        wr_prev = sb("wr_prev", [P, D])
        wk_now = sb("wk_now", [P, D])
        wk_prev = sb("wk_prev", [P, D])

        cur = sb("cur", [P, D + E])
        kcur = sb("kcur", [P, GW])
        y1T = sb("y1T", [P, P])
        gT = sb("gT", [E, P])
        mparts = prod.rearrange("p b n -> p (b n)")[:, 0:(E + 1) * D].rearrange("p (e n) -> p e n", n=D)
        res2 = sb("res2", [P, D])
        junk = sb("junk", [P, 3, D])
        lsum = sb("lsum", [P, 3])
        lneg = sb("lneg", [P, 3])
        lsq = sb("lsq", [P, 3])
        lvar = sb("lvar", [P, 3])
        lrs = sb("lrs", [P, 3])
        lnm = sb("lnm", [P, 3])
        yn = zob[:, 0]
        z2 = zob[:, 1]
        z2T = zob[:, 2]
        q1T = zob[:, 3]
        skeep = area_a.rearrange("p (a h k) -> p a h k", a=4, h=H)
        fresh = area_b[:, 3 * SW:4 * SW].rearrange("p (h k) -> p h k", h=H)
        left = area_b[:, 0 * SW:1 * SW].rearrange("p (h k) -> p h k", h=H)
        top = sb("top", [P, TOPK // 8, H, 8])
        mxc = sb("mxc", [P, 2, H])
        dif = d0
        cut = area_b[:, 1 * SW:2 * SW].rearrange("p (h k) -> p h k", h=H)
        ex1 = area_b[:, 2 * SW:3 * SW].rearrange("p (h k) -> p h k", h=H)
        p1 = e0
        pT1 = pT
        rden1 = sb("rden1", [P, H])
        att1 = sb("att1", [P, D])
        x3 = sb("x3", [P, 2, D])
        zf = sb("zf", [P, D])
        zfT = sb("zfT", [P, P + 1])
        ka = y1s[:, 0]
        er = y1s[:, 1]
        vv = y1s[:, 2]
        fin = sb("fin", [P, D])

        psS = pb("psS", [P, G, 512])
        psT = pb("psT", [P, 2, 512])
        psM = pb("psM", [P, 2, 512])
        psM0, psM1 = psM[:, 0], psM[:, 1]

        def score_banks(ap):
            return psS[:, :, 0:GW].rearrange("p g (i k) -> p g i k", k=KEYS) if ap is None else ap

        names = """x_in ctx_in mask_in consts_in weights_in w1_in w2_in k0_made k1_made k0_copied k1_copied mask_cast
        mrow_made k0_masked kblk0_made kblk1_made ctx_rep v_turned v_masked den_cols xbo_made h_xn h_turned
        h_xnT h_q h_qT s_made s_max s_sub s_exp t_turned t_copiedA t_copiedV pv_made pv_den pv_norm o_turned
        o_T o_proj x1_made q_z q_turned q_zT q_made q_stored zob_made m_prod m_sc m_sub m_exp m_w m_pv m_o
        m_turned m_oT m_proj m_res y_n y_g y_made y_stored y_turned y_T lg_made g_d g_exp seen pos_made
        gates_set w12_made w12_stored b1_spread b12_made b12_stored cur_set kcur_set c_turned c_copied mb_made mb_out
        mty n2_sum n2_neg n2_sq n2_step n2_nm n2_out x2_set n3_sum n3_neg n3_sq n3_step n3_nm n3_out z_turned
        z_T q1_made q1_T S_ready S_kept S_fresh S_read topk_step mx_copied dif_set cut_set exp_set sign_set keep_set
        p_set p_turned p_copied a_made a_den a_norm x3_set n4_sum n4_neg n4_sq n4_step n4_nm n4_out f_turned
        f_prev f_T f_kr f_relu f_sq f_r f_v f_vv f_one passed f_mul f_fin stored constants_set ln_stats
        ln_mv ln_veps ln_rstd m_soft g_step m_tree y2_step""".split()
        s = {n: sem(n) for n in names}

        def hold(e, semaphore, value, alone=False):
            if isinstance(value, int):
                if value > 0:
                    e.wait_ge(semaphore, value)
                return
            if not alone:
                e.wait_ge(s["constants_set"], 1)
            e.wait_ge(semaphore, value)
            if alone:
                e.sem_inc(s["passed"], 1)

        block = stack.enter_context(nc.Block())

        @block.sync
        def _(e):
            e.dma_start(ctx_sb[:], ctxT).then_inc(s["ctx_in"], 16)
            e.dma_start(weights[:], weights_d).then_inc(s["weights_in"], 16)
            e.dma_start(cols[:], cols_d).then_inc(s["weights_in"], 16)
            e.dma_start(mask_u8[:], mask.broadcast_to([P, B * KEYS]).rearrange("p (b k) -> p b k", b=B)).then_inc(s["mask_in"], 16)
            e.dma_start(xs[:], x).then_inc(s["x_in"], 16)
            e.dma_start(rows[:], rows_d.broadcast_to([P, sum(ROWS.values())])).then_inc(s["x_in"], 16)
            e.dma_start(b1T[:], b1T_d).then_inc(s["w2_in"], 16)
            e.dma_start(b2[:], b2_d).then_inc(s["w2_in"], 16)
            e.dma_start(w1T, w1T_d).then_inc(s["w1_in"], 16)
            e.wait_ge(s["v_turned"], 2 * B * 3)
            e.dma_start(w2, w2_d).then_inc(s["w2_in"], 16)
            with e.Fori(0, NT) as t:
                hold(e, s["f_fin"], t + 1)
                e.dma_start(out[t], fin[:]).then_inc(s["stored"], 16)
            e.wait_ge(s["stored"], 16 * NT)

        @block.gpsimd
        def _(e):
            e.memset(ones[:], 1.0).then_inc(s["constants_set"], 1)
            e.memset(expo[:], -0.5).then_inc(s["constants_set"], 1)
            e.memset(tiny[:], TINY).then_inc(s["constants_set"], 1)
            e.memset(mones[:], 1.0).then_inc(s["constants_set"], 1)
            e.memset(mrow[:], 0.0).then_inc(s["constants_set"], 1)
            e.memset(ctxrep[:, :, SW:], 0.0).then_inc(s["constants_set"], 1)
            e.memset(b1z[:], 0.0).then_inc(s["constants_set"], 1)
            e.memset(zfT[:], 0.0).then_inc(s["constants_set"], 1)
            e.wait_ge(s["consts_in"], 16)
            for v in (vblk0, vblk1):
                for b in range(B):
                    e.tensor_copy(v[:, b, :, D:VW], headmask[:, :, D:VW]).then_inc(s["den_cols"], 1)
            e.wait_ge(s["k1_copied"], 1)
            for b in range(B):
                e.tensor_tensor(kblk1[:, b], k1[:, b, None, :].broadcast_to([P, HG, KEYS]),
                                blk[:, :, None].broadcast_to([P, HG, KEYS]), ALU.mult).then_inc(s["kblk1_made"], 1)
            e.wait_ge(s["x_in"], 32)
            e.tensor_tensor(x1[:], xs[:], Rw["bo"][:, None, :].broadcast_to([P, NT, D]), ALU.add).then_inc(s["xbo_made"], 1)

            def rstd_of(n):
                hold(e, s["ln_veps"], n + 1)
                e.tensor_tensor(rstd[:], veps[:], expo[:], ALU.pow).then_inc(s["ln_rstd"], 1)

            e.wait_ge(s["constants_set"], 2)
            def group(j):
                rstd_of(3 * j)
                rstd_of(3 * j + 1)
                hold(e, s["q_z"], B * j + B)
                hold(e, s["m_res"], j)
                e.tensor_tensor(zob[:], zt[:], Rw["ob"][:, None, :].broadcast_to([P, B, D]), ALU.add).then_inc(s["zob_made"], 1)
                hold(e, s["q_stored"], B * j + B)
                for l in range(B):
                    hold(e, s["m_o"], B * j)
                    e.tensor_tensor(prod[:, l].rearrange("p (m n) -> p m n", m=B),
                                    qkv[:, l, None, 0:D].broadcast_to([P, B, D]),
                                    qkv[:, :, D:2 * D], ALU.mult).then_inc(s["m_prod"], 1)
                hold(e, s["m_w"], j + 1)
                for l in range(B):
                    hold(e, s["m_sc"], B * j + l + 1)
                    e.tensor_tensor(prod[:, l].rearrange("p (h d m) -> p h d m", h=MH, m=B),
                                    qkv[:, :, 2 * D:3 * D].rearrange("p m (h d) -> p h d m", h=MH),
                                    sc[:, l].rearrange("p m h -> p h m")[:, :, None, :].broadcast_to([P, MH, MHD, B]),
                                    ALU.mult).then_inc(s["m_pv"], 1)
                rstd_of(3 * j + 2)
                hold(e, s["y_n"], B * j + B)
                hold(e, s["y_turned"], j)
                hold(e, s["y_stored"], j)
                e.tensor_tensor(y1s[:], oo[:], Rw["g1"][:, None, :].broadcast_to([P, B, D]), ALU.mult).then_inc(s["y_g"], 1)
                hold(e, s["y_g"], j + 1)
                e.tensor_tensor(y1s[:], y1s[:], Rw["b1"][:, None, :].broadcast_to([P, B, D]), ALU.add).then_inc(s["y_made"], 1)
                hold(e, s["y_made"], j + 1)
                e.tensor_copy(yg.rearrange("p (b j) n -> p b j n", b=B)[:, :, j, 0:D], y1s[:]).then_inc(s["y_stored"], 1)

            group(0)
            with e.Fori(1, NJ) as j:
                group(j)

            def ln_scalars(k, t, n_sum, n_neg, n_sq, n_step, n_nm):
                def first():
                    hold(e, n_sum, t + 1, alone=True)
                    e.tensor_scalar(lneg[:, k:k + 1], lsum[:, k:k + 1], -1.0 / D, None, ALU.mult).then_inc(n_neg, 1)

                def second():
                    hold(e, n_sq, t + 1, alone=True)
                    e.tensor_scalar(lvar[:, k:k + 1], lsq[:, k:k + 1], 1.0 / D, EPS, ALU.mult, ALU.add).then_inc(n_step, 1)
                    hold(e, n_step, 2 * t + 1)
                    e.tensor_tensor(lrs[:, k:k + 1], lvar[:, k:k + 1], expo[:, 0:1], ALU.pow).then_inc(n_step, 1)
                    hold(e, n_step, 2 * t + 2)
                    e.tensor_tensor(lnm[:, k:k + 1], lneg[:, k:k + 1], lrs[:, k:k + 1], ALU.mult).then_inc(n_nm, 1)
                return first, second

            def front(t):
                n2a, n2b = ln_scalars(0, t, s["n2_sum"], s["n2_neg"], s["n2_sq"], s["n2_step"], s["n2_nm"])
                n3a, n3b = ln_scalars(1, t, s["n3_sum"], s["n3_neg"], s["n3_sq"], s["n3_step"], s["n3_nm"])

                def load():
                    if isinstance(t, int) and t == 0:
                        e.wait_ge(s["gates_set"], 1)
                    hold(e, s["c_turned"], t)
                    hold(e, s["mb_out"], 3 * t)
                    hold(e, s["mty"], t)
                    e.tensor_copy(cur[:], yg[:, t, :]).then_inc(s["cur_set"], 1)
                    hold(e, s["S_ready"], t)
                    e.tensor_copy(kcur[:], kblk1.rearrange("p b i k -> p b (i k)")[:, t // NJ]).then_inc(s["kcur_set"], 1)

                def tree():
                    hold(e, s["mb_out"], 3 * t + 3)
                    e.tensor_tensor(mparts[:, 0:4], mparts[:, 0:4], mparts[:, 4:8], ALU.add).then_inc(s["m_tree"], 1)
                    hold(e, s["m_tree"], 4 * t + 1)
                    e.tensor_tensor(mparts[:, 0:2], mparts[:, 0:2], mparts[:, 2:4], ALU.add).then_inc(s["m_tree"], 1)
                    hold(e, s["m_tree"], 4 * t + 2)
                    e.tensor_tensor(mparts[:, 0], mparts[:, 0], mparts[:, 1], ALU.add).then_inc(s["m_tree"], 1)
                    hold(e, s["m_tree"], 4 * t + 3)
                    e.tensor_tensor(mparts[:, 8], mparts[:, 8], mparts[:, 0], ALU.add).then_inc(s["m_tree"], 1)
                    hold(e, s["m_tree"], 4 * t + 4)
                    hold(e, s["n2_out"], t)
                    e.tensor_tensor(res2[:], mparts[:, 8], cur[:, 0:D], ALU.add).then_inc(s["mty"], 1)

                def affine():
                    hold(e, s["n2_out"], t + 1)
                    e.tensor_tensor(yn, yn, Rw["g2"], ALU.mult).then_inc(s["y2_step"], 1)
                    hold(e, s["y2_step"], 2 * t + 1)
                    e.tensor_tensor(yn, yn, Rw["b2"], ALU.add).then_inc(s["y2_step"], 1)
                    hold(e, s["y2_step"], 2 * t + 2)
                    e.tensor_tensor(x2[:, t % 4], yn, x1[:, t], ALU.add).then_inc(s["x2_set"], 1)
                return dict(load=load, tree=tree, neg2=n2a, scale2=n2b, affine=affine, neg3=n3a, scale3=n3b)

            def weigh(t):
                def a():
                    hold(e, s["mx_copied"], 2 * t + 2)
                    hold(e, s["S_kept"], t + 1)
                    hold(e, s["exp_set"], t)
                    e.tensor_tensor(dif[:], skeep[:, t % 4], mxc[:, 0, :, None].broadcast_to([P, H, KEYS]), ALU.subtract)\
                        .then_inc(s["dif_set"], 1)

                def b():
                    hold(e, s["p_set"], t)
                    e.tensor_tensor(cut, skeep[:, t % 4], mxc[:, 1, :, None].broadcast_to([P, H, KEYS]), ALU.subtract)\
                        .then_inc(s["cut_set"], 1)

                def c():
                    hold(e, s["exp_set"], t + 1)
                    hold(e, s["keep_set"], t + 1)
                    hold(e, s["p_turned"], 3 * t)
                    e.tensor_tensor(p1.rearrange("p (h k) -> p h k", k=KEYS), ex1, cut, ALU.mult).then_inc(s["p_set"], 1)

                def d():
                    hold(e, s["a_norm"], t + 1)
                    e.tensor_tensor(x3[:, t % 2], x2[:, t % 4], att1[:], ALU.add).then_inc(s["x3_set"], 1)
                return dict(dif=a, cut=b, product=c, x3=d)

            def ffn(t):
                n4a, n4b = ln_scalars(2, t, s["n4_sum"], s["n4_neg"], s["n4_sq"], s["n4_step"], s["n4_nm"])

                def one():
                    hold(e, s["f_r"], t + 1, alone=True)
                    e.tensor_scalar(er, er, 0.5, 0.5, ALU.mult, ALU.add).then_inc(s["f_one"], 1)

                def end():
                    hold(e, s["f_one"], t + 1)
                    hold(e, s["f_vv"], t + 1)
                    e.tensor_tensor(vv, vv, er, ALU.mult).then_inc(s["f_mul"], 1)
                    hold(e, s["f_mul"], t + 1)
                    hold(e, s["stored"], 16 * t)
                    e.tensor_tensor(fin[:], x3[:, t % 2], vv, ALU.add).then_inc(s["f_fin"], 1)
                return dict(neg4=n4a, scale4=n4b, half=one, end=end)

            run_tiles(e, front, lambda t: {}, weigh, ffn)

        @block.scalar
        def _(e):
            e.dma_start(consts[:], consts_d).then_inc(s["consts_in"], 16)
            e.wait_ge(s["weights_in"], 32)
            e.wait_ge(s["k0_made"], 1)
            e.activation(k0.rearrange("p b k -> p (b k)"), psM0[:, 0:B * KEYS], ACT.Identity, bias=Cl["bk"]).then_inc(s["k0_copied"], 1)
            e.wait_ge(s["k1_made"], 1)
            e.activation(k1.rearrange("p b k -> p (b k)"), psM1[:, 0:B * KEYS], ACT.Copy).then_inc(s["k1_copied"], 1)
            e.wait_ge(s["ctx_in"], 16)
            for b in range(B):
                e.activation(ctxrep[:, b, 0:SW].rearrange("p (h k) -> p h k", k=KEYS),
                             ctx_sb[:, b, None, :].broadcast_to([P, H, KEYS]), ACT.Copy).then_inc(s["ctx_rep"], 1)

            def group(j):
                hold(e, s["h_turned"], j + 1)
                hold(e, s["h_q"], j)
                e.activation(xnT.rearrange("p b n -> p (b n)"), psM0, ACT.Copy).then_inc(s["h_xnT"], 1)
                hold(e, s["h_q"], j + 1)
                hold(e, s["s_made"], B * j)
                e.activation(q0T.rearrange("p b n -> p (b n)"), psM1, ACT.Identity, bias=Cl["bq"]).then_inc(s["h_qT"], 1)
                for b in range(B):
                    u = B * j + b
                    hold(e, s["s_sub"], u + 1)
                    hold(e, s["t_turned"], 3 * u)
                    e.activation(e0[:], d0.rearrange("p h k -> p (h k)"), ACT.Exp, scale=SCALE).then_inc(s["s_exp"], 1)
                    hold(e, s["pv_made"], u)
                    for g in (0, 2):
                        hold(e, s["t_turned"], 3 * u + g + 1)
                        if g == 0:
                            e.activation(pT[:, 0:4].rearrange("p c n -> p (c n)"), psT[:, 0], ACT.Copy).then_inc(s["t_copiedA"], 1)
                        else:
                            e.activation(pT[:, 8], psT[:, 0, 0:P], ACT.Copy).then_inc(s["t_copiedA"], 1)
                            e.activation(pT[0:LAST, 9], psT[0:LAST, 0, P:2 * P], ACT.Copy).then_inc(s["t_copiedA"], 1)
                    hold(e, s["o_turned"], u + 1)
                    hold(e, s["o_proj"], u)
                    e.activation(at0T[:], psM0[:, 256:384], ACT.Identity, bias=Cl["bv"]).then_inc(s["o_T"], 1)
                hold(e, s["q_turned"], j + 1)
                hold(e, s["q_made"], B * j)
                e.activation(xnT.rearrange("p b n -> p (b n)"), psM0, ACT.Copy).then_inc(s["q_zT"], 1)
                hold(e, s["m_sub"], j + 1)
                e.activation(sce[:], sc[:], ACT.Exp, scale=MSCALE).then_inc(s["m_exp"], 1)
                hold(e, s["m_turned"], j + 1)
                e.activation(xnT.rearrange("p b n -> p (b n)"), psM0, ACT.Copy).then_inc(s["m_oT"], 1)
                hold(e, s["y_turned"], j + 1)
                e.activation(xnT.rearrange("p b n -> p (b n)"), psM0, ACT.Copy).then_inc(s["y_T"], 1)
                hold(e, s["g_d"], j + 1)
                e.activation(ge[:], gd[:], ACT.Exp).then_inc(s["g_exp"], 1)

            group(0)
            with e.Fori(1, NJ) as j:
                group(j)

            for n in range(2):
                e.wait_ge(s["w12_made"], n + 1)
                e.activation(w12[:, 4 * n:4 * n + 4].rearrange("p e n -> p (e n)"), psM[:, n], ACT.Copy).then_inc(s["w12_stored"], 1)

            def ln_passes(k, t, src, src_ready, n_sum, n_neg, n_sq, n_nm, n_out, dst, dst_free):
                def total():
                    src_ready()
                    e.activation(junk[:, k], src(), ACT.Identity, accum_out=lsum[:, k:k + 1]).then_inc(n_sum, 1)

                def square():
                    hold(e, n_neg, t + 1)
                    e.activation(junk[:, k], src(), ACT.Square, bias=lneg[:, k:k + 1], accum_out=lsq[:, k:k + 1]).then_inc(n_sq, 1)

                def norm():
                    hold(e, n_nm, t + 1)
                    dst_free()
                    e.activation(dst, src(), ACT.Identity, bias=lnm[:, k:k + 1], scale=lrs[:, k:k + 1]).then_inc(n_out, 1)
                return total, square, norm

            def front(t):
                def turn():
                    hold(e, s["c_turned"], t + 1)
                    hold(e, s["mb_made"], 4 * t)
                    e.activation(y1T[:], psM0[:, 0:P], ACT.Copy).then_inc(s["c_copied"], 1)
                    e.activation(gT[:], psM0[0:E, P:2 * P], ACT.Copy).then_inc(s["c_copied"], 1)

                def gated(n):
                    def f():
                        if n == 0:
                            hold(e, s["mty"], t)
                        hold(e, s["mb_made"], 4 * t + n + 2)
                        if n == 0:
                            e.activation(mparts[:, E], psM0[:, 0:D], ACT.Copy)
                        lo, hi, at = [(0, 3, D), (3, 7, 0), (7, 8, 0)][n]
                        for x_ in range(lo, hi):
                            ins = e.activation(mparts[:, x_], psM0[:, at + (x_ - lo) * D:at + (x_ - lo + 1) * D], ACT.Copy,
                                               scale=cur[:, D + x_:D + x_ + 1])
                        ins.then_inc(s["mb_out"], 1)
                    return f
                a1, a2, a3 = ln_passes(0, t, lambda: res2[:], lambda: hold(e, s["mty"], t + 1), s["n2_sum"], s["n2_neg"], s["n2_sq"],
                                       s["n2_nm"], s["n2_out"], yn, lambda: hold(e, s["x2_set"], t))
                c1, c2, c3 = ln_passes(1, t, lambda: x2[:, t % 4], lambda: hold(e, s["x2_set"], t + 1), s["n3_sum"], s["n3_neg"], s["n3_sq"],
                                       s["n3_nm"], s["n3_out"], z2, lambda: hold(e, s["z_turned"], t))

                def zT():
                    hold(e, s["z_turned"], t + 1)
                    hold(e, s["q1_made"], t)
                    e.activation(z2T, psM0[:, 0:P], ACT.Copy).then_inc(s["z_T"], 1)

                def qT():
                    hold(e, s["q1_made"], t + 1)
                    hold(e, s["S_ready"], t)
                    e.activation(q1T, psM0[:, P:2 * P], ACT.Copy).then_inc(s["q1_T"], 1)

                def keep():
                    hold(e, s["S_ready"], t + 1)
                    hold(e, s["S_read"], t)
                    e.activation(fresh.rearrange("p (g i) k -> p g (i k)", g=G), psS[:, :, 0:GW], ACT.Copy)\
                        .then_inc(s["S_fresh"], 1)
                    if not (isinstance(t, int) and t < 4):
                        hold(e, s["cut_set"], t - 3)
                    e.activation(skeep[:, t % 4].rearrange("p (g i) k -> p g (i k)", g=G), psS[:, :, 0:GW], ACT.Copy)\
                        .then_inc(s["S_kept"], 1)
                return dict(copy=turn, gated0=gated(0), gated1=gated(1), gated2=gated(2), sum2=a1, square2=a2, norm2=a3,
                            sum3=c1, square3=c2, norm3=c3, zT=zT, qT=qT, keep=keep)

            def weigh(t):
                def a():
                    hold(e, s["dif_set"], t + 1)
                    hold(e, s["p_set"], t)
                    e.activation(ex1, dif[:], ACT.Exp, scale=SCALE).then_inc(s["exp_set"], 1)

                def b():
                    hold(e, s["cut_set"], t + 1)
                    e.activation(cut, cut, ACT.Sign, bias=tiny[:]).then_inc(s["sign_set"], 1)
                    hold(e, s["sign_set"], t + 1)
                    e.activation(cut, cut, ACT.Relu).then_inc(s["keep_set"], 1)

                def c(g):
                    def f():
                        if g == 0:
                            hold(e, s["a_made"], t)
                        hold(e, s["p_turned"], 3 * t + g + 1)
                        if g < 2:
                            e.activation(pT1[:, 4 * g:4 * g + 4].rearrange("p c n -> p (c n)"), psT[:, 0], ACT.Copy)\
                                .then_inc(s["p_copied"], 1)
                        else:
                            e.activation(pT1[:, 8], psT[:, 0, 0:P], ACT.Copy)
                            e.activation(pT1[0:LAST, 9], psT[0:LAST, 0, P:2 * P], ACT.Copy).then_inc(s["p_copied"], 1)
                    return f
                return dict(exp=a, sign=b, copy0=c(0), copy1=c(1), copy2=c(2))

            def ffn(t):
                a1, a2, a3 = ln_passes(2, t, lambda: x3[:, t % 2], lambda: hold(e, s["x3_set"], t + 1), s["n4_sum"], s["n4_neg"], s["n4_sq"],
                                       s["n4_nm"], s["n4_out"], zf[:], lambda: hold(e, s["f_turned"], t))

                def shift():
                    hold(e, s["f_kr"], t)
                    e.activation(zfT[:, 0:1], zfT[:, P:P + 1], ACT.Copy, scale=C["notfirst"][:, t:t + 1] if isinstance(t, int) else C["notfirst"][:, bass.ds(t, 1)]).then_inc(s["f_prev"], 1)
                    hold(e, s["f_turned"], t + 1)
                    hold(e, s["f_prev"], t + 1)
                    e.activation(zfT[:, 1:P + 1], psT[:, 1, 0:P], ACT.Copy).then_inc(s["f_T"], 1)

                def acts():
                    hold(e, s["f_kr"], t + 1)
                    hold(e, s["f_v"], t)
                    e.activation(ka, psT[:, 1, P:2 * P], ACT.Relu).then_inc(s["f_relu"], 1)
                    hold(e, s["f_mul"], t)
                    e.activation(er, psT[:, 1, 2 * P:3 * P], ACT.Tanh, scale=0.5).then_inc(s["f_r"], 1)
                    hold(e, s["f_relu"], t + 1)
                    e.activation(ka, ka, ACT.Square).then_inc(s["f_sq"], 1)

                def value():
                    hold(e, s["f_v"], t + 1)
                    hold(e, s["f_fin"], t)
                    e.activation(vv, psT[:, 1, 3 * P:4 * P], ACT.Copy).then_inc(s["f_vv"], 1)
                return dict(sum4=a1, square4=a2, norm4=a3, shift=shift, acts=acts, fvalue=value)

            run_tiles(e, front, lambda t: {}, weigh, ffn)

        @block.vector
        def _(e):
            fills = fill_parts()
            e.wait_ge(s["mask_in"], 16)
            e.tensor_copy(mask_f[:], mask_u8[:]).then_inc(s["mask_cast"], 1)
            e.wait_ge(s["mask_cast"], 1)
            e.wait_ge(s["constants_set"], 5)
            for n, f in enumerate(fills):
                for i in range(HG):
                    e.tensor_scalar(mrow[32 * n:32 * n + 1, :, i, :], mask_f[32 * n:32 * n + 1], -f, f, ALU.mult, ALU.add)\
                        .then_inc(s["mrow_made"], 1)
            e.wait_ge(s["k0_copied"], 1)
            e.tensor_tensor(k0[:], k0[:], mask_f[:], ALU.mult).then_inc(s["k0_masked"], 1)
            e.wait_ge(s["k0_masked"], 1)
            e.wait_ge(s["consts_in"], 16)
            for b in range(B):
                e.tensor_tensor(kblk0[:, b], k0[:, b, None, :].broadcast_to([P, HG, KEYS]),
                                blk[:, :, None].broadcast_to([P, HG, KEYS]), ALU.mult).then_inc(s["kblk0_made"], 1)
            for n in range(2 * B * 3):
                v, b, g = (vblk0, vblk1)[n // (3 * B)], n // 3 % B, n % 3
                lo, hi = 4 * g, min(4 * g + 4, NCH)
                e.wait_ge(s["v_turned"], n + 1)
                e.tensor_tensor(v[:, b, lo:hi, 0:D], psT[:, n % 2, 0:(hi - lo) * P].rearrange("p (c n) -> p c n", n=P),
                                headmask[:, lo:hi, 0:D], ALU.mult).then_inc(s["v_masked"], 1)

            def statistics(src, n):
                for b in range(B):
                    e.bn_stats(stats[:, b], src(b)).then_inc(s["ln_stats"], 1)
                hold(e, s["ln_stats"], B * n + B, alone=True)
                for b in range(B):
                    e.bn_aggr(mv[:, b], stats[:, b]).then_inc(s["ln_mv"], 1)
                hold(e, s["ln_mv"], B * n + B)
                e.tensor_scalar(veps[:], mv[:, :, 1], EPS, None, ALU.add).then_inc(s["ln_veps"], 1)

            def normalise(dst, src, n, n_out):
                hold(e, s["ln_rstd"], n + 1)
                for b in range(B):
                    e.tensor_scalar(dst[:, b], src(b), mv[:, b, 0:1], rstd[:, b:b + 1], ALU.subtract, ALU.mult).then_inc(n_out, 1)

            e.wait_ge(s["x_in"], 32)
            e.wait_ge(s["xbo_made"], 1)
            def group(j):
                hold(e, s["y_n"], B * j)
                statistics(lambda b: xs[:, NJ * b + j], 3 * j)
                hold(e, s["h_turned"], j)
                normalise(xn, lambda b: xs[:, NJ * b + j], 3 * j, s["h_xn"])
                for b in range(B):
                    u = B * j + b
                    t = NJ * b + j
                    hold(e, s["s_made"], u + 1)
                    hold(e, s["s_sub"], u)
                    e.tensor_reduce(mx0.rearrange("p (g i) -> p g i", g=G), score_banks(None), AX, ALU.max).then_inc(s["s_max"], 1)
                    hold(e, s["s_max"], u + 1)
                    hold(e, s["s_exp"], u)
                    e.tensor_tensor(d0.rearrange("p (g i) k -> p g i k", g=G), score_banks(None),
                                    mx0.rearrange("p (g i) -> p g i", g=G)[:, :, :, None].broadcast_to([P, G, HG, KEYS]),
                                    ALU.subtract).then_inc(s["s_sub"], 1)
                    hold(e, s["t_turned"], 3 * u + 2)
                    hold(e, s["pv_made"], u)
                    e.tensor_copy(pT[:, 4:8].rearrange("p c n -> p (c n)"), psT[:, 1]).then_inc(s["t_copiedV"], 1)
                    hold(e, s["pv_made"], u + 1)
                    hold(e, s["pv_norm"], u)
                    e.reciprocal(rden[:], psM0[:, D:VW]).then_inc(s["pv_den"], 1)
                    hold(e, s["pv_den"], u + 1)
                    hold(e, s["o_turned"], u)
                    e.tensor_tensor(at0.rearrange("p (h d) -> p h d", h=H), psM0[:, 0:D].rearrange("p (h d) -> p h d", h=H),
                                    rden[:, :, None].broadcast_to([P, H, HD]), ALU.mult).then_inc(s["pv_norm"], 1)
                    hold(e, s["o_proj"], u + 1)
                    e.tensor_tensor(x1[:, t], psM0[:, 384:512], x1[:, t], ALU.add).then_inc(s["x1_made"], 1)
                hold(e, s["x1_made"], B * j + B)
                hold(e, s["h_xn"], B * j + B)
                statistics(lambda b: x1[:, NJ * b + j], 3 * j + 1)
                hold(e, s["zob_made"], j)
                hold(e, s["q_turned"], j)
                normalise(zt, lambda b: x1[:, NJ * b + j], 3 * j + 1, s["q_z"])
                for b in range(B):
                    hold(e, s["q_made"], B * j + b + 1)
                    if b == 0:
                        hold(e, s["m_pv"], B * j)
                    e.tensor_tensor(qkv[:, b], psM[:, 1 - b % 2, 0:3 * D], Rw["inb"], ALU.add).then_inc(s["q_stored"], 1)
                for l in range(B):
                    if l == 0:
                        hold(e, s["m_pv"], B * j)
                    hold(e, s["m_prod"], B * j + l + 1)
                    e.tensor_reduce(sc[:, l].rearrange("p m h -> p (m h)"), prod[:, l].rearrange("p (m d) -> p m d", d=MHD),
                                    AX, ALU.add).then_inc(s["m_sc"], 1)
                hold(e, s["m_sc"], B * j + B)
                e.tensor_reduce(scx[:], sc.rearrange("p l m h -> p l h m"), AX, ALU.max).then_inc(s["m_soft"], 1)
                hold(e, s["m_soft"], 3 * j + 1)
                e.tensor_tensor(sc[:], sc[:], scx[:, :, None, :].broadcast_to([P, B, B, MH]), ALU.subtract).then_inc(s["m_sub"], 1)
                hold(e, s["m_exp"], j + 1)
                e.tensor_reduce(scs[:], sce.rearrange("p l m h -> p l h m"), AX, ALU.add).then_inc(s["m_soft"], 1)
                hold(e, s["m_soft"], 3 * j + 2)
                e.reciprocal(scr[:], scs[:]).then_inc(s["m_soft"], 1)
                hold(e, s["m_soft"], 3 * j + 3)
                e.tensor_tensor(sc[:], sce[:], scr[:, :, None, :].broadcast_to([P, B, B, MH]), ALU.mult).then_inc(s["m_w"], 1)
                for l in range(B):
                    if l == 0:
                        hold(e, s["y_made"], j)
                    hold(e, s["m_pv"], B * j + l + 1)
                    e.tensor_reduce(oo[:, l], prod[:, l].rearrange("p (n m) -> p n m", m=B), AX, ALU.add).then_inc(s["m_o"], 1)
                hold(e, s["m_proj"], j + 1)
                hold(e, s["m_turned"], j + 1)
                hold(e, s["zob_made"], j + 1)
                e.tensor_tensor(oo[:], psM1.rearrange("p (b n) -> p b n", b=B), zob[:], ALU.add).then_inc(s["m_res"], 1)
                hold(e, s["m_res"], j + 1)
                hold(e, s["q_z"], B * j + B)
                statistics(lambda b: oo[:, b], 3 * j + 2)
                normalise(oo, lambda b: oo[:, b], 3 * j + 2, s["y_n"])
                lg = psM1[:, 0:B * E].rearrange("p (b e) -> p b e", b=B)
                hold(e, s["lg_made"], j + 1)
                e.tensor_reduce(gmx[:], lg, AX, ALU.max).then_inc(s["g_step"], 1)
                hold(e, s["g_step"], 8 * j + 1)
                e.tensor_tensor(gd[:], lg, gmx[:, :, None].broadcast_to([P, B, E]), ALU.subtract).then_inc(s["g_d"], 1)
                e.tensor_tensor(geq[:], lg, gmx[:, :, None].broadcast_to([P, B, E]), ALU.is_ge).then_inc(s["g_step"], 1)
                hold(e, s["g_step"], 8 * j + 2)
                e.tensor_tensor(gp[:], geq[:], C["prio"][:, None, :].broadcast_to([P, B, E]), ALU.mult).then_inc(s["g_step"], 1)
                hold(e, s["g_step"], 8 * j + 3)
                e.tensor_reduce(gpm[:], gp[:], AX, ALU.max).then_inc(s["g_step"], 1)
                hold(e, s["g_exp"], j + 1)
                e.tensor_reduce(gsum[:], ge[:], AX, ALU.add).then_inc(s["g_step"], 1)
                hold(e, s["g_step"], 8 * j + 5)
                e.reciprocal(gval[:], gsum[:]).then_inc(s["g_step"], 1)
                hold(e, s["g_step"], 8 * j + 4)
                ohj = oh.rearrange("p (b j) e -> p b j e", b=B)[:, :, j]
                e.tensor_tensor(ohj, gp[:], gpm[:, :, None].broadcast_to([P, B, E]), ALU.is_equal).then_inc(s["g_step"], 1)
                hold(e, s["g_step"], 8 * j + 7)
                hold(e, s["g_step"], 8 * j + 6)
                e.tensor_tensor(ohg.rearrange("p (b j) e -> p b j e", b=B)[:, :, j], ohj,
                                gval[:, :, None].broadcast_to([P, B, E]), ALU.mult).then_inc(s["g_step"], 1)

            group(0)
            with e.Fori(1, NJ) as j:
                group(j)

            e.memset(before[:, 0], 0.0).then_inc(s["seen"], 1)
            for t in range(1, NT):
                e.wait_ge(s["seen"], t)
                e.tensor_tensor(before[:, t], before[:, t - 1], oh[:, t - 1], ALU.add).then_inc(s["seen"], 1)
            e.wait_ge(s["pos_made"], 1)
            e.wait_ge(s["g_step"], 8 * NJ)
            e.wait_ge(s["y_stored"], NJ)
            e.scalar_tensor_tensor(yg[:, :, D:D + E], psM0[:, 0:NT * E].rearrange("p (t e) -> p t e", e=E), CAP - 0.5, ohg[:],
                                   ALU.is_lt, ALU.mult).then_inc(s["gates_set"], 1)
            e.wait_ge(s["constants_set"], 7)
            e.wait_ge(s["w2_in"], 48)
            e.tensor_copy(b1z[:, :, ::E + 1], b1T[:]).then_inc(s["b1_spread"], 1)
            e.tensor_scalar(omu[:], cols[:, 3:5], -1.0, 1.0, ALU.mult, ALU.add).then_inc(s["b1_spread"], 1)
            e.wait_ge(s["b1_spread"], 2)
            e.wait_ge(s["weights_in"], 32)
            for dst, w, c in ((wr_now, "wr", Cl["mur"]), (wr_prev, "wr", omu[:, 0:1]), (wk_now, "wk", Cl["muk"]), (wk_prev, "wk", omu[:, 1:2])):
                e.tensor_scalar(dst[:], Wt[w], c, None, ALU.mult).then_inc(s["b1_spread"], 1)
            e.wait_ge(s["b12_made"], 1)
            e.tensor_tensor(b12[:], psT[0:E, 0, 0:D], b2[:], ALU.add).then_inc(s["b12_stored"], 1)

            def topk(t):
                n = [0]

                def largest(r):
                    def f():
                        if r == 0:
                            hold(e, s["mx_copied"], 2 * t)
                            hold(e, s["S_fresh"], t + 1, alone=True)
                        for h in range(H):
                            if r and h % 4 == 0:
                                e.wait_ge(s["topk_step"], n[0] - 3 + h // 4)
                            ins = e.max(top[:, r, h], (left if r else fresh)[:, h])
                            if h % 4 == 3:
                                ins.then_inc(s["topk_step"], 1)
                        n[0] += 4
                    return f

                def mark(r):
                    def f():
                        for h in range(H):
                            if h % 4 == 0:
                                e.wait_ge(s["topk_step"], n[0] - 3 + h // 4)
                            ins = e.match_replace(left[:, h], top[:, r, h], (left if r else fresh)[:, h], GONE)
                            if h % 4 == 3:
                                ins.then_inc(s["topk_step"] if (r or h < H - 1) else s["topk_step"], 1)
                        n[0] += 4
                    return f

                def free_scores():
                    e.wait_ge(s["topk_step"], 8)
                    e.tensor_copy(mxc[:, 0], top[:, 0, :, 0]).then_inc(s["S_read"], 1)

                def ends():
                    e.wait_ge(s["topk_step"], n[0])
                    e.tensor_copy(mxc[:, 1], top[:, TOPK // 8 - 1, :, 7]).then_inc(s["mx_copied"], 1)
                    hold(e, s["S_read"], t + 1)
                    hold(e, s["mx_copied"], 2 * t + 1, alone=True)
                    e.sem_clear(s["topk_step"])
                    e.engine_nop().then_inc(s["mx_copied"], 1)

                out_ = {}
                for r in range(TOPK // 8):
                    out_[f"max{r}"] = largest(r)
                    if r < TOPK // 8 - 1:
                        out_[f"mark{r}"] = mark(r)
                    if r == 0:
                        out_["free"] = lambda: (hold(e, s["cut_set"], t), free_scores())
                out_["ends"] = ends
                return out_

            def weigh(t):
                def a():
                    hold(e, s["a_made"], t + 1)
                    e.reciprocal(rden1[:], psM1[:, D:VW]).then_inc(s["a_den"], 1)
                    hold(e, s["a_den"], t + 1)
                    hold(e, s["x3_set"], t)
                    e.tensor_tensor(att1.rearrange("p (h d) -> p h d", h=H), psM1[:, 0:D].rearrange("p (h d) -> p h d", h=H),
                                    rden1[:, :, None].broadcast_to([P, H, HD]), ALU.mult).then_inc(s["a_norm"], 1)
                return dict(norm=a)

            run_tiles(e, lambda t: {}, topk, weigh, lambda t: {})

        @block.tensor
        def _(e):
            mm, tr = e.matmul, e.transpose
            e.wait_ge(s["ctx_in"], 16)
            e.wait_ge(s["weights_in"], 32)
            keys = ctx_sb.rearrange("p b k -> p (b k)")
            mm(psM0[:, 0:B * KEYS], Wt["wk0"], keys, start=True, stop=True).then_inc(s["k0_made"], 1)
            mm(psM1[:, 0:B * KEYS], Wt["wk1"], keys, start=True, stop=True).then_inc(s["k1_made"], 1)
            e.wait_ge(s["constants_set"], 6)
            e.wait_ge(s["consts_in"], 16)
            for n in range(2 * B * 3):
                b, g = n // 3 % B, n % 3
                e.wait_ge(s["ctx_rep"], b + 1)
                if n >= 2:
                    e.wait_ge(s["v_masked"], n - 1)
                for c in range(4 * g, min(4 * g + 4, NCH)):
                    dst = psT[:, n % 2, (c % 4) * P:(c % 4 + 1) * P]
                    if n < 3 * B:
                        ins = mm(dst, ctxrep[:, b, c * P:(c + 1) * P], Wt["wv0"], start=True, stop=True)
                    else:
                        ins = tr(dst, ctxrep[:, b, c * P:(c + 1) * P], ident)
                ins.then_inc(s["v_turned"], 1)
            e.wait_ge(s["kblk0_made"], B)
            e.wait_ge(s["mrow_made"], 3 * HG)
            e.wait_ge(s["constants_set"], 4)
            e.wait_ge(s["k0_copied"], 1)
            e.wait_ge(s["k1_copied"], 1)
            e.wait_ge(s["v_masked"], 2 * B * 3)
            e.wait_ge(s["den_cols"], 2 * B)

            def turn4(src, ready, value, done, j):
                hold(e, ready, value)
                for b in range(B):
                    ins = tr(psM0[:, b * P:(b + 1) * P], src[:, b], ident)
                ins.then_inc(done, 1)

            def group(j):
                hold(e, s["y_T"], j)
                turn4(xn, s["h_xn"], B * j + B, s["h_turned"], j)
                hold(e, s["h_xnT"], j + 1)
                hold(e, s["g_step"], 8 * j)
                mm(psM1, Wt["wq0"], xnT.rearrange("p b n -> p (b n)"), start=True, stop=True).then_inc(s["h_q"], 1)
                hold(e, s["h_qT"], j + 1)

                def scores(b):
                    hold(e, s["s_sub"], B * j + b)
                    for g in range(G):
                        mm(psS[:, g, 0:GW], q0T[32 * g:32 * g + 32, b], kblk0[32 * g:32 * g + 32, b].rearrange("p i k -> p (i k)"),
                           start=True, stop=False)
                    for g in range(G):
                        ins = mm(psS[:, g, 0:GW], mones[:], mrow[:, b].rearrange("p i k -> p (i k)"), start=False, stop=True)
                    ins.then_inc(s["s_made"], 1)

                def attend(b):
                    u = B * j + b
                    hold(e, s["s_exp"], u + 1)
                    for g in range(3):
                        if g == 0:
                            hold(e, s["t_copiedA"], 3 * u)
                        elif g == 1:
                            hold(e, s["t_copiedV"], u)
                        else:
                            hold(e, s["t_copiedA"], 3 * u + 1)
                        for c in range(4 * g, min(4 * g + 4, NCH)):
                            w = P if c < NCH - 1 else LAST
                            ins = tr(psT[0:w, g % 2, (c % 4) * P:(c % 4 + 1) * P], e0[:, c * P:c * P + w], ident)
                        ins.then_inc(s["t_turned"], 1)
                    hold(e, s["t_copiedA"], 3 * u + 3)
                    hold(e, s["t_copiedV"], u + 1)
                    hold(e, s["x1_made"], u)
                    for c in range(NCH):
                        w = P if c < NCH - 1 else LAST
                        ins = mm(psM0[:, 0:VW], pT[0:w, c], vblk0[0:w, b, c], start=(c == 0), stop=(c == NCH - 1))
                    ins.then_inc(s["pv_made"], 1)
                    hold(e, s["pv_norm"], u + 1)
                    tr(psM0[:, 256:384], at0[:], ident).then_inc(s["o_turned"], 1)
                    hold(e, s["o_T"], u + 1)
                    mm(psM0[:, 384:512], at0T[:], Wt["wo0"], start=True, stop=True).then_inc(s["o_proj"], 1)

                scores(0)
                for b in range(B):
                    if b + 1 < B:
                        scores(b + 1)
                    attend(b)
                hold(e, s["x1_made"], B * j + B)
                turn4(zt, s["q_z"], B * j + B, s["q_turned"], j)
                hold(e, s["q_zT"], j + 1)
                for b in range(B):
                    if b >= 2:
                        hold(e, s["q_stored"], B * j + b - 1)
                    mm(psM[:, 1 - b % 2, 0:3 * D], xnT[:, b], Wt["inw"], start=True, stop=True).then_inc(s["q_made"], 1)
                hold(e, s["q_stored"], B * j + B)
                turn4(oo, s["m_o"], B * j + B, s["m_turned"], j)
                hold(e, s["m_oT"], j + 1)
                for b in range(B):
                    ins = mm(psM1[:, b * P:(b + 1) * P], xnT[:, b], Wt["outw"], start=True, stop=True)
                ins.then_inc(s["m_proj"], 1)
                turn4(y1s, s["y_made"], j + 1, s["y_turned"], j)
                hold(e, s["y_T"], j + 1)
                hold(e, s["m_res"], j + 1)
                for b in range(B):
                    ins = mm(psM1[:, b * E:(b + 1) * E], xnT[:, b], Wt["wg"], start=True, stop=True)
                ins.then_inc(s["lg_made"], 1)

            group(0)
            with e.Fori(1, NJ) as j:
                group(j)

            e.wait_ge(s["g_step"], 8 * NJ)
            mm(psM0[:, 0:NT * E], tri, oh.rearrange("p t e -> p (t e)"), start=True, stop=False)
            e.wait_ge(s["seen"], NT)
            mm(psM0[:, 0:NT * E], ones[:], before.rearrange("p t e -> p (t e)"), start=False, stop=True).then_inc(s["pos_made"], 1)
            e.wait_ge(s["w1_in"], 16)
            e.wait_ge(s["w2_in"], 48)
            e.wait_ge(s["gates_set"], 1)
            e.wait_ge(s["g_step"], 8 * NJ)
            for x_ in range(E):
                for c in range(FC):
                    ins = mm(psM[:, x_ // 4, (x_ % 4) * D:(x_ % 4 + 1) * D], w1T[:, c, x_], w2[:, c, x_], start=(c == 0), stop=(c == FC - 1))
                if x_ % 4 == 3:
                    ins.then_inc(s["w12_made"], 1)
            e.wait_ge(s["b1_spread"], 1)
            for x_ in range(E):
                for c in range(FC):
                    ins = mm(psT[0:E, 0, 0:D], b1z[:, c, x_ * E:(x_ + 1) * E], w2[:, c, x_],
                             start=(x_ == 0 and c == 0), stop=(x_ == E - 1 and c == FC - 1))
            ins.then_inc(s["b12_made"], 1)
            e.wait_ge(s["w12_stored"], 2)
            e.wait_ge(s["b12_stored"], 1)
            e.wait_ge(s["b1_spread"], 6)
            e.wait_ge(s["kblk1_made"], B)

            def front(t):
                def turn():
                    hold(e, s["cur_set"], t + 1)
                    hold(e, s["q1_T"], t)
                    tr(psM0[:, 0:P], cur[:, 0:D], ident)
                    tr(psM0[0:E, P:2 * P], cur[:, D:D + E], ident).then_inc(s["c_turned"], 1)

                def moe(n):
                    def f():
                        if n == 0:
                            hold(e, s["c_copied"], 2 * t + 2)
                            mm(psM0[:, 0:D], gT[:], b12[:], start=True, stop=True).then_inc(s["mb_made"], 1)
                            mm(psM0[:, D:4 * D], y1T[:], w12[:, 0:3].rearrange("p e n -> p (e n)"), start=True, stop=True)\
                                .then_inc(s["mb_made"], 1)
                        else:
                            hold(e, s["mb_out"], 3 * t + n)
                            lo, hi = ((3, 7), (7, 8))[n - 1]
                            mm(psM0[:, 0:(hi - lo) * D], y1T[:], w12[:, lo:hi].rearrange("p e n -> p (e n)"), start=True, stop=True)\
                                .then_inc(s["mb_made"], 1)
                    return f

                def zturn():
                    hold(e, s["n3_out"], t + 1)
                    tr(psM0[:, 0:P], z2, ident).then_inc(s["z_turned"], 1)

                def query():
                    hold(e, s["z_T"], t + 1)
                    mm(psM0[:, P:2 * P], Wt["wq1"], z2T, start=True, stop=True).then_inc(s["q1_made"], 1)

                def scores():
                    hold(e, s["q1_T"], t + 1)
                    hold(e, s["kcur_set"], t + 1)
                    hold(e, s["S_kept"], t)
                    for g in range(G):
                        ins = mm(psS[:, g, 0:GW], q1T[32 * g:32 * g + 32, :],
                                 kcur[32 * g:32 * g + 32], start=True, stop=True)
                    ins.then_inc(s["S_ready"], 1)
                return dict(turn=turn, moe0=moe(0), moe1=moe(1), moe2=moe(2), zturn=zturn, query=query, scores=scores)

            def weigh(t):
                def turn(g):
                    def f():
                        if g == 0:
                            hold(e, s["p_set"], t + 1)
                        hold(e, s["p_copied"], 3 * t + g)
                        for c in range(4 * g, min(4 * g + 4, NCH)):
                            w = P if c < NCH - 1 else LAST
                            ins = tr(psT[0:w, 0, (c % 4) * P:(c % 4 + 1) * P], p1[:, c * P:c * P + w], ident)
                        ins.then_inc(s["p_turned"], 1)
                    return f

                def value():
                    hold(e, s["p_copied"], 3 * t + 3)
                    hold(e, s["a_norm"], t)
                    for c in range(NCH):
                        w = P if c < NCH - 1 else LAST
                        ins = mm(psM1[:, 0:VW], pT1[0:w, c], vblk1[0:w, t // NJ, c], start=(c == 0), stop=(c == NCH - 1),
                                 skip_group_check=True)
                    ins.then_inc(s["a_made"], 1)
                return dict(turn0=turn(0), turn1=turn(1), turn2=turn(2), value=value)

            def ffn(t):
                def turn():
                    hold(e, s["n4_out"], t + 1)
                    hold(e, s["f_sq"], t)
                    hold(e, s["f_vv"], t)
                    tr(psT[:, 1, 0:P], zf[:], ident).then_inc(s["f_turned"], 1)

                def up():
                    hold(e, s["f_T"], t + 1)
                    now, prev = zfT[:, 1:P + 1], zfT[:, 0:P]
                    mm(psT[:, 1, P:2 * P], wk_now[:], now, start=True, stop=False, skip_group_check=True)
                    mm(psT[:, 1, P:2 * P], wk_prev[:], prev, start=False, stop=True, skip_group_check=True)
                    mm(psT[:, 1, 2 * P:3 * P], now, wr_now[:], start=True, stop=False, skip_group_check=True)
                    mm(psT[:, 1, 2 * P:3 * P], prev, wr_prev[:], start=False, stop=True, skip_group_check=True).then_inc(s["f_kr"], 1)

                def down():
                    hold(e, s["f_sq"], t + 1)
                    mm(psT[:, 1, 3 * P:4 * P], ka, Wt["wv"], start=True, stop=True, skip_group_check=True).then_inc(s["f_v"], 1)
                return dict(fturn=turn, up=up, down=down)

            run_tiles(e, front, lambda t: {}, weigh, ffn)


TURN = dict(
    front="load turn copy moe0 gated0 moe1 gated1 moe2 gated2 tree sum2 neg2 square2 scale2 norm2 affine "
          "sum3 neg3 square3 scale3 norm3 zturn zT query qT scores keep",
    topk="max0 mark0 free max1 mark1 max2 mark2 max3 ends",
    weigh="dif cut exp sign product turn0 copy0 turn1 copy1 turn2 copy2 value norm x3",
    mix="sum4 neg4 square4 scale4 norm4 fturn shift up acts half down fvalue end",
)
ORDER = """load dif max0 turn copy sum4 neg4 square4 scale4 cut exp moe0 gated0 norm4 fturn shift mark0 free moe1 gated1
sign up acts half moe2 gated2 max1 down tree product mark1 sum2 neg2 square2 scale2 fvalue end turn0 copy0 turn1
copy1 norm2 affine turn2 copy2 value max2 sum3 neg3 square3 scale3 norm mark2 norm3 x3 zturn zT query qT scores
keep max3 ends""".split()
assert sorted(ORDER) == sorted(" ".join(TURN.values()).split())
assert all([x for x in ORDER if x in c.split()] == c.split() for c in TURN.values())


def run_tiles(e, front, topk, weigh, mix):
    def turn(*stages):
        steps = {}
        for stage in stages:
            steps.update(stage)
        for name in ORDER:
            if name in steps:
                steps[name]()

    turn(front(0))
    for i in range(4):
        turn(front(i + 1), topk(i), weigh(i - 1) if i >= 1 else {}, mix(i - 2) if i >= 2 else {})
    with e.Fori(4, NT - 1) as i:
        turn(front(i + 1), topk(i), weigh(i - 1), mix(i - 2))
    turn(topk(NT - 1), weigh(NT - 2), mix(NT - 3))
    turn(weigh(NT - 1), mix(NT - 2))
    turn(mix(NT - 1))


def kernel(**inputs):
    import numpy as np
    import concourse.bacc as bacc
    from concourse.bass_utils import run_bass_kernel_spmd as run

    a = {k: np.asarray(v) for k, v in inputs.items()}
    f32 = np.float32
    head = np.arange(NCH * P) // KEYS
    cols_of = np.arange(VW)
    own = np.where(cols_of < D, cols_of // HD, cols_of - D)
    headmask = (head[:, None] == own[None, :]).astype(f32).reshape(NCH, P, VW).transpose(1, 0, 2).reshape(P, -1)
    consts = np.concatenate([
        np.eye(P, dtype=f32),
        np.triu(np.ones((P, P), f32), 1),
        (np.arange(P)[:, None] % 32 // HD == np.arange(HG)[None, :]).astype(f32),
        np.broadcast_to(np.arange(E, 0, -1, dtype=f32), (P, E)),
        np.broadcast_to((np.arange(NT) % NJ != 0).astype(f32), (P, NT)),
        headmask,
    ], axis=1)
    weights = np.concatenate([
        a["L0_xattn_Wk"].T, a["L0_xattn_Wv"].T, a["L0_xattn_Wq"].T, a["L0_xattn_Wo"].T, a["L0_ffn_in_proj_w"].T,
        a["L0_ffn_out_proj_w"].T, a["L1_xattn_Wq"].T, a["L1_xattn_Wk"].T, a["L1_ffn_W_r"].T, a["L1_ffn_W_k"].T,
        a["L1_ffn_W_v"].T, a["L0_ffn_wg"],
    ], axis=1)
    cols = np.stack([a["L0_xattn_bq"], a["L0_xattn_bk"], a["L0_xattn_bv"], a["L1_ffn_mu_r"], a["L1_ffn_mu_k"]], axis=1)
    rows = np.concatenate([a["L0_xattn_bo"], a["L0_ffn_in_proj_b"], a["L0_ffn_out_proj_b"], a["L0_ffn_ln1_g"],
                           a["L0_ffn_ln1_b"], a["L0_ffn_ln2_g"], a["L0_ffn_ln2_b"]])[None, :]
    arrays = dict(
        x=a["x"].reshape(NT, P, D).transpose(1, 0, 2),
        ctxT=a["ctx_1024"].transpose(2, 0, 1),
        mask=a["mask_BxS2_bf1"].view(np.uint8).reshape(1, B * KEYS),
        consts=consts, weights=weights, cols=cols, rows=rows,
        b1T=a["L0_ffn_b1"].reshape(E, FC, P).transpose(2, 1, 0),
        b2=a["L0_ffn_b2"],
        w1T=a["L0_ffn_w1"].reshape(E, D, FC, P).transpose(3, 2, 0, 1),
        w2=a["L0_ffn_w2"].reshape(E, FC, P, D).transpose(2, 1, 0, 3),
    )
    nc = bacc.Bacc("TRN2", target_bir_lowering=False, num_devices=1)
    feed, args = {}, []
    for name, v in arrays.items():
        v = np.ascontiguousarray(v)
        feed[f"in_{name}"] = v
        args.append(nc.dram_tensor(f"in_{name}", v.shape, mybir.dt.from_np(v.dtype), kind="ExternalInput").ap())
    out = nc.dram_tensor("out", (NT, P, D), F32, kind="ExternalOutput").ap()
    build(nc, *args, out)
    r = run(nc, [feed], core_ids=[0])
    return r.results[0]["out"].reshape(B, SEQ, D)
```

```python
from contextlib import ExitStack

import concourse.bass as bass
from concourse import mybir

P = 128
B, SEQ, D = 4, 512, 128
NJ = SEQ // P
NT = B * NJ
KEYS = 77
H, HD = 16, 8
G = 4
HG = H // G
GW = HG * KEYS
SW = H * KEYS
NCH = -(-SW // P)
LAST = SW - (NCH - 1) * P
VW = D + H
TOPK = 32
MH, MHD = 4, 32
E, FF = 8, 512
FC = FF // P
CAP = B * SEQ // E
EPS = 1e-5
MASK_FILL = -1e8
SCALE = float(HD) ** -0.5
MSCALE = float(MHD) ** -0.5
GONE = -3.0e38
TINY = 1e-30

F32 = mybir.dt.float32
BF16 = mybir.dt.bfloat16
U8 = mybir.dt.uint8
ALU = mybir.AluOpType
ACT = mybir.ActivationFunctionType
AX = mybir.AxisListType.X

CONSTS = dict(ident=P, tri=P, blk=HG, prio=E, notfirst=NT, headmask=NCH * VW)
WEIGHTS = dict(wk0=D, wv0=D, wq0=D, wo0=D, inw=3 * D, outw=D, wq1=D, wk1=D, wr=D, wk=D, wv=D, wg=E)
COLS = dict(bq=1, bk=1, bv=1, mur=1, muk=1)
ROWS = dict(bo=D, inb=3 * D, ob=D, g1=D, b1=D, g2=D, b2=D)


def parts(ap, widths):
    at, out = 0, {}
    for name, width in widths.items():
        out[name] = ap[:, at:at + width]
        at += width
    return out


def fill_parts():
    import numpy as np
    rest = np.float32(MASK_FILL / SCALE)
    out = []
    for _ in range(3):
        top = (rest.view(np.uint32) & np.uint32(0xFFFF0000)).view(np.float32)
        out.append(float(top))
        rest = np.float32(rest - top)
    return out


def build(nc, x, ctxT, mask, consts_d, weights_d, cols_d, rows_d, b1T_d, b2_d, w1T_d, w2_d, out):
    with ExitStack() as stack:
        def sb(name, shape, dt=F32):
            return stack.enter_context(nc.sbuf_tensor(name, shape, dt))

        def pb(name, shape, dt=F32):
            return stack.enter_context(nc.psum_tensor(name, shape, dt))

        def sem(name):
            return stack.enter_context(nc.semaphore(name))

        consts = sb("consts", [P, sum(CONSTS.values())])
        C = parts(consts, CONSTS)
        weights = sb("weights", [P, sum(WEIGHTS.values())])
        Wt = parts(weights, WEIGHTS)
        cols = sb("cols", [P, len(COLS)])
        Cl = parts(cols, COLS)
        rows = sb("rows", [P, sum(ROWS.values())])
        Rw = parts(rows, ROWS)
        ident, tri, blk = C["ident"], C["tri"], C["blk"]
        headmask = C["headmask"].rearrange("p (c n) -> p c n", n=VW)
        ones = sb("ones", [P, P])
        expo = sb("expo", [P, HG])
        tiny = sb("tiny", [P, 1])

        xs = sb("xs", [P, NT, D])
        x1 = sb("x1", [P, NT, D])
        yg = sb("yg", [P, NT, D + E])
        x2 = sb("x2", [P, 4, D])

        ctx_sb = sb("ctx_sb", [P, B, KEYS])
        area_a = sb("area_a", [P, 4 * SW])
        area_b = sb("area_b", [P, B * NCH * P])
        ctxrep = area_b.rearrange("p (b n) -> p b n", b=B)
        mask_u8 = sb("mask_u8", [P, B, KEYS], U8)
        mask_f = sb("mask_f", [P, B, KEYS])
        mrow = sb("mrow", [65, B, HG, KEYS], BF16)
        mones = sb("mones", [65, P], BF16)
        k0 = sb("k0", [P, B, KEYS])
        k1 = sb("k1", [P, B, KEYS])
        kblk0 = sb("kblk0", [P, B, HG, KEYS])
        kblk1 = sb("kblk1", [P, B, HG, KEYS])
        vblk0 = sb("vblk0", [P, B, NCH, VW])
        vblk1 = sb("vblk1", [P, B, NCH, VW])

        stats = sb("stats", [P, NJ, 6])
        mv = sb("mv", [P, NJ, 2])
        veps = sb("veps", [P, NJ])
        rstd = sb("rstd", [P, NJ])
        xn = sb("xn", [P, B, D])
        xnT = sb("xnT", [P, B, P])
        q0T = sb("q0T", [P, B, P])
        mx0 = sb("mx0", [P, H])
        d0 = sb("d0", [P, H, KEYS])
        e0 = sb("e0", [P, SW])
        pT = sb("pT", [P, NCH, P])
        rden = sb("rden", [P, H])
        at0 = sb("at0", [P, D])
        at0T = sb("at0T", [P, P])
        zt = sb("zt", [P, B, D])
        zob = sb("zob", [P, B, D])
        qkv = sb("qkv", [P, B, 3 * D])
        prod = sb("prod", [P, B, 4 * D])
        sc = sb("sc", [P, B, B, MH])
        scx = sb("scx", [P, B, MH])
        sce = sb("sce", [P, B, B, MH])
        scs = sb("scs", [P, B, MH])
        scr = sb("scr", [P, B, MH])
        oo = sb("oo", [P, B, D])
        y1s = sb("y1s", [P, B, D])
        gmx = sb("gmx", [P, B])
        gd = sb("gd", [P, B, E])
        geq = sb("geq", [P, B, E])
        ge = sb("ge", [P, B, E])
        gsum = sb("gsum", [P, B])
        gval = sb("gval", [P, B])
        gp = sb("gp", [P, B, E])
        gpm = sb("gpm", [P, B])
        oh = sb("oh", [P, NT, E])
        ohg = sb("ohg", [P, NT, E])
        before = sb("before", [P, NT, E])

        w1T = area_a[:, 0:FC * E * D].rearrange("p (c e n) -> p c e n", c=FC, e=E)
        w2 = area_b[:, 0:FC * E * D].rearrange("p (c e n) -> p c e n", c=FC, e=E)
        b1T = sb("b1T", [P, FC, E])
        b1z = sb("b1z", [P, FC, E * E])
        b2 = sb("b2", [E, D])
        w12 = qkv.rearrange("p b n -> p (b n)")[:, 0:E * D].rearrange("p (e n) -> p e n", e=E)
        b12 = sb("b12", [E, D])
        omu = sb("omu", [P, 2])
        wr_now = sb("wr_now", [P, D])
        wr_prev = sb("wr_prev", [P, D])
        wk_now = sb("wk_now", [P, D])
        wk_prev = sb("wk_prev", [P, D])

        cur = sb("cur", [P, D + E])
        kcur = sb("kcur", [P, GW])
        y1T = sb("y1T", [P, P])
        gT = sb("gT", [E, P])
        mparts = prod.rearrange("p b n -> p (b n)")[:, 0:(E + 1) * D].rearrange("p (e n) -> p e n", n=D)
        junk = sb("junk", [P, 3, D])
        lsum = sb("lsum", [P, 3])
        lneg = sb("lneg", [P, 3])
        lsq = sb("lsq", [P, 3])
        lvar = sb("lvar", [P, 3])
        lrs = sb("lrs", [P, 3])
        lnm = sb("lnm", [P, 3])
        yn = zob[:, 0]
        z2 = zob[:, 1]
        z2T = zob[:, 2]
        q1T = zob[:, 3]
        scores_sb = [area_a[:, n * SW:(n + 1) * SW].rearrange("p (h k) -> p h k", h=H) for n in range(2)]
        left = area_b[:, 0 * SW:1 * SW].rearrange("p (h k) -> p h k", h=H)
        top = sb("top", [P, TOPK // 8, H, 8])
        mxc = sb("mxc", [P, 2, H])
        dif = d0
        cut = area_b[:, 1 * SW:2 * SW].rearrange("p (h k) -> p h k", h=H)
        ex1 = area_b[:, 2 * SW:3 * SW].rearrange("p (h k) -> p h k", h=H)
        p1 = e0
        pT1 = pT
        rden1 = sb("rden1", [P, H])
        att1 = sb("att1", [P, D])
        x3 = sb("x3", [P, 2, D])
        zf = sb("zf", [P, D])
        zfT = sb("zfT", [P, P + 1])
        ka = y1s[:, 0]
        er = y1s[:, 1]
        vv = y1s[:, 2]
        fin = sb("fin", [P, D])

        psS = pb("psS", [P, G, 512])
        psT = pb("psT", [P, 2, 512])
        psM = pb("psM", [P, 2, 512])
        psM0, psM1 = psM[:, 0], psM[:, 1]

        def score_banks(ap):
            return psS[:, :, 0:GW].rearrange("p g (i k) -> p g i k", k=KEYS) if ap is None else ap

        names = """x_in ctx_in mask_in consts_in weights_in w1_in w2_in k0_made k1_made k0_copied k1_copied mask_cast
        mrow_made k0_masked kblk0_made kblk1_made ctx_rep v_turned v_masked den_cols xbo_made h_xn h_turned
        h_xnT h_q h_qT s_made s_max s_sub s_exp t_turned t_copiedA t_copiedV pv_made pv_den pv_norm o_turned
        o_T o_proj x1_made q_z q_turned q_zT q_made q_stored zob_made m_prod m_sc m_sub m_exp m_w m_pv m_o
        m_turned m_oT m_proj m_res y_n y_g y_made y_stored y_turned y_T lg_made g_d g_exp seen pos_made
        gates_set w12_made w12_stored b1_spread b12_made b12_stored cur_set kcur_set c_turned c_copied
        mb_made mb_out mty n2_neg n2_sq n2_step n2_nm n2_out x2_set n3_neg n3_sq n3_step n3_nm n3_out
        z_turned z_T q1_made q1_T S_ready S_kept S_read topk_step mx_copied dif_set cut_set exp_set sign_set
        keep_set p_set p_turned p_copied a_made a_den a_norm x3_set n4_neg n4_sq n4_step n4_nm n4_out
        f_turned f_prev f_T f_kr f_relu f_sq f_r f_v f_vv f_one passed f_mul f_fin stored constants_set
        ln_stats ln_mv ln_veps ln_rstd m_soft g_step y2_step x1_biased""".split()
        s = {n: sem(n) for n in names}

        def hold(e, semaphore, value, alone=False):
            if isinstance(value, int):
                if value > 0:
                    e.wait_ge(semaphore, value)
                return
            if not alone:
                e.wait_ge(s["constants_set"], 1)
            e.wait_ge(semaphore, value)
            if alone:
                e.sem_inc(s["passed"], 1)

        block = stack.enter_context(nc.Block())

        @block.sync
        def _(e):
            e.dma_start(ctx_sb[:], ctxT).then_inc(s["ctx_in"], 16)
            e.dma_start(weights[:], weights_d).then_inc(s["weights_in"], 16)
            e.dma_start(cols[:], cols_d).then_inc(s["weights_in"], 16)
            e.dma_start(mask_u8[:], mask.broadcast_to([P, B * KEYS]).rearrange("p (b k) -> p b k", b=B)).then_inc(s["mask_in"], 16)
            e.dma_start(xs[:], x).then_inc(s["x_in"], 16)
            e.dma_start(rows[:], rows_d.broadcast_to([P, sum(ROWS.values())])).then_inc(s["x_in"], 16)
            e.dma_start(b1T[:], b1T_d).then_inc(s["w2_in"], 16)
            e.dma_start(b2[:], b2_d).then_inc(s["w2_in"], 16)
            e.dma_start(w1T, w1T_d).then_inc(s["w1_in"], 16)
            e.wait_ge(s["v_turned"], 2 * B * 3)
            e.dma_start(w2, w2_d).then_inc(s["w2_in"], 16)
            with e.Fori(0, NT) as t:
                hold(e, s["f_fin"], t + 1)
                e.dma_start(out[t], fin[:]).then_inc(s["stored"], 16)
            e.wait_ge(s["stored"], 16 * NT)

        @block.gpsimd
        def _(e):
            e.memset(ones[:], 1.0).then_inc(s["constants_set"], 1)
            e.memset(expo[:], -0.5).then_inc(s["constants_set"], 1)
            e.memset(tiny[:], TINY).then_inc(s["constants_set"], 1)
            e.memset(mones[:], 1.0).then_inc(s["constants_set"], 1)
            e.memset(mrow[:], 0.0).then_inc(s["constants_set"], 1)
            e.memset(ctxrep[:, :, SW:], 0.0).then_inc(s["constants_set"], 1)
            e.memset(b1z[:], 0.0).then_inc(s["constants_set"], 1)
            e.memset(zfT[:], 0.0).then_inc(s["constants_set"], 1)
            e.wait_ge(s["consts_in"], 16)
            for v in (vblk0, vblk1):
                for b in range(B):
                    e.tensor_copy(v[:, b, :, D:VW], headmask[:, :, D:VW]).then_inc(s["den_cols"], 1)
            e.wait_ge(s["k1_copied"], 1)
            for b in range(B):
                e.tensor_tensor(kblk1[:, b], k1[:, b, None, :].broadcast_to([P, HG, KEYS]),
                                blk[:, :, None].broadcast_to([P, HG, KEYS]), ALU.mult).then_inc(s["kblk1_made"], 1)
            e.wait_ge(s["x_in"], 32)
            e.tensor_tensor(x1[:], xs[:], Rw["bo"][:, None, :].broadcast_to([P, NT, D]), ALU.add).then_inc(s["xbo_made"], 1)

            def rstd_of(n):
                hold(e, s["ln_veps"], n + 1)
                e.tensor_tensor(rstd[:], veps[:], expo[:], ALU.pow).then_inc(s["ln_rstd"], 1)

            e.wait_ge(s["constants_set"], 2)
            def group(j):
                rstd_of(3 * j)
                rstd_of(3 * j + 1)
                hold(e, s["q_z"], B * j + B)
                hold(e, s["m_res"], j)
                e.tensor_tensor(zob[:], zt[:], Rw["ob"][:, None, :].broadcast_to([P, B, D]), ALU.add).then_inc(s["zob_made"], 1)
                hold(e, s["q_z"], B * j + B, alone=True)
                for b in range(B):
                    e.tensor_tensor(x1[:, NJ * b + j], x1[:, NJ * b + j], Rw["b2"], ALU.add).then_inc(s["x1_biased"], 1)
                hold(e, s["q_stored"], B * j + B)
                for l in range(B):
                    hold(e, s["m_o"], B * j)
                    e.tensor_tensor(prod[:, l].rearrange("p (m n) -> p m n", m=B),
                                    qkv[:, l, None, 0:D].broadcast_to([P, B, D]),
                                    qkv[:, :, D:2 * D], ALU.mult).then_inc(s["m_prod"], 1)
                hold(e, s["m_w"], j + 1)
                for l in range(B):
                    hold(e, s["m_sc"], B * j + l + 1)
                    e.tensor_tensor(prod[:, l].rearrange("p (h d m) -> p h d m", h=MH, m=B),
                                    qkv[:, :, 2 * D:3 * D].rearrange("p m (h d) -> p h d m", h=MH),
                                    sc[:, l].rearrange("p m h -> p h m")[:, :, None, :].broadcast_to([P, MH, MHD, B]),
                                    ALU.mult).then_inc(s["m_pv"], 1)
                rstd_of(3 * j + 2)
                hold(e, s["y_n"], B * j + B)
                hold(e, s["y_turned"], j)
                hold(e, s["y_stored"], j)
                e.tensor_tensor(y1s[:], oo[:], Rw["g1"][:, None, :].broadcast_to([P, B, D]), ALU.mult).then_inc(s["y_g"], 1)
                hold(e, s["y_g"], j + 1)
                e.tensor_tensor(y1s[:], y1s[:], Rw["b1"][:, None, :].broadcast_to([P, B, D]), ALU.add).then_inc(s["y_made"], 1)
                hold(e, s["y_made"], j + 1)
                e.tensor_copy(yg.rearrange("p (b j) n -> p b j n", b=B)[:, :, j, 0:D], y1s[:]).then_inc(s["y_stored"], 1)

            group(0)
            with e.Fori(1, NJ) as j:
                group(j)

            def ln_scalars(k, t, n_sq, n_step, n_nm):
                def scale():
                    hold(e, n_sq, t + 1, alone=True)
                    e.tensor_scalar(lvar[:, k:k + 1], lsq[:, k:k + 1], 1.0 / D, EPS, ALU.mult, ALU.add).then_inc(n_step, 1)
                    hold(e, n_step, 2 * t + 1)
                    e.tensor_tensor(lrs[:, k:k + 1], lvar[:, k:k + 1], expo[:, 0:1], ALU.pow).then_inc(n_step, 1)
                    hold(e, n_step, 2 * t + 2)
                    e.tensor_tensor(lnm[:, k:k + 1], lneg[:, k:k + 1], lrs[:, k:k + 1], ALU.mult).then_inc(n_nm, 1)
                return scale

            def experts(t, par):
                def load():
                    if isinstance(t, int) and t == 0:
                        e.wait_ge(s["gates_set"], 1)
                    hold(e, s["mty"], t)
                    e.tensor_copy(cur[:], yg[:, t, :]).then_inc(s["cur_set"], 1)

                def affine():
                    hold(e, s["n2_out"], t + 1)
                    e.tensor_tensor(yn, yn, Rw["g2"], ALU.mult).then_inc(s["y2_step"], 1)
                    if isinstance(t, int) and t == 0:
                        e.wait_ge(s["x1_biased"], NT)
                    hold(e, s["y2_step"], t + 1, alone=True)
                    e.tensor_tensor(x2[:, t % 4], yn, x1[:, t], ALU.add).then_inc(s["x2_set"], 1)
                return dict(load=load, scale2=ln_scalars(0, t, s["n2_sq"], s["n2_step"], s["n2_nm"]), affine=affine)

            def query(t, par):
                def keys():
                    hold(e, s["S_ready"], t)
                    e.tensor_copy(kcur[:], kblk1.rearrange("p b i k -> p b (i k)")[:, t // NJ]).then_inc(s["kcur_set"], 1)
                return dict(keys=keys, scale3=ln_scalars(1, t, s["n3_sq"], s["n3_step"], s["n3_nm"]))

            def weigh(t, par):
                def a():
                    hold(e, s["mx_copied"], 2 * t + 2)
                    hold(e, s["exp_set"], t)
                    e.tensor_tensor(dif[:], scores_sb[par][:], mxc[:, 0, :, None].broadcast_to([P, H, KEYS]), ALU.subtract)\
                        .then_inc(s["dif_set"], 1)

                def b():
                    hold(e, s["p_set"], t)
                    e.tensor_tensor(cut, scores_sb[par][:], mxc[:, 1, :, None].broadcast_to([P, H, KEYS]), ALU.subtract)\
                        .then_inc(s["cut_set"], 1)

                def c():
                    hold(e, s["exp_set"], t + 1)
                    hold(e, s["keep_set"], t + 1)
                    hold(e, s["p_turned"], 3 * t)
                    e.tensor_tensor(p1.rearrange("p (h k) -> p h k", k=KEYS), ex1, cut, ALU.mult).then_inc(s["p_set"], 1)

                def d():
                    hold(e, s["a_norm"], t + 1, alone=True)
                    e.tensor_tensor(x3[:, par], x2[:, t % 4], att1[:], ALU.add).then_inc(s["x3_set"], 1)
                return dict(dif=a, cut=b, product=c, x3=d)

            def mix(t, par):
                def one():
                    hold(e, s["f_r"], t + 1, alone=True)
                    e.tensor_scalar(er, er, 0.5, 0.5, ALU.mult, ALU.add).then_inc(s["f_one"], 1)

                def end():
                    hold(e, s["f_one"], t + 1)
                    hold(e, s["f_vv"], t + 1)
                    e.tensor_tensor(vv, vv, er, ALU.mult).then_inc(s["f_mul"], 1)
                    hold(e, s["f_mul"], t + 1)
                    hold(e, s["stored"], 16 * t)
                    e.tensor_tensor(fin[:], x3[:, par], vv, ALU.add).then_inc(s["f_fin"], 1)
                return dict(scale4=ln_scalars(2, t, s["n4_sq"], s["n4_step"], s["n4_nm"]), half=one, end=end)

            run_tiles(e, experts=experts, query=query, weigh=weigh, mix=mix)

        @block.scalar
        def _(e):
            e.dma_start(consts[:], consts_d).then_inc(s["consts_in"], 16)
            e.wait_ge(s["weights_in"], 32)
            e.wait_ge(s["k0_made"], 1)
            e.activation(k0.rearrange("p b k -> p (b k)"), psM0[:, 0:B * KEYS], ACT.Identity, bias=Cl["bk"]).then_inc(s["k0_copied"], 1)
            e.wait_ge(s["k1_made"], 1)
            e.activation(k1.rearrange("p b k -> p (b k)"), psM1[:, 0:B * KEYS], ACT.Copy).then_inc(s["k1_copied"], 1)
            e.wait_ge(s["ctx_in"], 16)
            for b in range(B):
                e.activation(ctxrep[:, b, 0:SW].rearrange("p (h k) -> p h k", k=KEYS),
                             ctx_sb[:, b, None, :].broadcast_to([P, H, KEYS]), ACT.Copy).then_inc(s["ctx_rep"], 1)

            def group(j):
                hold(e, s["h_turned"], j + 1)
                hold(e, s["h_q"], j)
                e.activation(xnT.rearrange("p b n -> p (b n)"), psM0, ACT.Copy).then_inc(s["h_xnT"], 1)
                hold(e, s["h_q"], j + 1)
                hold(e, s["s_made"], B * j)
                e.activation(q0T.rearrange("p b n -> p (b n)"), psM1, ACT.Identity, bias=Cl["bq"]).then_inc(s["h_qT"], 1)
                for b in range(B):
                    u = B * j + b
                    hold(e, s["s_sub"], u + 1)
                    hold(e, s["t_turned"], 3 * u)
                    e.activation(e0[:], d0.rearrange("p h k -> p (h k)"), ACT.Exp, scale=SCALE).then_inc(s["s_exp"], 1)
                    hold(e, s["pv_made"], u)
                    for g in (0, 2):
                        hold(e, s["t_turned"], 3 * u + g + 1)
                        if g == 0:
                            e.activation(pT[:, 0:4].rearrange("p c n -> p (c n)"), psT[:, 0], ACT.Copy).then_inc(s["t_copiedA"], 1)
                        else:
                            e.activation(pT[:, 8], psT[:, 0, 0:P], ACT.Copy).then_inc(s["t_copiedA"], 1)
                            e.activation(pT[0:LAST, 9], psT[0:LAST, 0, P:2 * P], ACT.Copy).then_inc(s["t_copiedA"], 1)
                    hold(e, s["o_turned"], u + 1)
                    hold(e, s["o_proj"], u)
                    e.activation(at0T[:], psM0[:, 256:384], ACT.Identity, bias=Cl["bv"]).then_inc(s["o_T"], 1)
                hold(e, s["q_turned"], j + 1)
                hold(e, s["q_made"], B * j)
                e.activation(xnT.rearrange("p b n -> p (b n)"), psM0, ACT.Copy).then_inc(s["q_zT"], 1)
                hold(e, s["m_sub"], j + 1)
                e.activation(sce[:], sc[:], ACT.Exp, scale=MSCALE).then_inc(s["m_exp"], 1)
                hold(e, s["m_turned"], j + 1)
                e.activation(xnT.rearrange("p b n -> p (b n)"), psM0, ACT.Copy).then_inc(s["m_oT"], 1)
                hold(e, s["y_turned"], j + 1)
                e.activation(xnT.rearrange("p b n -> p (b n)"), psM0, ACT.Copy).then_inc(s["y_T"], 1)
                hold(e, s["g_d"], j + 1)
                e.activation(ge[:], gd[:], ACT.Exp).then_inc(s["g_exp"], 1)

            group(0)
            with e.Fori(1, NJ) as j:
                group(j)

            for n in range(2):
                e.wait_ge(s["w12_made"], n + 1)
                e.activation(w12[:, 4 * n:4 * n + 4].rearrange("p e n -> p (e n)"), psM[:, n], ACT.Copy).then_inc(s["w12_stored"], 1)

            def ln_passes(k, t, src, src_ready, n_neg, n_sq, n_nm, n_out, dst, dst_free):
                def total():
                    src_ready()
                    e.activation(junk[:, k], src, ACT.Identity, scale=-1.0 / D, accum_out=lneg[:, k:k + 1]).then_inc(n_neg, 1)

                def square():
                    hold(e, n_neg, t + 1)
                    e.activation(junk[:, k], src, ACT.Square, bias=lneg[:, k:k + 1], accum_out=lsq[:, k:k + 1]).then_inc(n_sq, 1)

                def norm():
                    hold(e, n_nm, t + 1)
                    dst_free()
                    e.activation(dst, src, ACT.Identity, bias=lnm[:, k:k + 1], scale=lrs[:, k:k + 1]).then_inc(n_out, 1)
                return total, square, norm

            def experts(t, par):
                def copy():
                    hold(e, s["c_turned"], t + 1)
                    hold(e, s["mb_made"], 4 * t)
                    e.activation(y1T[:], psM0[:, 0:P], ACT.Copy).then_inc(s["c_copied"], 1)
                    e.activation(gT[:], psM0[0:E, P:2 * P], ACT.Copy).then_inc(s["c_copied"], 1)

                def gated(n):
                    def f():
                        if n == 0:
                            hold(e, s["mty"], t)
                        hold(e, s["mb_made"], 4 * t + n + 2)
                        if n == 0:
                            e.activation(mparts[:, E], psM0[:, 0:D], ACT.Copy)
                        lo, hi, at = [(0, 3, D), (3, 7, 0), (7, 8, 0)][n]
                        for x_ in range(lo, hi):
                            ins = e.activation(mparts[:, x_], psM0[:, at + (x_ - lo) * D:at + (x_ - lo + 1) * D], ACT.Copy,
                                               scale=cur[:, D + x_:D + x_ + 1])
                        ins.then_inc(s["mb_out"], 1)
                    return f
                sum2, square2, norm2 = ln_passes(0, t, psM0[:, 0:D], lambda: hold(e, s["mty"], t + 1), s["n2_neg"], s["n2_sq"],
                                                 s["n2_nm"], s["n2_out"], yn, lambda: hold(e, s["x2_set"], t))
                return dict(copy=copy, gated0=gated(0), gated1=gated(1), gated2=gated(2), sum2=sum2, square2=square2, norm2=norm2)

            def query(t, par):
                sum3, square3, norm3 = ln_passes(1, t, x2[:, t % 4], lambda: hold(e, s["x2_set"], t + 1), s["n3_neg"], s["n3_sq"],
                                                 s["n3_nm"], s["n3_out"], z2, lambda: hold(e, s["z_turned"], t))

                def zT():
                    hold(e, s["z_turned"], t + 1)
                    hold(e, s["q1_made"], t)
                    e.activation(z2T, psS[:, 0, 0:P], ACT.Copy).then_inc(s["z_T"], 1)

                def qT():
                    hold(e, s["q1_made"], t + 1)
                    hold(e, s["S_ready"], t)
                    e.activation(q1T, psS[:, 1, 0:P], ACT.Copy).then_inc(s["q1_T"], 1)

                def keep():
                    hold(e, s["S_ready"], t + 1)
                    if not (isinstance(t, int) and t < 2):
                        hold(e, s["S_read"], t - 1)
                        hold(e, s["cut_set"], t - 1)
                    e.activation(scores_sb[par].rearrange("p (g i) k -> p g (i k)", g=G), psS[:, :, 0:GW], ACT.Copy)\
                        .then_inc(s["S_kept"], 1)
                return dict(sum3=sum3, square3=square3, norm3=norm3, zT=zT, qT=qT, keep=keep)

            def weigh(t, par):
                def a():
                    hold(e, s["dif_set"], t + 1)
                    hold(e, s["p_set"], t)
                    e.activation(ex1, dif[:], ACT.Exp, scale=SCALE).then_inc(s["exp_set"], 1)

                def b():
                    hold(e, s["cut_set"], t + 1)
                    e.activation(cut, cut, ACT.Sign, bias=tiny[:]).then_inc(s["sign_set"], 1)
                    hold(e, s["sign_set"], t + 1)
                    e.activation(cut, cut, ACT.Relu).then_inc(s["keep_set"], 1)

                def c(g):
                    def f():
                        if g == 0:
                            hold(e, s["a_made"], t)
                        hold(e, s["p_turned"], 3 * t + g + 1)
                        if g < 2:
                            e.activation(pT1[:, 4 * g:4 * g + 4].rearrange("p c n -> p (c n)"), psT[:, 0], ACT.Copy)\
                                .then_inc(s["p_copied"], 1)
                        else:
                            e.activation(pT1[:, 8], psT[:, 0, 0:P], ACT.Copy)
                            e.activation(pT1[0:LAST, 9], psT[0:LAST, 0, P:2 * P], ACT.Copy).then_inc(s["p_copied"], 1)
                    return f
                return dict(exp=a, sign=b, copy0=c(0), copy1=c(1), copy2=c(2))

            def mix(t, par):
                a1, a2, a3 = ln_passes(2, t, x3[:, par], lambda: hold(e, s["x3_set"], t + 1), s["n4_neg"], s["n4_sq"],
                                       s["n4_nm"], s["n4_out"], zf[:], lambda: hold(e, s["f_turned"], t))

                def shift():
                    hold(e, s["f_kr"], t)
                    e.activation(zfT[:, 0:1], zfT[:, P:P + 1], ACT.Copy, scale=C["notfirst"][:, t:t + 1] if isinstance(t, int) else C["notfirst"][:, bass.ds(t, 1)]).then_inc(s["f_prev"], 1)
                    hold(e, s["f_turned"], t + 1)
                    hold(e, s["f_prev"], t + 1)
                    e.activation(zfT[:, 1:P + 1], psT[:, 1, 0:P], ACT.Copy).then_inc(s["f_T"], 1)

                def acts():
                    hold(e, s["f_kr"], t + 1)
                    hold(e, s["f_v"], t)
                    e.activation(ka, psT[:, 1, P:2 * P], ACT.Relu).then_inc(s["f_relu"], 1)
                    hold(e, s["f_mul"], t)
                    e.activation(er, psT[:, 1, 2 * P:3 * P], ACT.Tanh, scale=0.5).then_inc(s["f_r"], 1)
                    hold(e, s["f_relu"], t + 1)
                    e.activation(ka, ka, ACT.Square).then_inc(s["f_sq"], 1)

                def value():
                    hold(e, s["f_v"], t + 1)
                    hold(e, s["f_fin"], t)
                    e.activation(vv, psT[:, 1, 3 * P:4 * P], ACT.Copy).then_inc(s["f_vv"], 1)
                return dict(sum4=a1, square4=a2, norm4=a3, shift=shift, acts=acts, fvalue=value)

            run_tiles(e, experts=experts, query=query, weigh=weigh, mix=mix)

        @block.vector
        def _(e):
            fills = fill_parts()
            e.wait_ge(s["mask_in"], 16)
            e.tensor_copy(mask_f[:], mask_u8[:]).then_inc(s["mask_cast"], 1)
            e.wait_ge(s["mask_cast"], 1)
            e.wait_ge(s["constants_set"], 5)
            for n, f in enumerate(fills):
                for i in range(HG):
                    e.tensor_scalar(mrow[32 * n:32 * n + 1, :, i, :], mask_f[32 * n:32 * n + 1], -f, f, ALU.mult, ALU.add)\
                        .then_inc(s["mrow_made"], 1)
            e.wait_ge(s["k0_copied"], 1)
            e.tensor_tensor(k0[:], k0[:], mask_f[:], ALU.mult).then_inc(s["k0_masked"], 1)
            e.wait_ge(s["k0_masked"], 1)
            e.wait_ge(s["consts_in"], 16)
            for b in range(B):
                e.tensor_tensor(kblk0[:, b], k0[:, b, None, :].broadcast_to([P, HG, KEYS]),
                                blk[:, :, None].broadcast_to([P, HG, KEYS]), ALU.mult).then_inc(s["kblk0_made"], 1)
            for n in range(2 * B * 3):
                v, b, g = (vblk0, vblk1)[n // (3 * B)], n // 3 % B, n % 3
                lo, hi = 4 * g, min(4 * g + 4, NCH)
                e.wait_ge(s["v_turned"], n + 1)
                e.tensor_tensor(v[:, b, lo:hi, 0:D], psT[:, n % 2, 0:(hi - lo) * P].rearrange("p (c n) -> p c n", n=P),
                                headmask[:, lo:hi, 0:D], ALU.mult).then_inc(s["v_masked"], 1)

            def statistics(src, n):
                for b in range(B):
                    e.bn_stats(stats[:, b], src(b)).then_inc(s["ln_stats"], 1)
                hold(e, s["ln_stats"], B * n + B, alone=True)
                for b in range(B):
                    e.bn_aggr(mv[:, b], stats[:, b]).then_inc(s["ln_mv"], 1)
                hold(e, s["ln_mv"], B * n + B)
                e.tensor_scalar(veps[:], mv[:, :, 1], EPS, None, ALU.add).then_inc(s["ln_veps"], 1)

            def normalise(dst, src, n, n_out):
                hold(e, s["ln_rstd"], n + 1)
                for b in range(B):
                    e.tensor_scalar(dst[:, b], src(b), mv[:, b, 0:1], rstd[:, b:b + 1], ALU.subtract, ALU.mult).then_inc(n_out, 1)

            e.wait_ge(s["x_in"], 32)
            e.wait_ge(s["xbo_made"], 1)
            def group(j):
                hold(e, s["y_n"], B * j)
                statistics(lambda b: xs[:, NJ * b + j], 3 * j)
                hold(e, s["h_turned"], j)
                normalise(xn, lambda b: xs[:, NJ * b + j], 3 * j, s["h_xn"])
                for b in range(B):
                    u = B * j + b
                    t = NJ * b + j
                    hold(e, s["s_made"], u + 1)
                    hold(e, s["s_sub"], u)
                    e.tensor_reduce(mx0.rearrange("p (g i) -> p g i", g=G), score_banks(None), AX, ALU.max).then_inc(s["s_max"], 1)
                    hold(e, s["s_max"], u + 1)
                    hold(e, s["s_exp"], u)
                    e.tensor_tensor(d0.rearrange("p (g i) k -> p g i k", g=G), score_banks(None),
                                    mx0.rearrange("p (g i) -> p g i", g=G)[:, :, :, None].broadcast_to([P, G, HG, KEYS]),
                                    ALU.subtract).then_inc(s["s_sub"], 1)
                    hold(e, s["t_turned"], 3 * u + 2)
                    hold(e, s["pv_made"], u)
                    e.tensor_copy(pT[:, 4:8].rearrange("p c n -> p (c n)"), psT[:, 1]).then_inc(s["t_copiedV"], 1)
                    hold(e, s["pv_made"], u + 1)
                    hold(e, s["pv_norm"], u)
                    e.reciprocal(rden[:], psM0[:, D:VW]).then_inc(s["pv_den"], 1)
                    hold(e, s["pv_den"], u + 1)
                    hold(e, s["o_turned"], u)
                    e.tensor_tensor(at0.rearrange("p (h d) -> p h d", h=H), psM0[:, 0:D].rearrange("p (h d) -> p h d", h=H),
                                    rden[:, :, None].broadcast_to([P, H, HD]), ALU.mult).then_inc(s["pv_norm"], 1)
                    hold(e, s["o_proj"], u + 1)
                    e.tensor_tensor(x1[:, t], psM0[:, 384:512], x1[:, t], ALU.add).then_inc(s["x1_made"], 1)
                hold(e, s["x1_made"], B * j + B)
                hold(e, s["h_xn"], B * j + B)
                statistics(lambda b: x1[:, NJ * b + j], 3 * j + 1)
                hold(e, s["zob_made"], j)
                hold(e, s["q_turned"], j)
                normalise(zt, lambda b: x1[:, NJ * b + j], 3 * j + 1, s["q_z"])
                for b in range(B):
                    hold(e, s["q_made"], B * j + b + 1)
                    if b == 0:
                        hold(e, s["m_pv"], B * j)
                    e.tensor_tensor(qkv[:, b], psM[:, 1 - b % 2, 0:3 * D], Rw["inb"], ALU.add).then_inc(s["q_stored"], 1)
                for l in range(B):
                    if l == 0:
                        hold(e, s["m_pv"], B * j)
                    hold(e, s["m_prod"], B * j + l + 1)
                    e.tensor_reduce(sc[:, l].rearrange("p m h -> p (m h)"), prod[:, l].rearrange("p (m d) -> p m d", d=MHD),
                                    AX, ALU.add).then_inc(s["m_sc"], 1)
                hold(e, s["m_sc"], B * j + B)
                e.tensor_reduce(scx[:], sc.rearrange("p l m h -> p l h m"), AX, ALU.max).then_inc(s["m_soft"], 1)
                hold(e, s["m_soft"], 3 * j + 1)
                e.tensor_tensor(sc[:], sc[:], scx[:, :, None, :].broadcast_to([P, B, B, MH]), ALU.subtract).then_inc(s["m_sub"], 1)
                hold(e, s["m_exp"], j + 1)
                e.tensor_reduce(scs[:], sce.rearrange("p l m h -> p l h m"), AX, ALU.add).then_inc(s["m_soft"], 1)
                hold(e, s["m_soft"], 3 * j + 2)
                e.reciprocal(scr[:], scs[:]).then_inc(s["m_soft"], 1)
                hold(e, s["m_soft"], 3 * j + 3)
                e.tensor_tensor(sc[:], sce[:], scr[:, :, None, :].broadcast_to([P, B, B, MH]), ALU.mult).then_inc(s["m_w"], 1)
                for l in range(B):
                    if l == 0:
                        hold(e, s["y_made"], j)
                    hold(e, s["m_pv"], B * j + l + 1)
                    e.tensor_reduce(oo[:, l], prod[:, l].rearrange("p (n m) -> p n m", m=B), AX, ALU.add).then_inc(s["m_o"], 1)
                hold(e, s["m_proj"], j + 1)
                hold(e, s["m_turned"], j + 1)
                hold(e, s["zob_made"], j + 1)
                e.tensor_tensor(oo[:], psM1.rearrange("p (b n) -> p b n", b=B), zob[:], ALU.add).then_inc(s["m_res"], 1)
                hold(e, s["m_res"], j + 1)
                hold(e, s["q_z"], B * j + B)
                statistics(lambda b: oo[:, b], 3 * j + 2)
                normalise(oo, lambda b: oo[:, b], 3 * j + 2, s["y_n"])
                lg = psM1[:, 0:B * E].rearrange("p (b e) -> p b e", b=B)
                hold(e, s["lg_made"], j + 1)
                e.tensor_reduce(gmx[:], lg, AX, ALU.max).then_inc(s["g_step"], 1)
                hold(e, s["g_step"], 8 * j + 1)
                e.tensor_tensor(gd[:], lg, gmx[:, :, None].broadcast_to([P, B, E]), ALU.subtract).then_inc(s["g_d"], 1)
                e.tensor_tensor(geq[:], lg, gmx[:, :, None].broadcast_to([P, B, E]), ALU.is_ge).then_inc(s["g_step"], 1)
                hold(e, s["g_step"], 8 * j + 2)
                e.tensor_tensor(gp[:], geq[:], C["prio"][:, None, :].broadcast_to([P, B, E]), ALU.mult).then_inc(s["g_step"], 1)
                hold(e, s["g_step"], 8 * j + 3)
                e.tensor_reduce(gpm[:], gp[:], AX, ALU.max).then_inc(s["g_step"], 1)
                hold(e, s["g_exp"], j + 1)
                e.tensor_reduce(gsum[:], ge[:], AX, ALU.add).then_inc(s["g_step"], 1)
                hold(e, s["g_step"], 8 * j + 5)
                e.reciprocal(gval[:], gsum[:]).then_inc(s["g_step"], 1)
                hold(e, s["g_step"], 8 * j + 4)
                ohj = oh.rearrange("p (b j) e -> p b j e", b=B)[:, :, j]
                e.tensor_tensor(ohj, gp[:], gpm[:, :, None].broadcast_to([P, B, E]), ALU.is_equal).then_inc(s["g_step"], 1)
                hold(e, s["g_step"], 8 * j + 7)
                hold(e, s["g_step"], 8 * j + 6)
                e.tensor_tensor(ohg.rearrange("p (b j) e -> p b j e", b=B)[:, :, j], ohj,
                                gval[:, :, None].broadcast_to([P, B, E]), ALU.mult).then_inc(s["g_step"], 1)

            group(0)
            with e.Fori(1, NJ) as j:
                group(j)

            e.memset(before[:, 0], 0.0).then_inc(s["seen"], 1)
            for t in range(1, NT):
                e.wait_ge(s["seen"], t)
                e.tensor_tensor(before[:, t], before[:, t - 1], oh[:, t - 1], ALU.add).then_inc(s["seen"], 1)
            e.wait_ge(s["pos_made"], 1)
            e.wait_ge(s["g_step"], 8 * NJ)
            e.wait_ge(s["y_stored"], NJ)
            e.scalar_tensor_tensor(yg[:, :, D:D + E], psM0[:, 0:NT * E].rearrange("p (t e) -> p t e", e=E), CAP - 0.5, ohg[:],
                                   ALU.is_lt, ALU.mult).then_inc(s["gates_set"], 1)
            e.wait_ge(s["constants_set"], 7)
            e.wait_ge(s["w2_in"], 48)
            e.tensor_copy(b1z[:, :, ::E + 1], b1T[:]).then_inc(s["b1_spread"], 1)
            e.tensor_scalar(omu[:], cols[:, 3:5], -1.0, 1.0, ALU.mult, ALU.add).then_inc(s["b1_spread"], 1)
            e.wait_ge(s["b1_spread"], 2)
            e.wait_ge(s["weights_in"], 32)
            for dst, w, c in ((wr_now, "wr", Cl["mur"]), (wr_prev, "wr", omu[:, 0:1]), (wk_now, "wk", Cl["muk"]), (wk_prev, "wk", omu[:, 1:2])):
                e.tensor_scalar(dst[:], Wt[w], c, None, ALU.mult).then_inc(s["b1_spread"], 1)
            e.wait_ge(s["b12_made"], 1)
            e.tensor_tensor(b12[:], psT[0:E, 0, 0:D], b2[:], ALU.add).then_inc(s["b12_stored"], 1)

            def topk(t, par):
                n = [0]

                def largest(r):
                    def f():
                        if r == 0:
                            hold(e, s["mx_copied"], 2 * t)
                            hold(e, s["S_kept"], t + 1, alone=True)
                        for h in range(H):
                            if r and h % 4 == 0:
                                e.wait_ge(s["topk_step"], n[0] - 3 + h // 4)
                            ins = e.max(top[:, r, h], (left if r else scores_sb[par])[:, h])
                            if h % 4 == 3:
                                ins.then_inc(s["topk_step"], 1)
                        n[0] += 4
                    return f

                def mark(r):
                    def f():
                        for h in range(H):
                            if h % 4 == 0:
                                e.wait_ge(s["topk_step"], n[0] - 3 + h // 4)
                            ins = e.match_replace(left[:, h], top[:, r, h], (left if r else scores_sb[par])[:, h], GONE)
                            if h % 4 == 3:
                                ins.then_inc(s["topk_step"] if (r or h < H - 1) else s["topk_step"], 1)
                        n[0] += 4
                    return f

                def free_scores():
                    e.wait_ge(s["topk_step"], 8)
                    e.tensor_copy(mxc[:, 0], top[:, 0, :, 0]).then_inc(s["S_read"], 1)

                def ends():
                    e.wait_ge(s["topk_step"], n[0])
                    e.tensor_copy(mxc[:, 1], top[:, TOPK // 8 - 1, :, 7]).then_inc(s["mx_copied"], 1)
                    hold(e, s["S_read"], t + 1)
                    hold(e, s["mx_copied"], 2 * t + 1, alone=True)
                    e.sem_clear(s["topk_step"])
                    e.engine_nop().then_inc(s["mx_copied"], 1)

                out_ = {}
                for r in range(TOPK // 8):
                    out_[f"max{r}"] = largest(r)
                    if r < TOPK // 8 - 1:
                        out_[f"mark{r}"] = mark(r)
                    if r == 0:
                        out_["free"] = lambda: (hold(e, s["cut_set"], t), free_scores())
                out_["ends"] = ends
                return out_

            def weigh(t, par):
                def a():
                    hold(e, s["a_made"], t + 1)
                    e.reciprocal(rden1[:], psM1[:, D:VW]).then_inc(s["a_den"], 1)
                    hold(e, s["a_den"], t + 1)
                    hold(e, s["x3_set"], t)
                    e.tensor_tensor(att1.rearrange("p (h d) -> p h d", h=H), psM1[:, 0:D].rearrange("p (h d) -> p h d", h=H),
                                    rden1[:, :, None].broadcast_to([P, H, HD]), ALU.mult).then_inc(s["a_norm"], 1)
                return dict(norm=a)

            run_tiles(e, topk=topk, weigh=weigh)

        @block.tensor
        def _(e):
            mm, tr = e.matmul, e.transpose
            e.wait_ge(s["ctx_in"], 16)
            e.wait_ge(s["weights_in"], 32)
            keys = ctx_sb.rearrange("p b k -> p (b k)")
            mm(psM0[:, 0:B * KEYS], Wt["wk0"], keys, start=True, stop=True).then_inc(s["k0_made"], 1)
            mm(psM1[:, 0:B * KEYS], Wt["wk1"], keys, start=True, stop=True).then_inc(s["k1_made"], 1)
            e.wait_ge(s["constants_set"], 6)
            e.wait_ge(s["consts_in"], 16)
            for n in range(2 * B * 3):
                b, g = n // 3 % B, n % 3
                e.wait_ge(s["ctx_rep"], b + 1)
                if n >= 2:
                    e.wait_ge(s["v_masked"], n - 1)
                for c in range(4 * g, min(4 * g + 4, NCH)):
                    dst = psT[:, n % 2, (c % 4) * P:(c % 4 + 1) * P]
                    if n < 3 * B:
                        ins = mm(dst, ctxrep[:, b, c * P:(c + 1) * P], Wt["wv0"], start=True, stop=True)
                    else:
                        ins = tr(dst, ctxrep[:, b, c * P:(c + 1) * P], ident)
                ins.then_inc(s["v_turned"], 1)
            e.wait_ge(s["kblk0_made"], B)
            e.wait_ge(s["mrow_made"], 3 * HG)
            e.wait_ge(s["constants_set"], 4)
            e.wait_ge(s["k0_copied"], 1)
            e.wait_ge(s["k1_copied"], 1)
            e.wait_ge(s["v_masked"], 2 * B * 3)
            e.wait_ge(s["den_cols"], 2 * B)

            def turn4(src, ready, value, done, j):
                hold(e, ready, value)
                for b in range(B):
                    ins = tr(psM0[:, b * P:(b + 1) * P], src[:, b], ident)
                ins.then_inc(done, 1)

            def group(j):
                hold(e, s["y_T"], j)
                turn4(xn, s["h_xn"], B * j + B, s["h_turned"], j)
                hold(e, s["h_xnT"], j + 1)
                hold(e, s["g_step"], 8 * j)
                mm(psM1, Wt["wq0"], xnT.rearrange("p b n -> p (b n)"), start=True, stop=True).then_inc(s["h_q"], 1)
                hold(e, s["h_qT"], j + 1)

                def scores(b):
                    hold(e, s["s_sub"], B * j + b)
                    for g in range(G):
                        mm(psS[:, g, 0:GW], q0T[32 * g:32 * g + 32, b], kblk0[32 * g:32 * g + 32, b].rearrange("p i k -> p (i k)"),
                           start=True, stop=False)
                    for g in range(G):
                        ins = mm(psS[:, g, 0:GW], mones[:], mrow[:, b].rearrange("p i k -> p (i k)"), start=False, stop=True)
                    ins.then_inc(s["s_made"], 1)

                def attend(b):
                    u = B * j + b
                    hold(e, s["s_exp"], u + 1)
                    for g in range(3):
                        if g == 0:
                            hold(e, s["t_copiedA"], 3 * u)
                        elif g == 1:
                            hold(e, s["t_copiedV"], u)
                        else:
                            hold(e, s["t_copiedA"], 3 * u + 1)
                        for c in range(4 * g, min(4 * g + 4, NCH)):
                            w = P if c < NCH - 1 else LAST
                            ins = tr(psT[0:w, g % 2, (c % 4) * P:(c % 4 + 1) * P], e0[:, c * P:c * P + w], ident)
                        ins.then_inc(s["t_turned"], 1)
                    hold(e, s["t_copiedA"], 3 * u + 3)
                    hold(e, s["t_copiedV"], u + 1)
                    hold(e, s["x1_made"], u)
                    for c in range(NCH):
                        w = P if c < NCH - 1 else LAST
                        ins = mm(psM0[:, 0:VW], pT[0:w, c], vblk0[0:w, b, c], start=(c == 0), stop=(c == NCH - 1))
                    ins.then_inc(s["pv_made"], 1)
                    hold(e, s["pv_norm"], u + 1)
                    tr(psM0[:, 256:384], at0[:], ident).then_inc(s["o_turned"], 1)
                    hold(e, s["o_T"], u + 1)
                    mm(psM0[:, 384:512], at0T[:], Wt["wo0"], start=True, stop=True).then_inc(s["o_proj"], 1)

                scores(0)
                for b in range(B):
                    if b + 1 < B:
                        scores(b + 1)
                    attend(b)
                hold(e, s["x1_made"], B * j + B)
                turn4(zt, s["q_z"], B * j + B, s["q_turned"], j)
                hold(e, s["q_zT"], j + 1)
                for b in range(B):
                    if b >= 2:
                        hold(e, s["q_stored"], B * j + b - 1)
                    mm(psM[:, 1 - b % 2, 0:3 * D], xnT[:, b], Wt["inw"], start=True, stop=True).then_inc(s["q_made"], 1)
                hold(e, s["q_stored"], B * j + B)
                turn4(oo, s["m_o"], B * j + B, s["m_turned"], j)
                hold(e, s["m_oT"], j + 1)
                for b in range(B):
                    ins = mm(psM1[:, b * P:(b + 1) * P], xnT[:, b], Wt["outw"], start=True, stop=True)
                ins.then_inc(s["m_proj"], 1)
                turn4(y1s, s["y_made"], j + 1, s["y_turned"], j)
                hold(e, s["y_T"], j + 1)
                hold(e, s["m_res"], j + 1)
                for b in range(B):
                    ins = mm(psM1[:, b * E:(b + 1) * E], xnT[:, b], Wt["wg"], start=True, stop=True)
                ins.then_inc(s["lg_made"], 1)

            group(0)
            with e.Fori(1, NJ) as j:
                group(j)

            e.wait_ge(s["g_step"], 8 * NJ)
            mm(psM0[:, 0:NT * E], tri, oh.rearrange("p t e -> p (t e)"), start=True, stop=False)
            e.wait_ge(s["seen"], NT)
            mm(psM0[:, 0:NT * E], ones[:], before.rearrange("p t e -> p (t e)"), start=False, stop=True).then_inc(s["pos_made"], 1)
            e.wait_ge(s["w1_in"], 16)
            e.wait_ge(s["w2_in"], 48)
            e.wait_ge(s["gates_set"], 1)
            e.wait_ge(s["g_step"], 8 * NJ)
            for x_ in range(E):
                for c in range(FC):
                    ins = mm(psM[:, x_ // 4, (x_ % 4) * D:(x_ % 4 + 1) * D], w1T[:, c, x_], w2[:, c, x_], start=(c == 0), stop=(c == FC - 1))
                if x_ % 4 == 3:
                    ins.then_inc(s["w12_made"], 1)
            e.wait_ge(s["b1_spread"], 1)
            for x_ in range(E):
                for c in range(FC):
                    ins = mm(psT[0:E, 0, 0:D], b1z[:, c, x_ * E:(x_ + 1) * E], w2[:, c, x_],
                             start=(x_ == 0 and c == 0), stop=(x_ == E - 1 and c == FC - 1))
            ins.then_inc(s["b12_made"], 1)
            e.wait_ge(s["w12_stored"], 2)
            e.wait_ge(s["b12_stored"], 1)
            e.wait_ge(s["b1_spread"], 6)
            e.wait_ge(s["kblk1_made"], B)

            def experts(t, par):
                def turn():
                    hold(e, s["cur_set"], t + 1)
                    hold(e, s["n2_out"], t)
                    tr(psM0[:, 0:P], cur[:, 0:D], ident)
                    tr(psM0[0:E, P:2 * P], cur[:, D:D + E], ident).then_inc(s["c_turned"], 1)

                def moe(n):
                    def f():
                        if n == 0:
                            hold(e, s["c_copied"], 2 * t + 2)
                            mm(psM0[:, 0:D], gT[:], b12[:], start=True, stop=True).then_inc(s["mb_made"], 1)
                            mm(psM0[:, D:4 * D], y1T[:], w12[:, 0:3].rearrange("p e n -> p (e n)"), start=True, stop=True)\
                                .then_inc(s["mb_made"], 1)
                        else:
                            hold(e, s["mb_out"], 3 * t + n)
                            lo, hi = ((3, 7), (7, 8))[n - 1]
                            mm(psM0[:, 0:(hi - lo) * D], y1T[:], w12[:, lo:hi].rearrange("p e n -> p (e n)"), start=True, stop=True)\
                                .then_inc(s["mb_made"], 1)
                    return f

                def total():
                    hold(e, s["mb_out"], 3 * t + 3)
                    mm(psM0[:, 0:D], ident, cur[:, 0:D], start=True, stop=False)
                    for x_ in range(E + 1):
                        ins = mm(psM0[:, 0:D], ident, mparts[:, x_], start=False, stop=(x_ == E))
                    ins.then_inc(s["mty"], 1)
                return dict(turn=turn, moe0=moe(0), moe1=moe(1), moe2=moe(2), total=total)

            def query(t, par):
                def zturn():
                    hold(e, s["n3_out"], t + 1)
                    hold(e, s["S_kept"], t)
                    tr(psS[:, 0, 0:P], z2, ident).then_inc(s["z_turned"], 1)

                def ask():
                    hold(e, s["z_T"], t + 1)
                    mm(psS[:, 1, 0:P], Wt["wq1"], z2T, start=True, stop=True).then_inc(s["q1_made"], 1)

                def scores():
                    hold(e, s["q1_T"], t + 1)
                    hold(e, s["kcur_set"], t + 1)
                    for g in range(G):
                        ins = mm(psS[:, g, 0:GW], q1T[32 * g:32 * g + 32, :], kcur[32 * g:32 * g + 32], start=True, stop=True)
                    ins.then_inc(s["S_ready"], 1)
                return dict(zturn=zturn, ask=ask, scores=scores)

            def weigh(t, par):
                def turn(g):
                    def f():
                        if g == 0:
                            hold(e, s["p_set"], t + 1)
                        hold(e, s["p_copied"], 3 * t + g)
                        for c in range(4 * g, min(4 * g + 4, NCH)):
                            w = P if c < NCH - 1 else LAST
                            ins = tr(psT[0:w, 0, (c % 4) * P:(c % 4 + 1) * P], p1[:, c * P:c * P + w], ident)
                        ins.then_inc(s["p_turned"], 1)
                    return f

                def value():
                    hold(e, s["p_copied"], 3 * t + 3)
                    hold(e, s["a_norm"], t)
                    for c in range(NCH):
                        w = P if c < NCH - 1 else LAST
                        ins = mm(psM1[:, 0:VW], pT1[0:w, c], vblk1[0:w, t // NJ, c], start=(c == 0), stop=(c == NCH - 1),
                                 skip_group_check=True)
                    ins.then_inc(s["a_made"], 1)
                return dict(turn0=turn(0), turn1=turn(1), turn2=turn(2), value=value)

            def mix(t, par):
                def turn():
                    hold(e, s["n4_out"], t + 1)
                    hold(e, s["f_sq"], t)
                    hold(e, s["f_vv"], t)
                    tr(psT[:, 1, 0:P], zf[:], ident).then_inc(s["f_turned"], 1)

                def up():
                    hold(e, s["f_T"], t + 1)
                    now, prev = zfT[:, 1:P + 1], zfT[:, 0:P]
                    mm(psT[:, 1, P:2 * P], wk_now[:], now, start=True, stop=False, skip_group_check=True)
                    mm(psT[:, 1, P:2 * P], wk_prev[:], prev, start=False, stop=True, skip_group_check=True)
                    mm(psT[:, 1, 2 * P:3 * P], now, wr_now[:], start=True, stop=False, skip_group_check=True)
                    mm(psT[:, 1, 2 * P:3 * P], prev, wr_prev[:], start=False, stop=True, skip_group_check=True).then_inc(s["f_kr"], 1)

                def down():
                    hold(e, s["f_sq"], t + 1)
                    mm(psT[:, 1, 3 * P:4 * P], ka, Wt["wv"], start=True, stop=True, skip_group_check=True).then_inc(s["f_v"], 1)
                return dict(fturn=turn, up=up, down=down)

            run_tiles(e, experts=experts, query=query, weigh=weigh, mix=mix)


STAGES = dict(
    experts="load turn copy moe0 gated0 moe1 gated1 moe2 gated2 total sum2 square2 scale2 norm2 affine",
    query="keys sum3 square3 scale3 norm3 zturn zT ask qT scores keep",
    topk="max0 mark0 free max1 mark1 max2 mark2 max3 ends",
    weigh="dif cut exp sign product turn0 copy0 turn1 copy1 turn2 copy2 value norm x3",
    mix="sum4 square4 scale4 norm4 fturn shift up acts half down fvalue end",
)
ORDER = """dif max0 sum4 square4 load mark0 cut turn copy moe0 keys free exp max1 scale4 gated0 sign moe1 mark1 sum3
product gated1 max2 square3 moe2 norm4 gated2 fturn total shift scale3 mark2 norm3 turn0 sum2 zturn copy0
max3 up zT square2 turn1 scale2 acts ask copy1 half ends qT turn2 norm2 scores copy2 affine value keep
down norm fvalue x3 end""".split()


def run_tiles(e, **stages):
    def turn(i, known):
        steps = {}
        for name, ahead in (("experts", 2), ("query", 1), ("topk", 0), ("weigh", -1), ("mix", -2)):
            if name in stages and (not known or 0 <= i + ahead < NT):
                steps.update(stages[name](i + ahead, (known_parity + ahead) % 2))
        for name in ORDER:
            if name in steps:
                steps[name]()

    first, last = 5, NT - 3
    for i in range(-2, first):
        known_parity = i % 2
        turn(i, True)
    with e.Fori(first, last, 2) as i:
        for n in range(2):
            known_parity = (first + n) % 2
            turn(i + n, False)
    for i in range(last, NT + 2):
        known_parity = i % 2
        turn(i, True)


def kernel(**inputs):
    import numpy as np
    import concourse.bacc as bacc
    from concourse.bass_utils import run_bass_kernel_spmd as run

    a = {k: np.asarray(v) for k, v in inputs.items()}
    f32 = np.float32
    head = np.arange(NCH * P) // KEYS
    cols_of = np.arange(VW)
    own = np.where(cols_of < D, cols_of // HD, cols_of - D)
    headmask = (head[:, None] == own[None, :]).astype(f32).reshape(NCH, P, VW).transpose(1, 0, 2).reshape(P, -1)
    consts = np.concatenate([
        np.eye(P, dtype=f32),
        np.triu(np.ones((P, P), f32), 1),
        (np.arange(P)[:, None] % 32 // HD == np.arange(HG)[None, :]).astype(f32),
        np.broadcast_to(np.arange(E, 0, -1, dtype=f32), (P, E)),
        np.broadcast_to((np.arange(NT) % NJ != 0).astype(f32), (P, NT)),
        headmask,
    ], axis=1)
    weights = np.concatenate([
        a["L0_xattn_Wk"].T, a["L0_xattn_Wv"].T, a["L0_xattn_Wq"].T, a["L0_xattn_Wo"].T, a["L0_ffn_in_proj_w"].T,
        a["L0_ffn_out_proj_w"].T, a["L1_xattn_Wq"].T, a["L1_xattn_Wk"].T, a["L1_ffn_W_r"].T, a["L1_ffn_W_k"].T,
        a["L1_ffn_W_v"].T, a["L0_ffn_wg"],
    ], axis=1)
    cols = np.stack([a["L0_xattn_bq"], a["L0_xattn_bk"], a["L0_xattn_bv"], a["L1_ffn_mu_r"], a["L1_ffn_mu_k"]], axis=1)
    rows = np.concatenate([a["L0_xattn_bo"], a["L0_ffn_in_proj_b"], a["L0_ffn_out_proj_b"], a["L0_ffn_ln1_g"],
                           a["L0_ffn_ln1_b"], a["L0_ffn_ln2_g"], a["L0_ffn_ln2_b"]])[None, :]
    arrays = dict(
        x=a["x"].reshape(NT, P, D).transpose(1, 0, 2),
        ctxT=a["ctx_1024"].transpose(2, 0, 1),
        mask=a["mask_BxS2_bf1"].view(np.uint8).reshape(1, B * KEYS),
        consts=consts, weights=weights, cols=cols, rows=rows,
        b1T=a["L0_ffn_b1"].reshape(E, FC, P).transpose(2, 1, 0),
        b2=a["L0_ffn_b2"],
        w1T=a["L0_ffn_w1"].reshape(E, D, FC, P).transpose(3, 2, 0, 1),
        w2=a["L0_ffn_w2"].reshape(E, FC, P, D).transpose(2, 1, 0, 3),
    )
    nc = bacc.Bacc("TRN2", target_bir_lowering=False, num_devices=1)
    feed, args = {}, []
    for name, v in arrays.items():
        v = np.ascontiguousarray(v)
        feed[f"in_{name}"] = v
        args.append(nc.dram_tensor(f"in_{name}", v.shape, mybir.dt.from_np(v.dtype), kind="ExternalInput").ap())
    out = nc.dram_tensor("out", (NT, P, D), F32, kind="ExternalOutput").ap()
    build(nc, *args, out)
    r = run(nc, [feed], core_ids=[0])
    return r.results[0]["out"].reshape(B, SEQ, D)
```

```python
from contextlib import ExitStack

import concourse.bass as bass
from concourse import mybir

P = 128
B, SEQ, D = 4, 512, 128
NJ = SEQ // P
NT = B * NJ
KEYS = 77
H, HD = 16, 8
G = 4
HG = H // G
GW = HG * KEYS
SW = H * KEYS
NCH = -(-SW // P)
LAST = SW - (NCH - 1) * P
VW = D + H
TOPK = 32
EARLY = NJ - 1
MH, MHD = 4, 32
E, FF = 8, 512
FC = FF // P
CAP = B * SEQ // E
EPS = 1e-5
MASK_FILL = -1e8
SCALE = float(HD) ** -0.5
MSCALE = float(MHD) ** -0.5
GONE = -3.0e38
TINY = 1e-30

F32 = mybir.dt.float32
BF16 = mybir.dt.bfloat16
U8 = mybir.dt.uint8
ALU = mybir.AluOpType
ACT = mybir.ActivationFunctionType
AX = mybir.AxisListType.X

CONSTS = dict(ident=P, tri=P, blk=HG, prio=E, notfirst=NT, headmask=NCH * VW)
WEIGHTS = dict(wk0=D, wv0=D, wq0=D, wo0=D, inw=3 * D, outw=D, wq1=D, wk1=D, wr=D, wk=D, wv=D, wg=E)
COLS = dict(bq=1, bk=1, bv=1, mur=1, muk=1)
ROWS = dict(bo=D, inb=3 * D, ob=D, g1=D, b1=D, g2=D, b2=D)


def parts(ap, widths):
    at, out = 0, {}
    for name, width in widths.items():
        out[name] = ap[:, at:at + width]
        at += width
    return out


def fill_parts():
    import numpy as np
    rest = np.float32(MASK_FILL / SCALE)
    out = []
    for _ in range(3):
        top = (rest.view(np.uint32) & np.uint32(0xFFFF0000)).view(np.float32)
        out.append(float(top))
        rest = np.float32(rest - top)
    return out


def build(nc, x, ctxT, mask, consts_d, weights_d, cols_d, rows_d, b1T_d, b2_d, w1T_d, w2_d, out):
    with ExitStack() as stack:
        def sb(name, shape, dt=F32):
            return stack.enter_context(nc.sbuf_tensor(name, shape, dt))

        def pb(name, shape, dt=F32):
            return stack.enter_context(nc.psum_tensor(name, shape, dt))

        def sem(name):
            return stack.enter_context(nc.semaphore(name))

        consts = sb("consts", [P, sum(CONSTS.values())])
        C = parts(consts, CONSTS)
        weights = sb("weights", [P, sum(WEIGHTS.values())])
        Wt = parts(weights, WEIGHTS)
        cols = sb("cols", [P, len(COLS)])
        Cl = parts(cols, COLS)
        rows = sb("rows", [P, sum(ROWS.values())])
        Rw = parts(rows, ROWS)
        ident, tri, blk = C["ident"], C["tri"], C["blk"]
        headmask = C["headmask"].rearrange("p (c n) -> p c n", n=VW)
        ones = sb("ones", [P, P])
        expo = sb("expo", [P, HG])
        tiny = sb("tiny", [P, 1])

        x1 = sb("x1", [P, NT, D])
        yg = sb("yg", [P, NT, D + E])
        hT = sb("hT", [P, 2, B, P])
        x2 = hT.rearrange("p n b c -> p (n b) c")

        ctx_sb = sb("ctx_sb", [P, B, KEYS])
        area_a = sb("area_a", [P, 4 * SW])
        area_b = sb("area_b", [P, B * NCH * P])
        ctxrep = area_b.rearrange("p (b n) -> p b n", b=B)
        mask_u8 = sb("mask_u8", [P, B, KEYS], U8)
        mask_f = sb("mask_f", [P, B, KEYS])
        mrow = sb("mrow", [65, B, HG, KEYS], BF16)
        mones = sb("mones", [65, P], BF16)
        k0 = sb("k0", [P, B, KEYS])
        k1 = sb("k1", [P, B, KEYS])
        kblk0 = sb("kblk0", [P, B, HG, KEYS])
        kblk1 = sb("kblk1", [P, B, HG, KEYS])
        vblk0 = sb("vblk0", [P, B, NCH, VW])
        vblk1 = sb("vblk1", [P, B, NCH, VW])

        stats, mv, veps, rstd = {}, {}, {}, {}
        for n in ("x", "m"):
            stats[n] = sb(f"stats_{n}", [P, B, 6])
            mv[n] = sb(f"mv_{n}", [P, B, 2])
            veps[n] = sb(f"veps_{n}", [P, B])
            rstd[n] = sb(f"rstd_{n}", [P, B])
        xn = sb("xn", [P, B, D])
        xnT = hT[:, 0]
        q0T = hT[:, 1]
        mx0 = sb("mx0", [P, H])
        d0 = sb("d0", [P, H, KEYS])
        e0 = sb("e0", [P, SW])
        pT = sb("pT", [P, NCH, P])
        rden = sb("rden", [P, H])
        at0 = sb("at0", [P, D])
        at0T = sb("at0T", [P, P])
        mT = sb("mT", [P, B, P])
        zt = sb("zt", [P, B, D])
        zob = sb("zob", [P, B, D])
        qkv = sb("qkv", [P, B, 3 * D])
        prod = sb("prod", [P, B, 4 * D])
        sc = sb("sc", [P, B, B, MH])
        scx = sb("scx", [P, B, MH])
        sce = sb("sce", [P, B, B, MH])
        scs = sb("scs", [P, B, MH])
        scr = sb("scr", [P, B, MH])
        oo = sb("oo", [P, B, D])
        y1s = sb("y1s", [P, B, D])
        gmx = sb("gmx", [P, B])
        gd = sb("gd", [P, B, E])
        geq = sb("geq", [P, B, E])
        ge = sb("ge", [P, B, E])
        gsum = sb("gsum", [P, B])
        gval = sb("gval", [P, B])
        gp = sb("gp", [P, B, E])
        gpm = sb("gpm", [P, B])
        oh = sb("oh", [P, NT, E])
        ohg = sb("ohg", [P, NT, E])
        seen_to = [sb("seen_even", [P, NT, E]), sb("seen_odd", [P, NT, E])]

        w1T = area_a[:, 0:FC * E * D].rearrange("p (c e n) -> p c e n", c=FC, e=E)
        w2 = area_b[:, 0:FC * E * D].rearrange("p (c e n) -> p c e n", c=FC, e=E)
        seen_early = sb("seen_early", [P, EARLY, E])
        b1T = sb("b1T", [P, FC, E])
        b1z = sb("b1z", [P, FC, E * E])
        b2 = sb("b2", [E, D])
        w12 = sb("w12", [P, E, D])
        b12 = sb("b12", [E, D])
        omu = sb("omu", [P, 2])
        wr_now = sb("wr_now", [P, D])
        wr_prev = sb("wr_prev", [P, D])
        wk_now = sb("wk_now", [P, D])
        wk_prev = sb("wk_prev", [P, D])

        cur = sb("cur", [P, D + E])
        kcur = sb("kcur", [P, GW])
        y1T = sb("y1T", [P, P])
        gT = sb("gT", [E, P])
        mparts = C["headmask"][:, 0:(E + 1) * D].rearrange("p (e n) -> p e n", n=D)
        junk = xn[:, 0:3]
        lsum = sb("lsum", [P, 3])
        lneg = sb("lneg", [P, 3])
        lsq = sb("lsq", [P, 3])
        lvar = sb("lvar", [P, 3])
        lrs = sb("lrs", [P, 3])
        lnm = sb("lnm", [P, 3])
        yn = Wt["wk0"]
        z2 = Wt["wv0"]
        z2T = Wt["wk1"]
        q1T = C["headmask"][:, (E + 1) * D:(E + 2) * D]
        scores_sb = [area_a[:, n * SW:(n + 1) * SW].rearrange("p (h k) -> p h k", h=H) for n in range(2)]
        left = area_b[:, 0 * SW:1 * SW].rearrange("p (h k) -> p h k", h=H)
        top = sb("top", [P, TOPK // 8, H, 8])
        mxc = sb("mxc", [P, 2, H])
        dif = d0
        cut = area_b[:, 1 * SW:2 * SW].rearrange("p (h k) -> p h k", h=H)
        ex1 = area_b[:, 2 * SW:3 * SW].rearrange("p (h k) -> p h k", h=H)
        p1 = e0
        pT1 = pT
        rden1 = sb("rden1", [P, H])
        att1 = sb("att1", [P, D])
        x3 = sb("x3", [P, 2, D])
        zf = xn[:, 3]
        zfT = sb("zfT", [P, P + 1])
        ka = y1s[:, 0]
        er = y1s[:, 1]
        vv = y1s[:, 2]
        fin = sb("fin", [P, D])

        psS = pb("psS", [P, G, 512])
        psT = pb("psT", [P, 2, 512])
        psM = pb("psM", [P, 2, 512])
        psM0, psM1 = psM[:, 0], psM[:, 1]

        scores_ps = psS[:, :, 0:GW].rearrange("p g (i k) -> p g i k", k=KEYS)

        names = """x_in b_in ctx_in mask_in consts_in weights_in w1_in w2_in k0_made k1_made k0_copied k1_copied mask_cast
        mrow_made k0_masked kblk0_made kblk1_made ctx_rep v_turned v_masked den_cols xbo_made h_xn h_turned
        h_xnT h_q h_qT s_made s_max s_sub s_exp t_turned t_copiedA t_copiedV pv_made pv_den pv_norm o_turned
        o_T o_proj x1_made q_z q_turned q_zT q_made q_stored zob_made m_prod m_sc m_sub m_exp m_w m_pv m_o
        m_turned m_oT m_proj m_res y_n y_g y_made y_stored y_turned y_T lg_made g_d g_exp seen pos_made
        gates_set w12_made w12_stored b1_spread b12_made b12_stored cur_set kcur_set c_turned c_copied
        mb_made mb_out mty n2_neg n2_sq n2_step n2_nm n2_out x2_set n3_neg n3_sq n3_step n3_nm n3_out
        z_turned z_T q1_made q1_T S_ready S_kept S_read topk_step mx_copied dif_set cut_set exp_set sign_set
        keep_set p_set p_turned p_copied a_made a_den a_norm x3_set n4_neg n4_sq n4_step n4_nm n4_out
        f_turned f_prev f_T f_kr f_relu f_sq f_r f_v f_vv f_one passed f_mul f_fin stored constants_set
        x_stats x_mv x_veps x_rstd m_stats m_mv m_veps m_rstd m_soft g_step y2_step x1_biased early_seen""".split()
        s = {n: sem(n) for n in names}

        def hold(e, semaphore, value, alone=False):
            if isinstance(value, int):
                if value > 0:
                    e.wait_ge(semaphore, value)
                return
            if not alone:
                e.wait_ge(s["constants_set"], 1)
            e.wait_ge(semaphore, value)
            if alone:
                e.sem_inc(s["passed"], 1)

        block = stack.enter_context(nc.Block())

        @block.sync
        def _(e):
            e.dma_start(ctx_sb[:], ctxT).then_inc(s["ctx_in"], 16)
            e.dma_start(weights[:], weights_d).then_inc(s["weights_in"], 16)
            e.dma_start(cols[:], cols_d).then_inc(s["weights_in"], 16)
            e.dma_start(mask_u8[:], mask.broadcast_to([P, B * KEYS]).rearrange("p (b k) -> p b k", b=B)).then_inc(s["mask_in"], 16)
            e.dma_start(x1[:], x).then_inc(s["x_in"], 16)
            e.dma_start(rows[:], rows_d.broadcast_to([P, sum(ROWS.values())])).then_inc(s["x_in"], 16)
            e.dma_start(b1T[:], b1T_d).then_inc(s["b_in"], 16)
            e.dma_start(b2[:], b2_d).then_inc(s["b_in"], 16)
            e.dma_start(w1T, w1T_d).then_inc(s["w1_in"], 16)
            e.wait_ge(s["v_turned"], 2 * B * 3)
            e.dma_start(w2, w2_d).then_inc(s["w2_in"], 16)
            with e.Fori(0, NT) as t:
                hold(e, s["f_fin"], t + 1)
                e.dma_start(out[t], fin[:]).then_inc(s["stored"], 16)
            e.wait_ge(s["stored"], 16 * NT)

        @block.gpsimd
        def _(e):
            e.memset(ones[:], 1.0).then_inc(s["constants_set"], 1)
            e.memset(expo[:], -0.5).then_inc(s["constants_set"], 1)
            e.memset(tiny[:], TINY).then_inc(s["constants_set"], 1)
            e.memset(mones[:], 1.0).then_inc(s["constants_set"], 1)
            e.memset(mrow[:], 0.0).then_inc(s["constants_set"], 1)
            e.memset(ctxrep[:, :, SW:], 0.0).then_inc(s["constants_set"], 1)
            e.memset(b1z[:], 0.0).then_inc(s["constants_set"], 1)
            e.memset(zfT[:], 0.0).then_inc(s["constants_set"], 1)
            e.wait_ge(s["consts_in"], 16)
            for v in (vblk0, vblk1):
                for b in range(B):
                    e.tensor_copy(v[:, b, :, D:VW], headmask[:, :, D:VW]).then_inc(s["den_cols"], 1)
            e.wait_ge(s["k1_copied"], 1)
            for b in range(B):
                e.tensor_tensor(kblk1[:, b], k1[:, b, None, :].broadcast_to([P, HG, KEYS]),
                                blk[:, :, None].broadcast_to([P, HG, KEYS]), ALU.mult).then_inc(s["kblk1_made"], 1)
            e.wait_ge(s["constants_set"], 2)

            def rstd_of(k, n):
                hold(e, s[k + "_veps"], n + 1)
                e.tensor_tensor(rstd[k][:], veps[k][:], expo[:], ALU.pow).then_inc(s[k + "_rstd"], 1)

            def attend(j, par):
                def bias():
                    if isinstance(j, int) and j == 0:
                        e.wait_ge(s["x_in"], 32)
                    hold(e, s["h_xn"], B * j + B, alone=True)
                    for b in range(B):
                        e.tensor_tensor(x1[:, NJ * b + j], x1[:, NJ * b + j], Rw["bo"], ALU.add).then_inc(s["xbo_made"], 1)
                return dict(hrstd=lambda: rstd_of("x", j), bias=bias)

            def among(j, par):
                def zbias():
                    hold(e, s["q_z"], B * j + B)
                    hold(e, s["m_res"], j)
                    e.tensor_tensor(zob[:], zt[:], Rw["ob"][:, None, :].broadcast_to([P, B, D]), ALU.add).then_inc(s["zob_made"], 1)

                def xbias():
                    hold(e, s["q_z"], B * j + B, alone=True)
                    for b in range(B):
                        e.tensor_tensor(x1[:, NJ * b + j], x1[:, NJ * b + j], Rw["b2"], ALU.add).then_inc(s["x1_biased"], 1)

                def affine():
                    hold(e, s["y_n"], B * j + B)
                    hold(e, s["y_turned"], j)
                    hold(e, s["y_stored"], j)
                    e.tensor_tensor(y1s[:], oo[:], Rw["g1"][:, None, :].broadcast_to([P, B, D]), ALU.mult).then_inc(s["y_g"], 1)
                    hold(e, s["y_g"], j + 1)
                    e.tensor_tensor(y1s[:], y1s[:], Rw["b1"][:, None, :].broadcast_to([P, B, D]), ALU.add).then_inc(s["y_made"], 1)

                def store():
                    hold(e, s["y_made"], j + 1)
                    e.tensor_copy(yg.rearrange("p (b j) n -> p b j n", b=B)[:, :, j, 0:D], y1s[:]).then_inc(s["y_stored"], 1)
                steps = dict(zrstd=lambda: rstd_of("m", 2 * j), zbias=zbias, xbias=xbias, yrstd=lambda: rstd_of("m", 2 * j + 1),
                             yaffine=affine, ystore=store)
                return steps

            run_groups(e, attend=attend, among=among)

            def ln_scalars(k, t, n_sq, n_step, n_nm):
                def scale():
                    hold(e, n_sq, t + 1, alone=True)
                    e.tensor_scalar(lvar[:, k:k + 1], lsq[:, k:k + 1], 1.0 / D, EPS, ALU.mult, ALU.add).then_inc(n_step, 1)
                    hold(e, n_step, 2 * t + 1)
                    e.tensor_tensor(lrs[:, k:k + 1], lvar[:, k:k + 1], expo[:, 0:1], ALU.pow).then_inc(n_step, 1)
                    hold(e, n_step, 2 * t + 2)
                    e.tensor_tensor(lnm[:, k:k + 1], lneg[:, k:k + 1], lrs[:, k:k + 1], ALU.mult).then_inc(n_nm, 1)
                return scale

            def experts(t, par):
                def load():
                    if isinstance(t, int) and t in (0, EARLY):
                        e.wait_ge(s["gates_set"], 1 if t < EARLY else 2)
                    hold(e, s["mty"], t)
                    e.tensor_copy(cur[:], yg[:, t, :]).then_inc(s["cur_set"], 1)

                def affine():
                    hold(e, s["n2_out"], t + 1)
                    e.tensor_tensor(yn, yn, Rw["g2"], ALU.mult).then_inc(s["y2_step"], 1)
                    if isinstance(t, int) and t in (0, EARLY):
                        e.wait_ge(s["x1_biased"], B * EARLY if t < EARLY else NT)
                    hold(e, s["y2_step"], t + 1, alone=True)
                    e.tensor_tensor(x2[:, t % 8], yn, x1[:, t], ALU.add).then_inc(s["x2_set"], 1)
                return dict(load=load, scale2=ln_scalars(0, t, s["n2_sq"], s["n2_step"], s["n2_nm"]), affine=affine)

            def query(t, par):
                def keys():
                    hold(e, s["S_ready"], t)
                    e.tensor_copy(kcur[:], kblk1.rearrange("p b i k -> p b (i k)")[:, t // NJ]).then_inc(s["kcur_set"], 1)
                return dict(keys=keys, scale3=ln_scalars(1, t, s["n3_sq"], s["n3_step"], s["n3_nm"]))

            def weigh(t, par):
                def a():
                    hold(e, s["mx_copied"], 2 * t + 2)
                    hold(e, s["exp_set"], t)
                    e.tensor_tensor(dif[:], scores_sb[par][:], mxc[:, 0, :, None].broadcast_to([P, H, KEYS]), ALU.subtract)\
                        .then_inc(s["dif_set"], 1)

                def b():
                    hold(e, s["p_set"], t)
                    e.tensor_tensor(cut, scores_sb[par][:], mxc[:, 1, :, None].broadcast_to([P, H, KEYS]), ALU.subtract)\
                        .then_inc(s["cut_set"], 1)

                def c():
                    hold(e, s["exp_set"], t + 1)
                    hold(e, s["keep_set"], t + 1)
                    hold(e, s["p_turned"], 3 * t)
                    e.tensor_tensor(p1.rearrange("p (h k) -> p h k", k=KEYS), ex1, cut, ALU.mult).then_inc(s["p_set"], 1)

                return dict(dif=a, cut=b, product=c)

            def value(t, par):
                def d():
                    if not (isinstance(t, int) and t < 2):
                        hold(e, s["f_fin"], t - 1)
                        hold(e, s["n4_out"], t - 1)
                    hold(e, s["a_norm"], t + 1, alone=True)
                    e.tensor_tensor(x3[:, par], x2[:, t % 8], att1[:], ALU.add).then_inc(s["x3_set"], 1)
                return dict(x3=d)

            def mix(t, par):
                def one():
                    hold(e, s["f_r"], t + 1, alone=True)
                    e.tensor_scalar(er, er, 0.5, 0.5, ALU.mult, ALU.add).then_inc(s["f_one"], 1)

                def end():
                    hold(e, s["f_one"], t + 1)
                    hold(e, s["f_vv"], t + 1)
                    e.tensor_tensor(vv, vv, er, ALU.mult).then_inc(s["f_mul"], 1)
                    hold(e, s["f_mul"], t + 1)
                    hold(e, s["stored"], 16 * t)
                    e.tensor_tensor(fin[:], x3[:, par], vv, ALU.add).then_inc(s["f_fin"], 1)
                return dict(scale4=ln_scalars(2, t, s["n4_sq"], s["n4_step"], s["n4_nm"]), half=one, end=end)

            hand_over(e, among=among, experts=experts, query=query, weigh=weigh)
            run_tiles(e, experts=experts, query=query, weigh=weigh, value=value, mix=mix)

        @block.scalar
        def _(e):
            e.dma_start(consts[:], consts_d).then_inc(s["consts_in"], 16)
            e.wait_ge(s["weights_in"], 32)
            e.wait_ge(s["k0_made"], 1)
            e.activation(k0.rearrange("p b k -> p (b k)"), psM0[:, 0:B * KEYS], ACT.Identity, bias=Cl["bk"]).then_inc(s["k0_copied"], 1)
            e.wait_ge(s["k1_made"], 1)
            e.activation(k1.rearrange("p b k -> p (b k)"), psM1[:, 0:B * KEYS], ACT.Copy).then_inc(s["k1_copied"], 1)
            e.wait_ge(s["ctx_in"], 16)
            for b in range(B):
                e.activation(ctxrep[:, b, 0:SW].rearrange("p (h k) -> p h k", k=KEYS),
                             ctx_sb[:, b, None, :].broadcast_to([P, H, KEYS]), ACT.Copy).then_inc(s["ctx_rep"], 1)

            def attend(j, par):
                def turned():
                    hold(e, s["h_turned"], j + 1)
                    hold(e, s["h_q"], j)
                    e.activation(xnT.rearrange("p b n -> p (b n)"), psM0, ACT.Copy).then_inc(s["h_xnT"], 1)

                def queries():
                    hold(e, s["h_q"], j + 1)
                    hold(e, s["s_made"], B * j)
                    e.activation(q0T.rearrange("p b n -> p (b n)"), psM0, ACT.Identity, bias=Cl["bq"]).then_inc(s["h_qT"], 1)

                def tile(b):
                    u = B * j + b

                    def exp():
                        hold(e, s["s_sub"], u + 1)
                        hold(e, s["t_turned"], 3 * u)
                        e.activation(e0[:], d0.rearrange("p h k -> p (h k)"), ACT.Exp, scale=SCALE).then_inc(s["s_exp"], 1)

                    def first():
                        hold(e, s["pv_made"], u)
                        hold(e, s["t_turned"], 3 * u + 1)
                        e.activation(pT[:, 0:4].rearrange("p c n -> p (c n)"), psT[:, 0], ACT.Copy).then_inc(s["t_copiedA"], 1)

                    def third():
                        hold(e, s["t_turned"], 3 * u + 3)
                        e.activation(pT[:, 8], psT[:, 0, 0:P], ACT.Copy).then_inc(s["t_copiedA"], 1)
                        e.activation(pT[0:LAST, 9], psT[0:LAST, 0, P:2 * P], ACT.Copy).then_inc(s["t_copiedA"], 1)

                    def turned():
                        hold(e, s["o_turned"], u + 1)
                        hold(e, s["o_proj"], u)
                        e.activation(at0T[:], psM0[:, 256:384], ACT.Identity, bias=Cl["bv"]).then_inc(s["o_T"], 1)
                    return {f"exp{b}": exp, f"ca{b}": first, f"cc{b}": third, f"oT{b}": turned}
                steps = dict(hT=turned, hqT=queries)
                for b in range(B):
                    steps.update(tile(b))
                if isinstance(j, int) and j == 0:
                    for n in range(2):
                        def keep(n=n):
                            e.wait_ge(s["w12_made"], n + 1)
                            e.activation(w12[:, 4 * n:4 * n + 4].rearrange("p e n -> p (e n)"), psM1, ACT.Copy).then_inc(s["w12_stored"], 1)
                        steps[f"w12c{n}"] = keep
                return steps

            def among(j, par):
                def turned(ready, done):
                    def f():
                        hold(e, s[ready], j + 1)
                        hold(e, s["lg_made"], j)
                        e.activation(mT.rearrange("p b n -> p (b n)"), psM1, ACT.Copy).then_inc(s[done], 1)
                    return f

                def exp():
                    hold(e, s["m_sub"], j + 1)
                    e.activation(sce[:], sc[:], ACT.Exp, scale=MSCALE).then_inc(s["m_exp"], 1)

                def gate():
                    hold(e, s["g_d"], j + 1)
                    e.activation(ge[:], gd[:], ACT.Exp).then_inc(s["g_exp"], 1)
                steps = dict(zT=turned("q_turned", "q_zT"), mexp=exp, mTc=turned("m_turned", "m_oT"), yT=turned("y_turned", "y_T"),
                             gexp=gate)
                return steps

            run_groups(e, attend=attend, among=among)

            def ln_passes(k, t, src, src_ready, n_neg, n_sq, n_nm, n_out, dst, dst_free):
                def total():
                    src_ready()
                    e.activation(junk[:, k], src, ACT.Identity, scale=-1.0 / D, accum_out=lneg[:, k:k + 1]).then_inc(n_neg, 1)

                def square():
                    hold(e, n_neg, t + 1)
                    e.activation(junk[:, k], src, ACT.Square, bias=lneg[:, k:k + 1], accum_out=lsq[:, k:k + 1]).then_inc(n_sq, 1)

                def norm():
                    hold(e, n_nm, t + 1)
                    dst_free()
                    e.activation(dst, src, ACT.Identity, bias=lnm[:, k:k + 1], scale=lrs[:, k:k + 1]).then_inc(n_out, 1)
                return total, square, norm

            def experts(t, par):
                def copy():
                    hold(e, s["c_turned"], t + 1)
                    hold(e, s["mb_made"], 4 * t)
                    e.activation(y1T[:], psM0[:, 0:P], ACT.Copy).then_inc(s["c_copied"], 1)
                    e.activation(gT[:], psM0[0:E, P:2 * P], ACT.Copy).then_inc(s["c_copied"], 1)

                def gated(n):
                    def f():
                        if n == 0:
                            hold(e, s["mty"], t)
                        hold(e, s["mb_made"], 4 * t + n + 2)
                        if n == 0:
                            e.activation(mparts[:, E], psM0[:, 0:D], ACT.Copy)
                        lo, hi, at = [(0, 3, D), (3, 7, 0), (7, 8, 0)][n]
                        for x_ in range(lo, hi):
                            ins = e.activation(mparts[:, x_], psM0[:, at + (x_ - lo) * D:at + (x_ - lo + 1) * D], ACT.Copy,
                                               scale=cur[:, D + x_:D + x_ + 1])
                        ins.then_inc(s["mb_out"], 1)
                    return f
                sum2, square2, norm2 = ln_passes(0, t, psM0[:, 0:D], lambda: hold(e, s["mty"], t + 1), s["n2_neg"], s["n2_sq"],
                                                 s["n2_nm"], s["n2_out"], yn, lambda: hold(e, s["x2_set"], t))
                return dict(copy=copy, gated0=gated(0), gated1=gated(1), gated2=gated(2), sum2=sum2, square2=square2, norm2=norm2)

            def query(t, par):
                sum3, square3, norm3 = ln_passes(1, t, x2[:, t % 8], lambda: hold(e, s["x2_set"], t + 1), s["n3_neg"], s["n3_sq"],
                                                 s["n3_nm"], s["n3_out"], z2, lambda: hold(e, s["z_turned"], t))

                def zT():
                    hold(e, s["z_turned"], t + 1)
                    hold(e, s["q1_made"], t)
                    e.activation(z2T, psS[:, 0, 0:P], ACT.Copy).then_inc(s["z_T"], 1)

                def qT():
                    hold(e, s["q1_made"], t + 1)
                    hold(e, s["S_ready"], t)
                    e.activation(q1T, psS[:, 1, 0:P], ACT.Copy).then_inc(s["q1_T"], 1)

                return dict(sum3=sum3, square3=square3, norm3=norm3, zT=zT, qT=qT)

            def kept(t, par):
                def keep():
                    hold(e, s["S_ready"], t + 1)
                    if not (isinstance(t, int) and t < 2):
                        hold(e, s["S_read"], t - 1)
                        hold(e, s["cut_set"], t - 1)
                    e.activation(scores_sb[par].rearrange("p (g i) k -> p g (i k)", g=G), psS[:, :, 0:GW], ACT.Copy)\
                        .then_inc(s["S_kept"], 1)
                return dict(keep=keep)

            def weigh(t, par):
                def a():
                    hold(e, s["dif_set"], t + 1)
                    hold(e, s["p_set"], t)
                    e.activation(ex1, dif[:], ACT.Exp, scale=SCALE).then_inc(s["exp_set"], 1)

                def b():
                    hold(e, s["cut_set"], t + 1)
                    e.activation(cut, cut, ACT.Sign, bias=tiny[:]).then_inc(s["sign_set"], 1)
                    hold(e, s["sign_set"], t + 1)
                    e.activation(cut, cut, ACT.Relu).then_inc(s["keep_set"], 1)

                def c(g):
                    def f():
                        if g == 0:
                            hold(e, s["a_made"], t)
                        hold(e, s["p_turned"], 3 * t + g + 1)
                        if g < 2:
                            e.activation(pT1[:, 4 * g:4 * g + 4].rearrange("p c n -> p (c n)"), psT[:, 0], ACT.Copy)\
                                .then_inc(s["p_copied"], 1)
                        else:
                            e.activation(pT1[:, 8], psT[:, 0, 0:P], ACT.Copy)
                            e.activation(pT1[0:LAST, 9], psT[0:LAST, 0, P:2 * P], ACT.Copy).then_inc(s["p_copied"], 1)
                    return f
                return dict(exp=a, sign=b, copy0=c(0), copy1=c(1), copy2=c(2))

            def mix(t, par):
                a1, a2, a3 = ln_passes(2, t, x3[:, par], lambda: hold(e, s["x3_set"], t + 1), s["n4_neg"], s["n4_sq"],
                                       s["n4_nm"], s["n4_out"], zf, lambda: hold(e, s["f_turned"], t))

                def shift():
                    hold(e, s["f_kr"], t)
                    e.activation(zfT[:, 0:1], zfT[:, P:P + 1], ACT.Copy, scale=C["notfirst"][:, t:t + 1] if isinstance(t, int) else C["notfirst"][:, bass.ds(t, 1)]).then_inc(s["f_prev"], 1)
                    hold(e, s["f_turned"], t + 1)
                    hold(e, s["f_prev"], t + 1)
                    e.activation(zfT[:, 1:P + 1], psT[:, 1, 0:P], ACT.Copy).then_inc(s["f_T"], 1)

                def acts():
                    hold(e, s["f_kr"], t + 1)
                    hold(e, s["f_v"], t)
                    e.activation(ka, psT[:, 1, P:2 * P], ACT.Relu).then_inc(s["f_relu"], 1)
                    hold(e, s["f_mul"], t)
                    e.activation(er, psT[:, 1, 2 * P:3 * P], ACT.Tanh, scale=0.5).then_inc(s["f_r"], 1)
                    hold(e, s["f_relu"], t + 1)
                    e.activation(ka, ka, ACT.Square).then_inc(s["f_sq"], 1)

                def value():
                    hold(e, s["f_v"], t + 1)
                    hold(e, s["f_fin"], t)
                    e.activation(vv, psT[:, 1, 3 * P:4 * P], ACT.Copy).then_inc(s["f_vv"], 1)
                return dict(sum4=a1, square4=a2, norm4=a3, shift=shift, acts=acts, fvalue=value)

            hand_over(e, among=among, experts=experts, query=query, kept=kept, weigh=weigh)
            run_tiles(e, experts=experts, query=query, kept=kept, weigh=weigh, mix=mix)

        @block.vector
        def _(e):
            fills = fill_parts()
            e.wait_ge(s["mask_in"], 16)
            e.tensor_copy(mask_f[:], mask_u8[:]).then_inc(s["mask_cast"], 1)
            e.wait_ge(s["mask_cast"], 1)
            e.wait_ge(s["constants_set"], 5)
            for n, f in enumerate(fills):
                for i in range(HG):
                    e.tensor_scalar(mrow[32 * n:32 * n + 1, :, i, :], mask_f[32 * n:32 * n + 1], -f, f, ALU.mult, ALU.add)\
                        .then_inc(s["mrow_made"], 1)
            e.wait_ge(s["k0_copied"], 1)
            e.tensor_tensor(k0[:], k0[:], mask_f[:], ALU.mult).then_inc(s["k0_masked"], 1)
            e.wait_ge(s["k0_masked"], 1)
            e.wait_ge(s["consts_in"], 16)
            for b in range(B):
                e.tensor_tensor(kblk0[:, b], k0[:, b, None, :].broadcast_to([P, HG, KEYS]),
                                blk[:, :, None].broadcast_to([P, HG, KEYS]), ALU.mult).then_inc(s["kblk0_made"], 1)
            for n in range(2 * B * 3):
                v, b, g = (vblk0, vblk1)[n // (3 * B)], n // 3 % B, n % 3
                lo, hi = 4 * g, min(4 * g + 4, NCH)
                e.wait_ge(s["v_turned"], n + 1)
                e.tensor_tensor(v[:, b, lo:hi, 0:D], psT[:, n % 2, 0:(hi - lo) * P].rearrange("p (c n) -> p c n", n=P),
                                headmask[:, lo:hi, 0:D], ALU.mult).then_inc(s["v_masked"], 1)

            e.wait_ge(s["constants_set"], 7)
            e.wait_ge(s["b_in"], 32)
            e.tensor_copy(b1z[:, :, ::E + 1], b1T[:]).then_inc(s["b1_spread"], 1)
            e.wait_ge(s["weights_in"], 32)
            e.tensor_scalar(omu[:], cols[:, 3:5], -1.0, 1.0, ALU.mult, ALU.add).then_inc(s["b1_spread"], 1)
            e.wait_ge(s["b1_spread"], 2)
            for dst, w, c in ((wr_now, "wr", Cl["mur"]), (wr_prev, "wr", omu[:, 0:1]), (wk_now, "wk", Cl["muk"]), (wk_prev, "wk", omu[:, 1:2])):
                e.tensor_scalar(dst[:], Wt[w], c, None, ALU.mult).then_inc(s["b1_spread"], 1)
            e.wait_ge(s["x_in"], 32)

            def statistics(k, src, n):
                for b in range(B):
                    e.bn_stats(stats[k][:, b], src(b)).then_inc(s[k + "_stats"], 1)
                hold(e, s[k + "_stats"], B * n + B, alone=True)
                for b in range(B):
                    e.bn_aggr(mv[k][:, b], stats[k][:, b]).then_inc(s[k + "_mv"], 1)
                hold(e, s[k + "_mv"], B * n + B)
                e.tensor_scalar(veps[k][:], mv[k][:, :, 1], EPS, None, ALU.add).then_inc(s[k + "_veps"], 1)

            def normalise(k, dst, src, n, n_out):
                hold(e, s[k + "_rstd"], n + 1)
                for b in range(B):
                    e.tensor_scalar(dst[:, b], src(b), mv[k][:, b, 0:1], rstd[k][:, b:b + 1], ALU.subtract, ALU.mult).then_inc(n_out, 1)

            def attend(j, par):
                def hstats():
                    hold(e, s["h_xn"], B * j)
                    statistics("x", lambda b: x1[:, NJ * b + j], j)

                def hnorm():
                    hold(e, s["h_turned"], j)
                    normalise("x", xn, lambda b: x1[:, NJ * b + j], j, s["h_xn"])

                def tile(b):
                    u = B * j + b
                    t = NJ * b + j

                    def highest():
                        hold(e, s["s_made"], u + 1)
                        hold(e, s["s_sub"], u)
                        e.tensor_reduce(mx0.rearrange("p (g i) -> p g i", g=G), scores_ps, AX, ALU.max).then_inc(s["s_max"], 1)

                    def subtract():
                        hold(e, s["s_max"], u + 1)
                        hold(e, s["s_exp"], u)
                        e.tensor_tensor(d0.rearrange("p (g i) k -> p g i k", g=G), scores_ps,
                                        mx0.rearrange("p (g i) -> p g i", g=G)[:, :, :, None].broadcast_to([P, G, HG, KEYS]),
                                        ALU.subtract).then_inc(s["s_sub"], 1)

                    def second():
                        hold(e, s["t_turned"], 3 * u + 2)
                        hold(e, s["pv_made"], u)
                        e.tensor_copy(pT[:, 4:8].rearrange("p c n -> p (c n)"), psT[:, 1]).then_inc(s["t_copiedV"], 1)

                    def norm():
                        hold(e, s["pv_made"], u + 1)
                        hold(e, s["pv_norm"], u)
                        e.reciprocal(rden[:], psM0[:, D:VW]).then_inc(s["pv_den"], 1)
                        hold(e, s["pv_den"], u + 1)
                        hold(e, s["o_turned"], u)
                        e.tensor_tensor(at0.rearrange("p (h d) -> p h d", h=H), psM0[:, 0:D].rearrange("p (h d) -> p h d", h=H),
                                        rden[:, :, None].broadcast_to([P, H, HD]), ALU.mult).then_inc(s["pv_norm"], 1)

                    def add():
                        hold(e, s["xbo_made"], B * j + B)
                        hold(e, s["o_proj"], u + 1)
                        e.tensor_tensor(x1[:, t], psM0[:, 384:512], x1[:, t], ALU.add).then_inc(s["x1_made"], 1)
                    return {f"mx{b}": highest, f"sub{b}": subtract, f"cb{b}": second, f"nm{b}": norm, f"x{b}": add}
                steps = dict(hstats=hstats, hnorm=hnorm)
                for b in range(B):
                    steps.update(tile(b))
                if isinstance(j, int) and j == 0:
                    def bias():
                        e.wait_ge(s["b12_made"], 1)
                        e.tensor_tensor(b12[:], psM1[0:E, 0:D], b2[:], ALU.add).then_inc(s["b12_stored"], 1)
                    steps["b12c"] = bias
                return steps

            def among(j, par):
                def zstats():
                    hold(e, s["y_n"], B * j)
                    hold(e, s["x1_made"], B * j + B)
                    statistics("m", lambda b: x1[:, NJ * b + j], 2 * j)

                def znorm():
                    hold(e, s["zob_made"], j)
                    hold(e, s["q_turned"], j)
                    normalise("m", zt, lambda b: x1[:, NJ * b + j], 2 * j, s["q_z"])

                def store(b):
                    def f():
                        hold(e, s["q_made"], B * j + b + 1)
                        if b == 0:
                            hold(e, s["m_pv"], B * j)
                        e.tensor_tensor(qkv[:, b], psM1[:, 0:3 * D], Rw["inb"], ALU.add).then_inc(s["q_stored"], 1)
                    return f

                def product(l):
                    def f():
                        hold(e, s["q_stored"], B * j + B)
                        hold(e, s["m_o"], B * j)
                        e.tensor_tensor(prod[:, l].rearrange("p (m n) -> p m n", m=B),
                                        qkv[:, l, None, 0:D].broadcast_to([P, B, D]),
                                        qkv[:, :, D:2 * D], ALU.mult).then_inc(s["m_prod"], 1)
                    return f

                def weighed(l):
                    def f():
                        hold(e, s["m_w"], j + 1)
                        hold(e, s["m_sc"], B * j + l + 1)
                        e.tensor_tensor(prod[:, l].rearrange("p (h d m) -> p h d m", h=MH, m=B),
                                        qkv[:, :, 2 * D:3 * D].rearrange("p m (h d) -> p h d m", h=MH),
                                        sc[:, l].rearrange("p m h -> p h m")[:, :, None, :].broadcast_to([P, MH, MHD, B]),
                                        ALU.mult).then_inc(s["m_pv"], 1)
                    return f

                def dot(l):
                    def f():
                        if l == 0:
                            hold(e, s["m_pv"], B * j)
                        hold(e, s["m_prod"], B * j + l + 1)
                        e.tensor_reduce(sc[:, l].rearrange("p m h -> p (m h)"), prod[:, l].rearrange("p (m d) -> p m d", d=MHD),
                                        AX, ALU.add).then_inc(s["m_sc"], 1)
                    return f

                def soft():
                    hold(e, s["m_sc"], B * j + B)
                    e.tensor_reduce(scx[:], sc.rearrange("p l m h -> p l h m"), AX, ALU.max).then_inc(s["m_soft"], 1)
                    hold(e, s["m_soft"], 3 * j + 1)
                    e.tensor_tensor(sc[:], sc[:], scx[:, :, None, :].broadcast_to([P, B, B, MH]), ALU.subtract).then_inc(s["m_sub"], 1)

                def weights_():
                    hold(e, s["m_exp"], j + 1)
                    e.tensor_reduce(scs[:], sce.rearrange("p l m h -> p l h m"), AX, ALU.add).then_inc(s["m_soft"], 1)
                    hold(e, s["m_soft"], 3 * j + 2)
                    e.reciprocal(scr[:], scs[:]).then_inc(s["m_soft"], 1)
                    hold(e, s["m_soft"], 3 * j + 3)
                    e.tensor_tensor(sc[:], sce[:], scr[:, :, None, :].broadcast_to([P, B, B, MH]), ALU.mult).then_inc(s["m_w"], 1)

                def total(l):
                    def f():
                        if l == 0:
                            hold(e, s["y_made"], j)
                        hold(e, s["m_pv"], B * j + l + 1)
                        e.tensor_reduce(oo[:, l], prod[:, l].rearrange("p (n m) -> p n m", m=B), AX, ALU.add).then_inc(s["m_o"], 1)
                    return f

                def residual():
                    hold(e, s["m_proj"], j + 1)
                    hold(e, s["m_turned"], j + 1)
                    hold(e, s["zob_made"], j + 1)
                    e.tensor_tensor(oo[:], psM1.rearrange("p (b n) -> p b n", b=B), zob[:], ALU.add).then_inc(s["m_res"], 1)
                    hold(e, s["m_res"], j + 1)
                    hold(e, s["q_z"], B * j + B)
                    statistics("m", lambda b: oo[:, b], 2 * j + 1)

                def ynorm():
                    normalise("m", oo, lambda b: oo[:, b], 2 * j + 1, s["y_n"])

                lg = psM1[:, 0:B * E].rearrange("p (b e) -> p b e", b=B)

                def differences():
                    hold(e, s["lg_made"], j + 1)
                    e.tensor_reduce(gmx[:], lg, AX, ALU.max).then_inc(s["g_step"], 1)
                    hold(e, s["g_step"], 8 * j + 1)
                    e.tensor_tensor(gd[:], lg, gmx[:, :, None].broadcast_to([P, B, E]), ALU.subtract).then_inc(s["g_d"], 1)
                    e.tensor_tensor(geq[:], lg, gmx[:, :, None].broadcast_to([P, B, E]), ALU.is_ge).then_inc(s["g_step"], 1)
                    hold(e, s["g_step"], 8 * j + 2)
                    e.tensor_tensor(gp[:], geq[:], C["prio"][:, None, :].broadcast_to([P, B, E]), ALU.mult).then_inc(s["g_step"], 1)
                    hold(e, s["g_step"], 8 * j + 3)
                    e.tensor_reduce(gpm[:], gp[:], AX, ALU.max).then_inc(s["g_step"], 1)

                def gates():
                    hold(e, s["g_exp"], j + 1)
                    e.tensor_reduce(gsum[:], ge[:], AX, ALU.add).then_inc(s["g_step"], 1)
                    hold(e, s["g_step"], 8 * j + 5)
                    e.reciprocal(gval[:], gsum[:]).then_inc(s["g_step"], 1)
                    hold(e, s["g_step"], 8 * j + 4)
                    ohj = oh.rearrange("p (b j) e -> p b j e", b=B)[:, :, j]
                    e.tensor_tensor(ohj, gp[:], gpm[:, :, None].broadcast_to([P, B, E]), ALU.is_equal).then_inc(s["g_step"], 1)
                    hold(e, s["g_step"], 8 * j + 7)
                    hold(e, s["g_step"], 8 * j + 6)
                    e.tensor_tensor(ohg.rearrange("p (b j) e -> p b j e", b=B)[:, :, j], ohj,
                                    gval[:, :, None].broadcast_to([P, B, E]), ALU.mult).then_inc(s["g_step"], 1)
                steps = dict(zstats=zstats, znorm=znorm, soft=soft, softw=weights_, res=residual, ynorm=ynorm, gdiff=differences, gate=gates)
                for b in range(B):
                    steps[f"qs{b}"] = store(b)
                    steps[f"qk{b}"] = product(b)
                    steps[f"wv{b}"] = weighed(b)
                    steps[f"dot{b}"] = dot(b)
                    steps[f"tot{b}"] = total(b)
                return steps

            run_groups(e, attend=attend, among=among)

            def gates_of(early):
                def total():
                    if early:
                        e.wait_ge(s["g_step"], 8 * EARLY)
                        e.tensor_copy(seen_early[:, 0], oh[:, 0]).then_inc(s["early_seen"], 1)
                        for t in range(1, EARLY):
                            e.wait_ge(s["early_seen"], t)
                            e.tensor_tensor(seen_early[:, t], seen_early[:, t - 1], oh[:, t], ALU.add).then_inc(s["early_seen"], 1)
                        return
                    src = oh
                    e.wait_ge(s["g_step"], 8 * NJ)
                    for n in range(4):
                        dst, span = seen_to[n % 2], 2 ** n
                        e.wait_ge(s["seen"], 2 * n)
                        e.tensor_copy(dst[:, 0:span], src[:, 0:span]).then_inc(s["seen"], 1)
                        e.tensor_tensor(dst[:, span:], src[:, span:], src[:, 0:NT - span], ALU.add).then_inc(s["seen"], 1)
                        src = dst

                def cap():
                    e.wait_ge(s["pos_made"], 1 if early else 2)
                    e.wait_ge(s["y_stored"], EARLY if early else NJ)
                    bank, lo, hi = (psM0, 0, EARLY) if early else (psM1, EARLY, NT)
                    e.scalar_tensor_tensor(yg[:, lo:hi, D:D + E], bank[:, 0:NT * E].rearrange("p (t e) -> p t e", e=E)[:, lo:hi],
                                           CAP - 0.5, ohg[:, lo:hi], ALU.is_lt, ALU.mult).then_inc(s["gates_set"], 1)
                return dict(total=total, cap=cap)

            def topk(t, par):
                n = [0]

                def largest(r):
                    def f():
                        if r == 0:
                            hold(e, s["mx_copied"], 2 * t)
                            hold(e, s["S_kept"], t + 1, alone=True)
                        for h in range(H):
                            if r and h % 4 == 0:
                                e.wait_ge(s["topk_step"], n[0] - 3 + h // 4)
                            ins = e.max(top[:, r, h], (left if r else scores_sb[par])[:, h])
                            if h % 4 == 3:
                                ins.then_inc(s["topk_step"], 1)
                        n[0] += 4
                    return f

                def mark(r):
                    def f():
                        for h in range(H):
                            if h % 4 == 0:
                                e.wait_ge(s["topk_step"], n[0] - 3 + h // 4)
                            ins = e.match_replace(left[:, h], top[:, r, h], (left if r else scores_sb[par])[:, h], GONE)
                            if h % 4 == 3:
                                ins.then_inc(s["topk_step"] if (r or h < H - 1) else s["topk_step"], 1)
                        n[0] += 4
                    return f

                def free_scores():
                    e.wait_ge(s["topk_step"], 8)
                    e.tensor_copy(mxc[:, 0], top[:, 0, :, 0]).then_inc(s["S_read"], 1)

                def ends():
                    e.wait_ge(s["topk_step"], n[0])
                    e.tensor_copy(mxc[:, 1], top[:, TOPK // 8 - 1, :, 7]).then_inc(s["mx_copied"], 1)
                    hold(e, s["S_read"], t + 1)
                    hold(e, s["mx_copied"], 2 * t + 1, alone=True)
                    e.sem_clear(s["topk_step"])
                    e.engine_nop().then_inc(s["mx_copied"], 1)

                out_ = {}
                for r in range(TOPK // 8):
                    out_[f"max{r}"] = largest(r)
                    if r < TOPK // 8 - 1:
                        out_[f"mark{r}"] = mark(r)
                    if r == 0:
                        out_["free"] = lambda: (hold(e, s["cut_set"], t), free_scores())
                out_["ends"] = ends
                return out_

            def value(t, par):
                def a():
                    hold(e, s["a_made"], t + 1)
                    e.reciprocal(rden1[:], psM1[:, D:VW]).then_inc(s["a_den"], 1)
                    hold(e, s["a_den"], t + 1)
                    hold(e, s["x3_set"], t)
                    e.tensor_tensor(att1.rearrange("p (h d) -> p h d", h=H), psM1[:, 0:D].rearrange("p (h d) -> p h d", h=H),
                                    rden1[:, :, None].broadcast_to([P, H, HD]), ALU.mult).then_inc(s["a_norm"], 1)
                return dict(norm=a)

            hand_over(e, among=among, topk=topk, gates=gates_of)
            run_tiles(e, topk=topk, value=value)

        @block.tensor
        def _(e):
            mm, tr = e.matmul, e.transpose
            e.wait_ge(s["ctx_in"], 16)
            e.wait_ge(s["weights_in"], 32)
            keys = ctx_sb.rearrange("p b k -> p (b k)")
            mm(psM0[:, 0:B * KEYS], Wt["wk0"], keys, start=True, stop=True).then_inc(s["k0_made"], 1)
            mm(psM1[:, 0:B * KEYS], Wt["wk1"], keys, start=True, stop=True).then_inc(s["k1_made"], 1)
            e.wait_ge(s["constants_set"], 6)
            e.wait_ge(s["consts_in"], 16)
            for n in range(2 * B * 3):
                b, g = n // 3 % B, n % 3
                e.wait_ge(s["ctx_rep"], b + 1)
                if n >= 2:
                    e.wait_ge(s["v_masked"], n - 1)
                for c in range(4 * g, min(4 * g + 4, NCH)):
                    dst = psT[:, n % 2, (c % 4) * P:(c % 4 + 1) * P]
                    if n < 3 * B:
                        ins = mm(dst, ctxrep[:, b, c * P:(c + 1) * P], Wt["wv0"], start=True, stop=True)
                    else:
                        ins = tr(dst, ctxrep[:, b, c * P:(c + 1) * P], ident)
                ins.then_inc(s["v_turned"], 1)
            e.wait_ge(s["kblk0_made"], B)
            e.wait_ge(s["mrow_made"], 3 * HG)
            e.wait_ge(s["constants_set"], 4)
            e.wait_ge(s["k0_copied"], 1)
            e.wait_ge(s["k1_copied"], 1)
            e.wait_ge(s["v_masked"], 2 * B * 3)
            e.wait_ge(s["den_cols"], 2 * B)

            def turn4(bank, src, done):
                for b in range(B):
                    ins = tr(bank[:, b * P:(b + 1) * P], src[:, b], ident)
                ins.then_inc(done, 1)

            def attend(j, par):
                def hturn():
                    hold(e, s["x1_made"], B * j)
                    hold(e, s["h_xn"], B * j + B)
                    turn4(psM0, xn, s["h_turned"])

                def hq():
                    hold(e, s["h_xnT"], j + 1)
                    mm(psM0, Wt["wq0"], xnT.rearrange("p b n -> p (b n)"), start=True, stop=True).then_inc(s["h_q"], 1)

                def tile(b):
                    u = B * j + b

                    def scores():
                        hold(e, s["h_qT"], j + 1)
                        hold(e, s["s_sub"], u)
                        for g in range(G):
                            mm(psS[:, g, 0:GW], q0T[32 * g:32 * g + 32, b], kblk0[32 * g:32 * g + 32, b].rearrange("p i k -> p (i k)"),
                               start=True, stop=False)
                        for g in range(G):
                            ins = mm(psS[:, g, 0:GW], mones[:], mrow[:, b].rearrange("p i k -> p (i k)"), start=False, stop=True)
                        ins.then_inc(s["s_made"], 1)

                    def turn(g):
                        def f():
                            if g == 0:
                                hold(e, s["s_exp"], u + 1)
                                hold(e, s["t_copiedA"], 3 * u)
                            elif g == 1:
                                hold(e, s["t_copiedV"], u)
                            else:
                                hold(e, s["t_copiedA"], 3 * u + 1)
                            for c in range(4 * g, min(4 * g + 4, NCH)):
                                w = P if c < NCH - 1 else LAST
                                ins = tr(psT[0:w, g % 2, (c % 4) * P:(c % 4 + 1) * P], e0[:, c * P:c * P + w], ident)
                            ins.then_inc(s["t_turned"], 1)
                        return f

                    def value():
                        hold(e, s["t_copiedA"], 3 * u + 3)
                        hold(e, s["t_copiedV"], u + 1)
                        hold(e, s["x1_made"], u)
                        for c in range(NCH):
                            w = P if c < NCH - 1 else LAST
                            ins = mm(psM0[:, 0:VW], pT[0:w, c], vblk0[0:w, b, c], start=(c == 0), stop=(c == NCH - 1))
                        ins.then_inc(s["pv_made"], 1)

                    def oturn():
                        hold(e, s["pv_norm"], u + 1)
                        tr(psM0[:, 256:384], at0[:], ident).then_inc(s["o_turned"], 1)

                    def project():
                        hold(e, s["o_T"], u + 1)
                        mm(psM0[:, 384:512], at0T[:], Wt["wo0"], start=True, stop=True).then_inc(s["o_proj"], 1)
                    return {f"s{b}": scores, f"ta{b}": turn(0), f"tb{b}": turn(1), f"tc{b}": turn(2), f"v{b}": value,
                            f"ot{b}": oturn, f"op{b}": project}
                steps = dict(hturn=hturn, hq=hq)
                for b in range(B):
                    steps.update(tile(b))
                if isinstance(j, int) and j == 0:
                    def merged(n):
                        def f():
                            e.wait_ge(s["w1_in"], 16)
                            e.wait_ge(s["w2_in"], 16)
                            hold(e, s["w12_stored"], n)
                            for x_ in range(4 * n, 4 * n + 4):
                                for c in range(FC):
                                    ins = mm(psM1[:, (x_ % 4) * D:(x_ % 4 + 1) * D], w1T[:, c, x_], w2[:, c, x_], start=(c == 0), stop=(c == FC - 1))
                            ins.then_inc(s["w12_made"], 1)
                        return f

                    def bias():
                        e.wait_ge(s["w12_stored"], 2)
                        e.wait_ge(s["b1_spread"], 1)
                        for x_ in range(E):
                            for c in range(FC):
                                ins = mm(psM1[0:E, 0:D], b1z[:, c, x_ * E:(x_ + 1) * E], w2[:, c, x_],
                                         start=(x_ == 0 and c == 0), stop=(x_ == E - 1 and c == FC - 1))
                        ins.then_inc(s["b12_made"], 1)
                    steps.update(w12a=merged(0), w12b=merged(1), b12=bias)
                return steps

            def among(j, par):
                def zturn():
                    if isinstance(j, int) and j == 0:
                        e.wait_ge(s["b12_stored"], 1)
                    hold(e, s["g_step"], 8 * j)
                    hold(e, s["q_z"], B * j + B)
                    turn4(psM1, zt, s["q_turned"])

                def inproj(b):
                    def f():
                        hold(e, s["q_zT"], j + 1)
                        hold(e, s["q_stored"], B * j + b)
                        mm(psM1[:, 0:3 * D], mT[:, b], Wt["inw"], start=True, stop=True).then_inc(s["q_made"], 1)
                    return f

                def mturn():
                    hold(e, s["q_stored"], B * j + B)
                    hold(e, s["m_o"], B * j + B)
                    turn4(psM1, oo, s["m_turned"])

                def proj():
                    hold(e, s["m_oT"], j + 1)
                    for b in range(B):
                        ins = mm(psM1[:, b * P:(b + 1) * P], mT[:, b], Wt["outw"], start=True, stop=True)
                    ins.then_inc(s["m_proj"], 1)

                def yturn():
                    hold(e, s["m_res"], j + 1)
                    hold(e, s["y_made"], j + 1)
                    turn4(psM1, y1s, s["y_turned"])

                def logits():
                    hold(e, s["y_T"], j + 1)
                    for b in range(B):
                        ins = mm(psM1[:, b * E:(b + 1) * E], mT[:, b], Wt["wg"], start=True, stop=True)
                    ins.then_inc(s["lg_made"], 1)
                steps = dict(zturn=zturn, mturn=mturn, proj=proj, yturn=yturn, lg=logits)
                for b in range(B):
                    steps[f"q{b}"] = inproj(b)
                return steps

            run_groups(e, attend=attend, among=among)

            def gates_of(early):
                def places():
                    bank, n, upto = (psM0, EARLY, seen_early) if early else (psM1, NT, seen_to[1])
                    e.wait_ge(s["x1_made"], NT)
                    e.wait_ge(s["s_sub"], NT)
                    e.wait_ge(s["g_step"], 8 * (EARLY if early else NJ))
                    mm(bank[:, 0:n * E], tri, oh[:, 0:n].rearrange("p t e -> p (t e)"), start=True, stop=False)
                    e.wait_ge(s["early_seen"], EARLY)
                    if not early:
                        e.wait_ge(s["seen"], 8)
                    mm(bank[:, 0:n * E], ones[:], upto.rearrange("p t e -> p (t e)"), start=False, stop=True).then_inc(s["pos_made"], 1)
                return dict(places=places)

            e.wait_ge(s["w12_stored"], 2)
            e.wait_ge(s["b12_stored"], 1)
            e.wait_ge(s["b1_spread"], 6)
            e.wait_ge(s["kblk1_made"], B)

            def experts(t, par):
                def turn():
                    hold(e, s["cur_set"], t + 1)
                    hold(e, s["n2_out"], t)
                    tr(psM0[:, 0:P], cur[:, 0:D], ident)
                    tr(psM0[0:E, P:2 * P], cur[:, D:D + E], ident).then_inc(s["c_turned"], 1)

                def moe(n):
                    def f():
                        if n == 0:
                            hold(e, s["c_copied"], 2 * t + 2)
                            mm(psM0[:, 0:D], gT[:], b12[:], start=True, stop=True).then_inc(s["mb_made"], 1)
                            mm(psM0[:, D:4 * D], y1T[:], w12[:, 0:3].rearrange("p e n -> p (e n)"), start=True, stop=True)\
                                .then_inc(s["mb_made"], 1)
                        else:
                            hold(e, s["mb_out"], 3 * t + n)
                            lo, hi = ((3, 7), (7, 8))[n - 1]
                            mm(psM0[:, 0:(hi - lo) * D], y1T[:], w12[:, lo:hi].rearrange("p e n -> p (e n)"), start=True, stop=True)\
                                .then_inc(s["mb_made"], 1)
                    return f

                def total():
                    hold(e, s["mb_out"], 3 * t + 3)
                    mm(psM0[:, 0:D], ident, cur[:, 0:D], start=True, stop=False)
                    for x_ in range(E + 1):
                        ins = mm(psM0[:, 0:D], ident, mparts[:, x_], start=False, stop=(x_ == E))
                    ins.then_inc(s["mty"], 1)
                return dict(turn=turn, moe0=moe(0), moe1=moe(1), moe2=moe(2), total=total)

            def query(t, par):
                def zturn():
                    hold(e, s["n3_out"], t + 1)
                    hold(e, s["S_kept"], t)
                    tr(psS[:, 0, 0:P], z2, ident).then_inc(s["z_turned"], 1)

                def ask():
                    hold(e, s["z_T"], t + 1)
                    mm(psS[:, 1, 0:P], Wt["wq1"], z2T, start=True, stop=True).then_inc(s["q1_made"], 1)

                def scores():
                    hold(e, s["q1_T"], t + 1)
                    hold(e, s["kcur_set"], t + 1)
                    for g in range(G):
                        ins = mm(psS[:, g, 0:GW], q1T[32 * g:32 * g + 32, :], kcur[32 * g:32 * g + 32], start=True, stop=True)
                    ins.then_inc(s["S_ready"], 1)
                return dict(zturn=zturn, ask=ask, scores=scores)

            def weigh(t, par):
                def turn(g):
                    def f():
                        if g == 0:
                            hold(e, s["p_set"], t + 1)
                        hold(e, s["p_copied"], 3 * t + g)
                        for c in range(4 * g, min(4 * g + 4, NCH)):
                            w = P if c < NCH - 1 else LAST
                            ins = tr(psT[0:w, 0, (c % 4) * P:(c % 4 + 1) * P], p1[:, c * P:c * P + w], ident)
                        ins.then_inc(s["p_turned"], 1)
                    return f

                return dict(turn0=turn(0), turn1=turn(1), turn2=turn(2))

            def value(t, par):
                def times():
                    if isinstance(t, int) and t == 0:
                        e.wait_ge(s["gates_set"], 2)
                    hold(e, s["p_copied"], 3 * t + 3)
                    hold(e, s["a_norm"], t)
                    for c in range(NCH):
                        w = P if c < NCH - 1 else LAST
                        ins = mm(psM1[:, 0:VW], pT1[0:w, c], vblk1[0:w, t // NJ, c], start=(c == 0), stop=(c == NCH - 1),
                                 skip_group_check=True)
                    ins.then_inc(s["a_made"], 1)
                return dict(value=times)

            def mix(t, par):
                def turn():
                    hold(e, s["n4_out"], t + 1)
                    hold(e, s["f_sq"], t)
                    hold(e, s["f_vv"], t)
                    tr(psT[:, 1, 0:P], zf, ident).then_inc(s["f_turned"], 1)

                def up():
                    hold(e, s["f_T"], t + 1)
                    now, prev = zfT[:, 1:P + 1], zfT[:, 0:P]
                    mm(psT[:, 1, P:2 * P], wk_now[:], now, start=True, stop=False, skip_group_check=True)
                    mm(psT[:, 1, P:2 * P], wk_prev[:], prev, start=False, stop=True, skip_group_check=True)
                    mm(psT[:, 1, 2 * P:3 * P], now, wr_now[:], start=True, stop=False, skip_group_check=True)
                    mm(psT[:, 1, 2 * P:3 * P], prev, wr_prev[:], start=False, stop=True, skip_group_check=True).then_inc(s["f_kr"], 1)

                def down():
                    hold(e, s["f_sq"], t + 1)
                    mm(psT[:, 1, 3 * P:4 * P], ka, Wt["wv"], start=True, stop=True, skip_group_check=True).then_inc(s["f_v"], 1)
                return dict(fturn=turn, up=up, down=down)

            hand_over(e, among=among, gates=gates_of, experts=experts, query=query, weigh=weigh)
            run_tiles(e, experts=experts, query=query, weigh=weigh, value=value, mix=mix)


GROUP_AHEAD = dict(attend=0, among=-1)
GROUP_ORDER = """hstats zstats hrstd hnorm hturn hT zrstd znorm zturn hq zT q0 qs0 hqT s0 w12a mx0 sub0 q1 s1 w12b qs1 q2
exp0 w12c0 mx1 ta0 qs2 q3 tb0 sub1 ca0 qs3 cb0 qk0 tc0 s2 b12 bias qk1 dot0 qk2 dot1 cc0 qk3 dot2 mx2 dot3
v0 nm0 exp1 w12c1 ta1 ca1 soft tb1 cb1 ot0 mexp oT0 tc1 op0 softw x0 wv0 cc1 sub2 v1 wv1 zbias tot0 wv2
tot1 exp2 s3 wv3 tot2 ta2 nm1 ot1 tot3 tb2 mturn ca2 oT1 mx3 op1 cb2 b12c xbias x1 tc2 sub3 mTc proj res
cc2 v2 yrstd exp3 ta3 nm2 ynorm ca3 ot2 tb3 cb3 tc3 oT2 yaffine op2 x2 cc3 v3 ystore yturn yT nm3 ot3 lg
oT3 gdiff op3 x3 gexp gate""".split()

TILE_AHEAD = dict(experts=3, query=2, kept=1, topk=0, weigh=-1, value=-2, mix=-3)
TILE_ORDER = """load max0 sum4 turn square4 scale4 norm4 sum3 fturn copy dif cut mark0 moe0 free keys shift up max1
square3 scale3 gated0 moe1 exp value gated1 moe2 sign mark1 product gated2 acts half total norm turn0 x3
keep down norm3 max2 sum2 copy0 zturn square2 zT turn1 ask scale2 fvalue copy1 qT mark2 turn2 max3 end
scores norm2 ends affine copy2""".split()

HANDED = 2
HAND_OVER = """total@early places@early zstats cap@early keys@0 load@0 turn@0 zrstd copy@0 moe0@0 gated0@0 znorm zturn
moe1@0 zbias zT gated1@0 q0 qs0 moe2@0 gated2@0 q1 total@0 qs1 sum2@0 xbias q2 load@1 square2@0 qs2 q3 qs3
scale2@0 norm2@0 turn@1 copy@1 qk0 affine@0 qk1 moe0@1 dot0 sum3@0 square3@0 qk2 gated0@1 qk3 scale3@0
moe1@1 dot1 dot2 norm3@0 dot3 gated1@1 soft zturn@0 moe2@1 mexp gated2@1 softw total@1 wv0 zT@0 tot0 wv1
tot1 wv2 wv3 tot2 sum2@1 ask@0 load@2 square2@1 tot3 qT@0 mturn scale2@1 norm2@1 mTc turn@2 proj copy@2
affine@1 res moe0@2 sum3@1 square3@1 gated0@2 scale3@1 yrstd ynorm scores@0 moe1@2 norm3@1 yaffine keep@0
yturn gated1@2 keys@1 max0@0 yT ystore moe2@2 zturn@1 gated2@2 lg total@2 gdiff gexp gate total@late
sum2@2 square2@2 scale2@2 mark0@0 free@0 zT@1 max1@0 ask@1 qT@1 places@late cap@late scores@1 norm2@2
load@3 affine@2 sum3@2 mark1@0 square3@2 max2@0 scale3@2 turn@3 copy@3 moe0@3 keys@2 keep@1 mark2@0
gated0@3 moe1@3 max3@0 norm3@2 ends@0 gated1@3 zturn@2 moe2@3 gated2@3 total@3 max0@1 dif@0 zT@2 cut@0
mark0@1 sum2@3 load@4 ask@2 square2@3 free@1 scale2@3 max1@1 qT@2 exp@0 scores@2 norm2@3 turn@4 sign@0
affine@3 sum3@3 copy@4 product@0 mark1@1 moe0@4 max2@1 square3@3 keep@2 gated0@4 scale3@3 turn0@0 mark2@1
keys@3 moe1@4 norm3@3 copy0@0 gated1@4 zturn@3 max3@1 turn1@0 moe2@4 zT@3 ends@1 copy1@0 gated2@4 ask@3
total@4 qT@3 turn2@0 sum2@4 square2@4 scale2@4 norm2@4 affine@4 copy2@0 scores@3""".split()


def pipeline(e, order, aheads, count, least, each, stages, begin, end):
    def turn(i, parity, known):
        steps = {}
        for name, ahead in aheads.items():
            if name in stages and (not known or 0 <= i + ahead < count):
                steps.update(stages[name](i + ahead, (parity + ahead) % 2))
        for name in order:
            if name in steps:
                steps[name]()

    first, last = least - min(aheads.values()), count - max(aheads.values())
    for i in range(begin, first):
        turn(i, i % 2, True)
    with e.Fori(first, last - each + 1, each) as i:
        for n in range(each):
            turn(i + n, (first + n) % 2, False)
    for i in range(last, end):
        turn(i, i % 2, True)


def run_groups(e, **stages):
    pipeline(e, GROUP_ORDER, GROUP_AHEAD, NJ, 1, 1, stages, 0, NJ)


def hand_over(e, among, gates=None, **stages):
    steps = dict(among(NJ - 1, (NJ - 1) % 2))
    if gates:
        for when in ("early", "late"):
            for name, step in gates(when == "early").items():
                steps[f"{name}@{when}"] = step
    for stage, ahead in TILE_AHEAD.items():
        if stage in stages:
            for t in range(HANDED + ahead):
                for name, step in stages[stage](t, t % 2).items():
                    steps[f"{name}@{t}"] = step
    for name in HAND_OVER:
        if name in steps:
            steps[name]()


def run_tiles(e, **stages):
    pipeline(e, TILE_ORDER, TILE_AHEAD, NT, 2, 2, stages, HANDED, NT - min(TILE_AHEAD.values()))


def kernel(**inputs):
    import numpy as np
    import concourse.bacc as bacc
    from concourse.bass_utils import run_bass_kernel_spmd as run

    a = {k: np.asarray(v) for k, v in inputs.items()}
    f32 = np.float32
    head = np.arange(NCH * P) // KEYS
    cols_of = np.arange(VW)
    own = np.where(cols_of < D, cols_of // HD, cols_of - D)
    headmask = (head[:, None] == own[None, :]).astype(f32).reshape(NCH, P, VW).transpose(1, 0, 2).reshape(P, -1)
    consts = np.concatenate([
        np.eye(P, dtype=f32),
        np.triu(np.ones((P, P), f32), 1) - 1,
        (np.arange(P)[:, None] % 32 // HD == np.arange(HG)[None, :]).astype(f32),
        np.broadcast_to(np.arange(E, 0, -1, dtype=f32), (P, E)),
        np.broadcast_to((np.arange(NT) % NJ != 0).astype(f32), (P, NT)),
        headmask,
    ], axis=1)
    weights = np.concatenate([
        a["L0_xattn_Wk"].T, a["L0_xattn_Wv"].T, a["L0_xattn_Wq"].T, a["L0_xattn_Wo"].T, a["L0_ffn_in_proj_w"].T,
        a["L0_ffn_out_proj_w"].T, a["L1_xattn_Wq"].T, a["L1_xattn_Wk"].T, a["L1_ffn_W_r"].T, a["L1_ffn_W_k"].T,
        a["L1_ffn_W_v"].T, a["L0_ffn_wg"],
    ], axis=1)
    cols = np.stack([a["L0_xattn_bq"], a["L0_xattn_bk"], a["L0_xattn_bv"], a["L1_ffn_mu_r"], a["L1_ffn_mu_k"]], axis=1)
    rows = np.concatenate([a["L0_xattn_bo"], a["L0_ffn_in_proj_b"], a["L0_ffn_out_proj_b"], a["L0_ffn_ln1_g"],
                           a["L0_ffn_ln1_b"], a["L0_ffn_ln2_g"], a["L0_ffn_ln2_b"]])[None, :]
    arrays = dict(
        x=a["x"].reshape(NT, P, D).transpose(1, 0, 2),
        ctxT=a["ctx_1024"].transpose(2, 0, 1),
        mask=a["mask_BxS2_bf1"].view(np.uint8).reshape(1, B * KEYS),
        consts=consts, weights=weights, cols=cols, rows=rows,
        b1T=a["L0_ffn_b1"].reshape(E, FC, P).transpose(2, 1, 0),
        b2=a["L0_ffn_b2"],
        w1T=a["L0_ffn_w1"].reshape(E, D, FC, P).transpose(3, 2, 0, 1),
        w2=a["L0_ffn_w2"].reshape(E, FC, P, D).transpose(2, 1, 0, 3),
    )
    nc = bacc.Bacc("TRN2", target_bir_lowering=False, num_devices=1)
    feed, args = {}, []
    for name, v in arrays.items():
        v = np.ascontiguousarray(v)
        feed[f"in_{name}"] = v
        args.append(nc.dram_tensor(f"in_{name}", v.shape, mybir.dt.from_np(v.dtype), kind="ExternalInput").ap())
    out = nc.dram_tensor("out", (NT, P, D), F32, kind="ExternalOutput").ap()
    build(nc, *args, out)
    r = run(nc, [feed], core_ids=[0])
    return r.results[0]["out"].reshape(B, SEQ, D)
```
